# Optimizing a Trainium2 kernel written in Bass

```python
import numpy as np
import jax
import jax.numpy as jnp

def _softmax(x, axis=-1):
    return jax.nn.softmax(x, axis=axis)

def _gelu(x):
    return jax.nn.gelu(x, approximate=True)

def _silu(x):
    return jax.nn.silu(x)

def _sigmoid(x):
    return jax.nn.sigmoid(x)

def _layernorm(x, axis=-1, eps=1e-05):
    m = jnp.mean(x, axis=axis, keepdims=True)
    v = jnp.var(x, axis=axis, keepdims=True)
    return (x - m) / jnp.sqrt(v + eps)

def _scatter_add(tgt, idx, src, axis=0):
    return tgt.at[idx].add(src)

def _segment_sum(src, seg, n):
    return jax.ops.segment_sum(src, seg, n)
kernel_name = 'mk_xattn_ffn_d2_seqx_r2_f90aae'

def setup_inputs(seed: int=0):
    np.random.seed(seed)
    _w = jnp.asarray

    def _rec_inputs():
        import jax
        import jax.numpy as jnp
        _rk = jax.random.key(seed)
        x = -0.0002928 + 1 * jax.random.normal(jax.random.fold_in(_rk, 1), (2, 2048, 512), jnp.float32)
        _lenS = 2048 - jax.random.randint(jax.random.fold_in(_rk, 7), (2,), 0, max(1, 2048 // 4) + 1, jnp.int32)
        _lenS2 = 154 - jax.random.randint(jax.random.fold_in(_rk, 8), (2,), 0, max(1, 154 // 4) + 1, jnp.int32)
        _ctx_1024P = jax.random.normal(jax.random.fold_in(_rk, 11), (2, 16, 512), jnp.float32)
        _ctx_1024c = jax.random.dirichlet(jax.random.fold_in(_rk, 511), 0.3 * jnp.ones((16,), jnp.float32), (2, 154))
        _ctx_1024t = jnp.einsum('bsk,bkd->bsd', _ctx_1024c, _ctx_1024P)
        _ctx_1024t = _ctx_1024t * jax.lax.rsqrt(jnp.mean(jnp.square(_ctx_1024t)) + 1e-12) * 0.953939
        ctx_1024 = -1.39393e-06 + 0.999914 * (_ctx_1024t + 0.3 * jax.random.normal(jax.random.fold_in(_rk, 611), (2, 154, 512), jnp.float32))
        return (x, ctx_1024)
    x, ctx_1024 = _rec_inputs()

    def _L0_xattn_setup():
        import jax, jax.numpy as jnp
        import numpy as np
        D_MODEL = 512
        NUM_HEADS = 16
        D_K = D_MODEL // NUM_HEADS

        def _split_heads(x):
            B, S, _ = x.shape
            return x.reshape(B, S, NUM_HEADS, D_K).transpose(0, 2, 1, 3)
        key = jax.random.key(seed)
        ks = jax.random.split(key, 11)
        B, S, D = (2, 1024, D_MODEL)
        scale = 1.0 / np.sqrt(D)
        inp = {'queries': jax.random.normal(ks[0], (B, S, D), jnp.float32), 'keys': jax.random.normal(ks[1], (B, S, D), jnp.float32), 'values': jax.random.normal(ks[2], (B, S, D), jnp.float32), 'w_q': jax.random.normal(ks[3], (D, D), jnp.float32) * scale, 'b_q': jnp.zeros((D,), jnp.float32), 'w_k': jax.random.normal(ks[4], (D, D), jnp.float32) * scale, 'b_k': jnp.zeros((D,), jnp.float32), 'w_v': jax.random.normal(ks[5], (D, D), jnp.float32) * scale, 'b_v': jnp.zeros((D,), jnp.float32), 'w_o': jax.random.normal(ks[6], (D, D), jnp.float32) * scale, 'b_o': jnp.zeros((D,), jnp.float32)}
        return inp
    _L0_xattn_all = _L0_xattn_setup()
    _L0_xattn_in = {k: v for k, v in _L0_xattn_all.items() if k in ('w_q', 'b_q', 'w_k', 'b_k', 'w_v', 'b_v', 'w_o', 'b_o')}
    del _L0_xattn_all

    def _L0_ffn_setup():
        import jax, jax.numpy as jnp
        import numpy as np
        B, T, D = (2, 1024, 512)
        DCD = 2048
        RET = 128
        NEXP = 2048
        NKEYS = 64
        H = 4
        KPH = 8
        key = jax.random.key(seed)
        ks = jax.random.split(key, 10)
        s = lambda k, shape, scale: jax.random.normal(k, shape, jnp.float32) * scale
        return {'hidden_states': jax.random.normal(ks[0], (B, T, D), jnp.float32), 'Wg': s(ks[1], (D, DCD), 0.02), 'bg': jnp.zeros((DCD,), jnp.float32), 'Wu': s(ks[2], (D, DCD), 0.02), 'bu': jnp.zeros((DCD,), jnp.float32), 'Wd': s(ks[3], (DCD, D), 0.02), 'bd': jnp.zeros((D,), jnp.float32), 'Wq': s(ks[4], (D, RET * H), 0.02), 'keys': s(ks[5], (H, NKEYS, 2, RET // 2), 0.02), 'down_embed': s(ks[6], (NEXP, D), 0.02), 'up_embed': s(ks[7], (NEXP, D), 0.02)}
    _L0_ffn_all = _L0_ffn_setup()
    _L0_ffn_in = {k: v for k, v in _L0_ffn_all.items() if k in ('Wg', 'bg', 'Wu', 'bu', 'Wd', 'bd', 'Wq', 'keys', 'down_embed', 'up_embed')}
    del _L0_ffn_all

    def _L1_xattn_setup():
        import jax, jax.numpy as jnp
        import numpy as np
        DIM = 512
        HEADS = 16
        HEAD_DIM = 64
        INNER = HEADS * HEAD_DIM

        def _split_heads(t):
            b, n, _ = t.shape
            return t.reshape(b, n, HEADS, HEAD_DIM).transpose(0, 2, 1, 3)
        key = jax.random.key(seed)
        ks = jax.random.split(key, 7)
        b, n, m = (2, 1024, 1024)
        s = 0.02
        return {'x': jax.random.normal(ks[0], (b, n, DIM), dtype=jnp.float32), 'context': jax.random.normal(ks[1], (b, m, DIM), dtype=jnp.float32), 'w_kv': jax.random.normal(ks[2], (DIM, 2 * INNER), dtype=jnp.float32) * s, 'w_q': jax.random.normal(ks[3], (DIM, INNER), dtype=jnp.float32) * s, 'w_out1': jax.random.normal(ks[4], (INNER, DIM), dtype=jnp.float32) * s, 'w_out2': jax.random.normal(ks[5], (DIM, DIM), dtype=jnp.float32) * s, 'gamma': jnp.ones((DIM,), dtype=jnp.float32)}
    _L1_xattn_all = _L1_xattn_setup()
    _L1_xattn_in = {k: v for k, v in _L1_xattn_all.items() if k in ('w_kv', 'w_q', 'w_out1', 'w_out2', 'gamma')}
    del _L1_xattn_all

    def _L1_ffn_setup():
        import jax, jax.numpy as jnp
        import numpy as np
        D_MODEL = 512
        EXPANSION = 4
        D_HIDDEN = D_MODEL * EXPANSION
        NUM_STAGES = int(np.log2(D_HIDDEN))

        def butterfly(y, weights, dim):
            lead = y.shape[:-1]
            for stage in range(weights.shape[0]):
                s = 2 ** stage
                nb = dim // (2 * s)
                yr = y.reshape(*lead, nb, 2, s)
                a = yr[..., 0, :]
                b = yr[..., 1, :]
                w = weights[stage].reshape(nb, s, 2, 2)
                na = w[..., 0, 0] * a + w[..., 0, 1] * b
                nb2 = w[..., 1, 0] * a + w[..., 1, 1] * b
                y = jnp.stack([na, nb2], axis=-2).reshape(*lead, dim)
            return y
        key = jax.random.key(seed)
        ks = jax.random.split(key, 6)
        B, S = (4, 1024)
        x = jax.random.normal(ks[0], (B, S, D_MODEL), jnp.float32)
        W_exp = jax.random.normal(ks[1], (D_MODEL, D_HIDDEN), jnp.float32) * 0.02
        b_exp = jnp.zeros((D_HIDDEN,), jnp.float32)
        up_weights = jax.random.normal(ks[2], (NUM_STAGES, D_HIDDEN // 2, 2, 2), jnp.float32) * 0.02
        up_bias = jnp.zeros((D_HIDDEN,), jnp.float32)
        down_weights = jax.random.normal(ks[3], (NUM_STAGES, D_HIDDEN // 2, 2, 2), jnp.float32) * 0.02
        W_con = jax.random.normal(ks[4], (D_HIDDEN, D_MODEL), jnp.float32) * 0.02
        b_con = jnp.zeros((D_MODEL,), jnp.float32)
        down_bias = jnp.zeros((D_MODEL,), jnp.float32)
        return dict(x=x, W_exp=W_exp, b_exp=b_exp, up_weights=up_weights, up_bias=up_bias, down_weights=down_weights, W_con=W_con, b_con=b_con, down_bias=down_bias)
    _L1_ffn_all = _L1_ffn_setup()
    _L1_ffn_in = {k: v for k, v in _L1_ffn_all.items() if k in ('W_exp', 'b_exp', 'up_weights', 'up_bias', 'down_weights', 'W_con', 'b_con', 'down_bias')}
    del _L1_ffn_all
    return {'x': x, 'ctx_1024': ctx_1024, 'L0_xattn_w_q': _L0_xattn_in['w_q'], 'L0_xattn_b_q': _L0_xattn_in['b_q'], 'L0_xattn_w_k': _L0_xattn_in['w_k'], 'L0_xattn_b_k': _L0_xattn_in['b_k'], 'L0_xattn_w_v': _L0_xattn_in['w_v'], 'L0_xattn_b_v': _L0_xattn_in['b_v'], 'L0_xattn_w_o': _L0_xattn_in['w_o'], 'L0_xattn_b_o': _L0_xattn_in['b_o'], 'L0_ffn_Wg': _L0_ffn_in['Wg'], 'L0_ffn_bg': _L0_ffn_in['bg'], 'L0_ffn_Wu': _L0_ffn_in['Wu'], 'L0_ffn_bu': _L0_ffn_in['bu'], 'L0_ffn_Wd': _L0_ffn_in['Wd'], 'L0_ffn_bd': _L0_ffn_in['bd'], 'L0_ffn_Wq': _L0_ffn_in['Wq'], 'L0_ffn_keys': _L0_ffn_in['keys'], 'L0_ffn_down_embed': _L0_ffn_in['down_embed'], 'L0_ffn_up_embed': _L0_ffn_in['up_embed'], 'L1_xattn_w_kv': _L1_xattn_in['w_kv'], 'L1_xattn_w_q': _L1_xattn_in['w_q'], 'L1_xattn_w_out1': _L1_xattn_in['w_out1'], 'L1_xattn_w_out2': _L1_xattn_in['w_out2'], 'L1_xattn_gamma': _L1_xattn_in['gamma'], 'L1_ffn_W_exp': _L1_ffn_in['W_exp'], 'L1_ffn_b_exp': _L1_ffn_in['b_exp'], 'L1_ffn_up_weights': _L1_ffn_in['up_weights'], 'L1_ffn_up_bias': _L1_ffn_in['up_bias'], 'L1_ffn_down_weights': _L1_ffn_in['down_weights'], 'L1_ffn_W_con': _L1_ffn_in['W_con'], 'L1_ffn_b_con': _L1_ffn_in['b_con'], 'L1_ffn_down_bias': _L1_ffn_in['down_bias']}

def reference(x, ctx_1024, L0_xattn_w_q, L0_xattn_b_q, L0_xattn_w_k, L0_xattn_b_k, L0_xattn_w_v, L0_xattn_b_v, L0_xattn_w_o, L0_xattn_b_o, L0_ffn_Wg, L0_ffn_bg, L0_ffn_Wu, L0_ffn_bu, L0_ffn_Wd, L0_ffn_bd, L0_ffn_Wq, L0_ffn_keys, L0_ffn_down_embed, L0_ffn_up_embed, L1_xattn_w_kv, L1_xattn_w_q, L1_xattn_w_out1, L1_xattn_w_out2, L1_xattn_gamma, L1_ffn_W_exp, L1_ffn_b_exp, L1_ffn_up_weights, L1_ffn_up_bias, L1_ffn_down_weights, L1_ffn_W_con, L1_ffn_b_con, L1_ffn_down_bias):
    import jax
    import jax.numpy as jnp

    def _L0_xattn_ref(queries, keys, values, w_q, b_q, w_k, b_k, w_v, b_v, w_o, b_o):
        import jax, jax.numpy as jnp
        import numpy as np
        D_MODEL = 512
        NUM_HEADS = 16
        D_K = D_MODEL // NUM_HEADS

        def _split_heads(x):
            B, S, _ = x.shape
            return x.reshape(B, S, NUM_HEADS, D_K).transpose(0, 2, 1, 3)
        q = _split_heads(queries @ w_q.T + b_q)
        k = _split_heads(keys @ w_k.T + b_k)
        v = _split_heads(values @ w_v.T + b_v)
        scores = jnp.einsum('bhqd,bhkd->bhqk', q, k) / jnp.sqrt(jnp.asarray(D_K, q.dtype))
        weights = jax.nn.softmax(scores, axis=-1)
        attn = jnp.einsum('bhqk,bhkd->bhqd', weights, v)
        B, H, S, dk = attn.shape
        merged = attn.transpose(0, 2, 1, 3).reshape(B, S, H * dk)
        return merged @ w_o.T + b_o

    def _L0_ffn_ref(hidden_states, Wg, bg, Wu, bu, Wd, bd, Wq, keys, down_embed, up_embed):
        import jax, jax.numpy as jnp
        import numpy as np
        B, T, D = (2, 1024, 512)
        DCD = 2048
        RET = 128
        NEXP = 2048
        NKEYS = 64
        H = 4
        KPH = 8
        b, t, d = hidden_states.shape
        q = (hidden_states @ Wq).reshape(b, t, 2, H, RET // 2)
        sim = jnp.einsum('btphn,hkpn->pbthk', q, keys)
        sc, ix = jax.lax.top_k(sim, KPH)
        sx, sy = (sc[0], sc[1])
        ixx, ixy = (ix[0], ix[1])
        all_sc = (sx[..., :, None] + sy[..., None, :]).reshape(b, t, H, KPH * KPH)
        all_ix = (ixx[..., :, None] * NKEYS + ixy[..., None, :]).reshape(b, t, H, KPH * KPH)
        scores, pk = jax.lax.top_k(all_sc, KPH)
        idx = jnp.take_along_axis(all_ix, pk, axis=-1)
        de = down_embed[idx]
        ue = up_embed[idx]
        w = jnp.einsum('btd,bthkd->bthk', hidden_states, de)
        w = jax.nn.silu(w) * jax.nn.softmax(scores, axis=-1)
        experts_states = jnp.einsum('bthk,bthkd->btd', w, ue)
        mlp = jax.nn.silu(hidden_states @ Wg + bg) * (hidden_states @ Wu + bu) @ Wd + bd
        return mlp + experts_states

    def _L1_xattn_ref(x, context, w_kv, w_q, w_out1, w_out2, gamma):
        import jax, jax.numpy as jnp
        import numpy as np
        DIM = 512
        HEADS = 16
        HEAD_DIM = 64
        INNER = HEADS * HEAD_DIM

        def _split_heads(t):
            b, n, _ = t.shape
            return t.reshape(b, n, HEADS, HEAD_DIM).transpose(0, 2, 1, 3)
        scale = HEAD_DIM ** (-0.5)
        kv = context @ w_kv
        k, v = jnp.split(kv, 2, axis=-1)
        q = _split_heads(x @ w_q)
        k = _split_heads(k)
        v = _split_heads(v)
        dots = jnp.einsum('bhid,bhjd->bhij', q, k) * scale
        attn = jax.nn.softmax(dots, axis=-1)
        out = jnp.einsum('bhij,bhjd->bhid', attn, v)
        b, h, n, d = out.shape
        out = out.transpose(0, 2, 1, 3).reshape(b, n, h * d)
        out = jax.nn.relu(out @ w_out1) @ w_out2
        mean = jnp.mean(out, axis=-1, keepdims=True)
        var = jnp.var(out, axis=-1, keepdims=True)
        return (out - mean) * jax.lax.rsqrt(var + 1e-05) * gamma

    def _L1_ffn_ref(x, W_exp, b_exp, up_weights, up_bias, down_weights, W_con, b_con, down_bias):
        import jax, jax.numpy as jnp
        import numpy as np
        D_MODEL = 512
        EXPANSION = 4
        D_HIDDEN = D_MODEL * EXPANSION
        NUM_STAGES = int(np.log2(D_HIDDEN))

        def butterfly(y, weights, dim):
            lead = y.shape[:-1]
            for stage in range(weights.shape[0]):
                s = 2 ** stage
                nb = dim // (2 * s)
                yr = y.reshape(*lead, nb, 2, s)
                a = yr[..., 0, :]
                b = yr[..., 1, :]
                w = weights[stage].reshape(nb, s, 2, 2)
                na = w[..., 0, 0] * a + w[..., 0, 1] * b
                nb2 = w[..., 1, 0] * a + w[..., 1, 1] * b
                y = jnp.stack([na, nb2], axis=-2).reshape(*lead, dim)
            return y
        h = jnp.einsum('bsd,dh->bsh', x, W_exp) + b_exp
        h = butterfly(h, up_weights, D_HIDDEN)
        h = jax.nn.gelu(h + up_bias, approximate=False)
        h = butterfly(h, down_weights, D_HIDDEN)
        y = jnp.einsum('bsh,hd->bsd', h, W_con) + b_con
        return y + down_bias
    x = x + _L0_xattn_ref(_layernorm(x, axis=-1), ctx_1024, ctx_1024, L0_xattn_w_q, L0_xattn_b_q, L0_xattn_w_k, L0_xattn_b_k, L0_xattn_w_v, L0_xattn_b_v, L0_xattn_w_o, L0_xattn_b_o)
    x = x + _L0_ffn_ref(_layernorm(x, axis=-1), L0_ffn_Wg, L0_ffn_bg, L0_ffn_Wu, L0_ffn_bu, L0_ffn_Wd, L0_ffn_bd, L0_ffn_Wq, L0_ffn_keys, L0_ffn_down_embed, L0_ffn_up_embed)
    x = x + _L1_xattn_ref(_layernorm(x, axis=-1), ctx_1024, L1_xattn_w_kv, L1_xattn_w_q, L1_xattn_w_out1, L1_xattn_w_out2, L1_xattn_gamma)
    x = x + _L1_ffn_ref(_layernorm(x, axis=-1), L1_ffn_W_exp, L1_ffn_b_exp, L1_ffn_up_weights, L1_ffn_up_bias, L1_ffn_down_weights, L1_ffn_W_con, L1_ffn_b_con, L1_ffn_down_bias)
    return x

_drawn_inputs = setup_inputs


def setup_inputs(seed=0):
    import zlib

    import numpy as np

    out = dict(_drawn_inputs(seed))
    spreads = {'L0_xattn_b_q': (0.0, 0.587),
     'L0_xattn_b_k': (0.0, 0.8),
     'L0_xattn_b_v': (0.0, 0.1),
     'L0_xattn_b_o': (0.0, 0.1),
     'L0_ffn_bg': (0.0, 0.545),
     'L0_ffn_bu': (0.0, 0.556),
     'L0_ffn_bd': (0.0, 0.1),
     'L1_xattn_gamma': (1.0, 0.2),
     'L1_ffn_b_exp': (0.0, 0.1),
     'L1_ffn_up_bias': (0.0, 0.1),
     'L1_ffn_b_con': (0.0, 0.1),
     'L1_ffn_down_bias': (0.0, 0.1)}
    factors = {'L0_ffn_Wq': 8.0, 'L0_ffn_keys': 8.0, 'L0_ffn_down_embed': 8.0, 'L0_ffn_up_embed': 8.0}
    for name, (base, spread) in spreads.items():
        noise = np.random.default_rng([zlib.crc32(name.encode()), seed]).standard_normal(out[name].shape)
        drawn = base * np.exp(spread * noise) if base else spread * noise
        out[name] = jnp.asarray(drawn.astype(out[name].dtype))
    for name, factor in factors.items():
        out[name] = (out[name] * factor).astype(out[name].dtype)
    return out
```

```python
import concourse.bass as bass
from concourse import mybir
from contextlib import ExitStack

F32 = mybir.dt.float32
BF16 = mybir.dt.bfloat16
U32 = mybir.dt.uint32
ALU = mybir.AluOpType
ACT = mybir.ActivationFunctionType
AX = mybir.AxisListType

P = 128
D = 512
DC = D // P
TILES = 4
BLOCK = TILES * P
TOKENS = 4096
BLOCKS = TOKENS // BLOCK
BATCH = 2
CTX = 154
REM = CTX - P
HEADS = 16
GH = 4
GROUPS = HEADS // GH
UNITS = TILES * GROUPS
F = 2048
FI = F // P
EPS = 1e-5
KEYS = 64
RH = 4
TOPK = 8
NEXP = 2048
XROWS = NEXP // KEYS
STAGES = 11
LOW = -3.0e38


class Named(dict):

    def __init__(self, make):
        super().__init__()
        self.make = make

    def __missing__(self, name):
        self[name] = self.make(name)
        return self[name]


class Ring:

    def __init__(self, sem, name, buffers, uses, parts=1, drains=1):
        assert uses % len(buffers) == 0
        self.buffers, self.parts, self.drains, self.each = buffers, parts, drains, uses // len(buffers)
        self.filled = Named(lambda i: sem(f"{name}_filled{i}"))
        self.emptied = Named(lambda i: sem(f"{name}_emptied{i}"))

    def buf(self, n):
        return self.buffers[n % len(self.buffers)]

    def full(self, n):
        return self.filled[n % len(self.buffers)]

    def free(self, n):
        return self.emptied[n % len(self.buffers)]

    def fillings(self, it, n):
        return it * (self.each * self.parts) + (n // len(self.buffers) + 1) * self.parts

    def emptyings(self, it, n):
        return (it * self.each + n // len(self.buffers)) * self.drains

    def emptied_by(self, it, n):
        return it * (self.each * self.drains) + (n // len(self.buffers) + 1) * self.drains


class Steps:

    def __init__(self, sem, it, each):
        self.sem, self.it, self.each, self.n = sem, it, each, 0

    def give(self, ins):
        ins.then_inc(self.sem, 1)
        self.n += 1

    def level(self):
        return self.it * self.each + self.n

    def end(self):
        assert self.n == self.each, f"a pass gives {self.n} steps"


def make_sem(nc, ctx, prefix):
    return lambda name: ctx.enter_context(nc.semaphore(f"{prefix}_{name}"))


def hold(engine, sem, value, held):
    engine.wait_ge(sem, value)
    engine.sem_inc(held, 1)


def make_identity(pool, ident, zeroed, done):
    pool.memset(ident[:, :], 0.0).then_inc(zeroed, 1)
    pool.wait_ge(zeroed, 1)
    pool.affine_select(out=ident[:, :], in_=ident[:, :], compare_op=ALU.not_equal, fill=1.0, base=0,
                       pattern=[[-1, P]], channel_multiplier=1).then_inc(done, 1)


def prepare(nc, a, s):
    with ExitStack() as ctx:
        sem = make_sem(nc, s["sems"], "prep")
        sb = lambda name, shape, dt=F32: ctx.enter_context(nc.sbuf_tensor("prep_" + name, shape, dt))
        ctxT = sb("ctxT", [P, BATCH, DC, CTX])
        wk0 = sb("wk0", [P, DC, D])
        wv0 = sb("wv0", [P, DC, D])
        wkv1 = sb("wkv1", [P, DC, 2048])
        wqT = sb("wqT", [P, DC, D])
        keyz = sb("keyz", [P, RH, P])
        bk0 = sb("bk0", [P, DC])
        bv0 = sb("bv0", [P, D])
        kz = [sb(f"kz{i}", [P, BATCH, HEADS, CTX]) for i in range(2)]
        dks = (32, 64)
        vm = [sb(f"vm{i}", [P, BATCH, HEADS, dks[i] + 1]) for i in range(2)]
        vr = [sb(f"vr{i}", [REM, BATCH, HEADS, dks[i] + 1]) for i in range(2)]
        fold = sb("fold", [P, DC, D])
        banks = [ctx.enter_context(nc.psum_tensor(f"prep_ps{i}", [P, 512], F32)) for i in range(8)]
        loaded = sem("loaded")
        keys_loaded = sem("keys_loaded")
        zeroed = sem("zeroed")
        stored = sem("stored")

        jobs = [("fold", 0, 0, c) for c in range(DC)]
        for layer in range(2):
            for b in range(BATCH):
                jobs += [("k", layer, b, f) for f in range(HEADS * dks[layer] // P)]
                jobs += [("v", layer, b, (part, n)) for part in range(2) for n in range(HEADS * dks[layer] // 512)]
        jobs += [("pad", 0, 0, 0)] * (-len(jobs) % 8)
        ring = Ring(sem, "ps", banks, len(jobs))
        k_done, v_done = sem("k_done"), sem("v_done")
        n_k = sum(P // dks[j[1]] for j in jobs if j[0] == "k")
        n_v = sum(j[0] in ("v", "fold") for j in jobs)

        with nc.Block() as block:
            @block.sync
            def _(sp):
                sp.dma_start(ctxT[:, :, :, :], a["ctxT"].rearrange("b (c p) s -> p b c s", p=P)).then_inc(loaded, 16)
                for w, src in ((wk0, a["wkT0"]), (wv0, a["wvT0"]), (wkv1, a["wkv1"]), (wqT, a["WqT"])):
                    sp.dma_start(w[:, :, :], src.rearrange("(c p) n -> p c n", p=P)).then_inc(loaded, 16)
                sp.dma_start(bk0[:, :], a["bk0"]).then_inc(loaded, 16)
                sp.dma_start(bv0[:, :], a["bv0"].partition_broadcast(P)).then_inc(loaded, 16)
                sp.wait_ge(zeroed, 1)
                src = a["keysT"].rearrange("(g q n) k -> q n g k", q=2, n=KEYS)
                for q in range(2):
                    rows = slice(q * KEYS, (q + 1) * KEYS)
                    sp.dma_start(keyz[rows, :, rows], src[q]).then_inc(keys_loaded, 16)
                sp.wait_ge(k_done, n_k)
                sp.wait_ge(v_done, n_v)
                for layer in range(2):
                    sp.dma_start(s["kz"][layer].rearrange("b p n -> p b n"),
                                 kz[layer][:, :, :, :].rearrange("p b h k -> p b (h k)")).then_inc(stored, 16)
                    sp.dma_start(s["vm"][layer].rearrange("b p n -> p b n"),
                                 vm[layer][:, :, :, :].rearrange("p b h k -> p b (h k)")).then_inc(stored, 16)
                    sp.dma_start(s["vr"][layer].rearrange("b p n -> p b n"),
                                 vr[layer][:, :, :, :].rearrange("p b h k -> p b (h k)")).then_inc(stored, 16)
                sp.dma_start(s["fold"], fold[:, :, :].rearrange("p c n -> p (c n)")).then_inc(stored, 16)
                sp.wait_ge(stored, 7 * 16)

            @block.gpsimd
            def _(pool):
                pool.memset(keyz[:, :, :], 0.0).then_inc(zeroed, 1)
                for layer in range(2):
                    pool.memset(kz[layer][:, :, :, :], 0.0).then_inc(zeroed, 1)
                    pool.memset(vm[layer][:, :, :, dks[layer]:], 1.0).then_inc(zeroed, 1)
                    pool.memset(vr[layer][:, :, :, dks[layer]:], 1.0).then_inc(zeroed, 1)

            @block.tensor
            def _(pe):
                pe.wait_ge(loaded, 7 * 16)
                pe.wait_ge(keys_loaded, 32)
                for n, (kind, layer, b, i) in enumerate(jobs):
                    bank = ring.buf(n)
                    if n >= 8:
                        before = jobs[n - 8][0]
                        if before == "k":
                            pe.wait_ge(k_done, sum(P // dks[q[1]] for q in jobs[:n - 7] if q[0] == "k"))
                        else:
                            pe.wait_ge(v_done, sum(q[0] != "k" for q in jobs[:n - 7]))
                    if kind == "fold":
                        for g in range(RH):
                            last = pe.matmul(bank[:, g * P:(g + 1) * P], wqT[:, g, i * P:(i + 1) * P],
                                             keyz[:, g, :], start=True, stop=True)
                    elif kind == "k":
                        w = wkv1 if layer else wk0
                        for c in range(DC):
                            last = pe.matmul(bank[:, 0:CTX], w[:, c, i * P:(i + 1) * P], ctxT[:, b, c, :],
                                             start=c == 0, stop=c == DC - 1)
                    elif kind == "v":
                        part, m = i
                        rows = slice(0, P) if part == 0 else slice(P, CTX)
                        for c in range(DC):
                            w = wkv1[:, c, 1024 + m * 512:1024 + m * 512 + 512] if layer else wv0[:, c, :]
                            last = pe.matmul(bank[0:rows.stop - rows.start, :], ctxT[:, b, c, rows], w,
                                             start=c == 0, stop=c == DC - 1)
                    else:
                        continue
                    last.then_inc(ring.full(n), 1)

            @block.scalar
            def _(act):
                act.wait_ge(loaded, 7 * 16)
                act.wait_ge(zeroed, 7)
                for n, (kind, layer, b, i) in enumerate(jobs):
                    if kind != "k":
                        continue
                    dk = dks[layer]
                    per = P // dk
                    act.wait_ge(ring.full(n), ring.fillings(0, n))
                    for j in range(per):
                        rows = slice(j * dk, (j + 1) * dk)
                        bias = bk0[rows, i:i + 1] if layer == 0 else 0.0
                        last = act.activation(kz[layer][rows, b, i * per + j, :], ring.buf(n)[rows, 0:CTX],
                                              ACT.Identity, bias=bias)
                        last.then_inc(k_done, 1)

            @block.vector
            def _(dve):
                dve.wait_ge(loaded, 7 * 16)
                for n, (kind, layer, b, i) in enumerate(jobs):
                    if kind == "fold":
                        dve.wait_ge(ring.full(n), ring.fillings(0, n))
                        last = dve.tensor_copy(fold[:, i, :], ring.buf(n)[:, :])
                    elif kind == "v":
                        part, m = i
                        dk = dks[layer]
                        heads = slice(m * (512 // dk), (m + 1) * (512 // dk))
                        rows = P if part == 0 else REM
                        dve.wait_ge(ring.full(n), ring.fillings(0, n))
                        out = (vr if part else vm)[layer][0:rows, b, heads, 0:dk]
                        src = ring.buf(n)[0:rows, :].rearrange("p (h d) -> p h d", d=dk)
                        if layer == 0:
                            last = dve.tensor_tensor(out, src, bv0[0:rows, :].rearrange("p (h d) -> p h d", d=dk), ALU.add)
                        else:
                            last = dve.tensor_copy(out, src)
                    else:
                        continue
                    last.then_inc(v_done, 1)


def layernorm_stats(dve, st, tiles, stats, mv, var_ready, held):
    for t, x in enumerate(tiles):
        st.give(dve.bn_stats(stats[:, t, :], x))
    hold(dve, st.sem, st.level(), held)
    for t in range(len(tiles)):
        dve.bn_aggr(mv[:, t, :], stats[:, t, :]).then_inc(var_ready, 1)


def butterfly_stage(pool, y, w, s, transposed, t, done, base, held):
    st = 2 ** s
    v = y.rearrange("p (n two s) -> p n two s", two=2, s=st)
    lo, hi = v[:, :, 0, :], v[:, :, 1, :]
    rows = y.shape[0]
    wv = lambda i, j: w[0:rows, 2 * i + j, :].rearrange("p (n s) -> p n s", s=st)
    tv = lambda k: t[0:rows, k, :].rearrange("p (n s) -> p n s", s=st)
    w01, w10 = (wv(1, 0), wv(0, 1)) if transposed else (wv(0, 1), wv(1, 0))
    pool.tensor_tensor(tv(0), lo, wv(0, 0), ALU.mult).then_inc(done, 1)
    pool.tensor_tensor(tv(1), hi, w01, ALU.mult).then_inc(done, 1)
    pool.tensor_tensor(tv(2), lo, w10, ALU.mult).then_inc(done, 1)
    pool.tensor_tensor(tv(3), hi, wv(1, 1), ALU.mult).then_inc(done, 1)
    hold(pool, done, base + 4, held)
    pool.tensor_tensor(lo, tv(0), tv(1), ALU.add).then_inc(done, 1)
    pool.tensor_tensor(hi, tv(2), tv(3), ALU.add).then_inc(done, 1)
    hold(pool, done, base + 6, held)


def attention(nc, a, s, layer, x_in, x_out):
    dk = (32, 64)[layer]
    FT = HEADS * dk // P
    CG = FT // GROUPS
    VW = dk + 1
    pre = f"at{layer}"
    U_XT, U_Q = 0, DC
    U_PV = U_Q + FT
    U_OT = U_PV + UNITS
    U_R = U_OT + FT
    U_OUT = U_R + (DC if layer else 0)
    USES = U_OUT + TILES
    with ExitStack() as ctx:
        sem = make_sem(nc, s["sems"], pre)
        sb = lambda name, shape, dt=F32: ctx.enter_context(nc.sbuf_tensor(f"{pre}_{name}", shape, dt))
        ident = sb("ident", [P, P])
        eps = sb("eps", [P, 1])
        wq = sb("wq", [P, DC, HEADS * dk])
        wo = sb("wo", [P, FT, D])
        xin = sb("xin", [P, TILES, D])
        xres = sb("xres", [P, TILES, D])
        xn = sb("xn", [P, TILES, D])
        xnT = sb("xnT", [P, DC, BLOCK])
        qT = sb("qT", [P, FT, BLOCK])
        kz = sb("kz", [P, HEADS, CTX])
        vm = sb("vm", [P, HEADS, VW])
        vr = sb("vr", [GH * REM, GROUPS, GH, VW])
        probs = [sb(f"probs{i}", [P, GH, CTX]) for i in range(4)]
        tails = [sb(f"tails{i}", [P, GH * REM]) for i in range(4)]
        ptS = [sb(f"ptS{i}", [P, GH + 1, P]) for i in range(2)]
        o = sb("o", [P, TILES, HEADS, dk])
        oT = qT
        stats, mv = sb("stats", [P, TILES, 6]), sb("mv", [P, TILES, 2])
        std, rstd = sb("std", [P, TILES]), sb("rstd", [P, TILES])
        mx, rz = sb("mx", [P, 2, GH]), sb("rz", [P, 2, GH])
        if layer:
            w2 = sb("w2", [P, DC, D])
            rT = xnT
            row = sb("gamma", [P, D])
            y = xn
            bst, bmv = sb("bst", [P, TILES, 6]), sb("bmv", [P, TILES, 2])
            bstd, brstd = sb("bstd", [P, TILES]), sb("brstd", [P, TILES])
        else:
            bq = sb("bq", [P, FT])
            bqs = sb("bqs", [P, FT])
            row = sb("bo", [P, D])
        bw = sb("bw", [P, 4, 1024])
        bt = sb("bt", [P, 4, 1024])
        by = sb("by", [P, DC, F])
        bias_row, up_row = by[0:1, 0, :], by[0:1, 1, :]

        ps = lambda name, shape: ctx.enter_context(nc.psum_tensor(f"{pre}_{name}", shape, F32))
        score = Ring(sem, "score", [ps(f"score{i}", [P, 2, 512]) for i in range(2)], UNITS)
        pt = Ring(sem, "pt", [ps("pt", [P, 2, 512])], UNITS, drains=2)
        acc = Ring(sem, "acc", [ps(f"acc{i}", [P, 512]) for i in range(2)], USES)

        z = Named(sem)

        with nc.Block() as block:
            @block.sync
            def _(sp):
                sp.dma_start(xin[:, :, :], x_in[0].rearrange("p t d -> p (t d)")).then_inc(z["x_loaded"], 16)
                sp.dma_start(wq[:, :, :], a[f"wq{layer}"].rearrange("(c p) n -> p c n", p=P)).then_inc(z["w_loaded"], 16)
                sp.dma_start(wo[:, :, :], a[f"wo{layer}"].rearrange("(c p) n -> p c n", p=P)).then_inc(z["w_loaded"], 16)
                if layer:
                    sp.dma_start(w2[:, :, :], a["w2"].rearrange("(c p) n -> p c n", p=P)).then_inc(z["w_loaded"], 16)
                    sp.dma_start(row[:, :], a["gamma"].partition_broadcast(P)).then_inc(z["w_loaded"], 16)
                else:
                    sp.dma_start(bq[:, :], a["bq0"]).then_inc(z["w_loaded"], 16)
                    sp.dma_start(row[:, :], a["bo0"].partition_broadcast(P)).then_inc(z["w_loaded"], 16)
                sp.wait_ge(z["vr_zeroed"], 1)

                def load_kv(b):
                    sp.dma_start(kz[:, :, :], s["kz"][layer][b].rearrange("a p n -> (a p) n")).then_inc(z["kv_loaded"], 16)
                    sp.dma_start(vm[:, :, :], s["vm"][layer][b].rearrange("a p n -> (a p) n")).then_inc(z["kv_loaded"], 16)
                    src = s["vr"][layer][b].rearrange("a p (g j v) -> (a p) g j v", g=GROUPS, j=GH)
                    for j in range(GH):
                        sp.dma_start(vr[REM * j:REM * (j + 1), :, j, :], src[:, :, j, :]).then_inc(z["kv_loaded"], 16)

                load_kv(slice(0, 1))

                def block_io(it, more):
                    sp.wait_ge(z["xn_ready"], (it + 1) * TILES)
                    if more:
                        sp.dma_start(xin[:, :, :], x_in[bass.ds(it + 1, 1)].rearrange("a p t d -> (a p) (t d)")).then_inc(z["x_loaded"], 16)
                    if not isinstance(it, int) or it:
                        sp.wait_ge(z["stored"], it * 16)
                    sp.dma_start(xres[:, :, :], x_in[bass.ds(it, 1)].rearrange("a p t d -> (a p) (t d)")).then_inc(z["res_loaded"], 16)
                    if more:
                        sp.wait_ge(acc.free(U_OT - 1), acc.emptied_by(it, U_OT - 1))
                        load_kv(bass.ds((it + 1) // (BLOCKS // BATCH), 1))
                    if layer:
                        sp.wait_ge(z["out_ready"], (it + 1) * TILES)
                    else:
                        for n in (USES - 2, USES - 1):
                            sp.wait_ge(acc.free(n), acc.emptied_by(it, n))
                    sp.dma_start(x_out[bass.ds(it, 1)].rearrange("a p t d -> (a p) (t d)"), xres[:, :, :]).then_inc(z["stored"], 16)

                block_io(0, True)
                with sp.Fori(1, BLOCKS - 1) as it:
                    block_io(it, True)
                block_io(BLOCKS - 1, False)
                sp.wait_ge(z["stored"], BLOCKS * 16)

            @block.tensor
            def _(pe):
                pe.wait_ge(z["w_loaded"], 64)
                pe.wait_ge(z["id_done"], 1)
                with pe.Fori(0, BLOCKS) as it:
                    def take(n):
                        if n >= 2:
                            pe.wait_ge(acc.free(n), acc.emptyings(it, n))
                        return acc.buf(n)

                    def made(n):
                        for m in (n - 1, n):
                            pe.wait_ge(acc.free(m), acc.emptied_by(it, m))

                    pe.wait_ge(z["xn_ready"], (it + 1) * TILES)
                    for c in range(DC):
                        bank = take(U_XT + c)
                        for t in range(TILES):
                            last = pe.transpose(bank[:, t * P:(t + 1) * P], xn[:, t, c * P:(c + 1) * P], ident[:, :])
                        last.then_inc(acc.full(U_XT + c), 1)
                    made(U_Q - 1)
                    for f in range(FT):
                        bank = take(U_Q + f)
                        for c in range(DC):
                            last = pe.matmul(bank[:, :], wq[:, c, f * P:(f + 1) * P], xnT[:, c, :],
                                             start=c == 0, stop=c == DC - 1)
                        last.then_inc(acc.full(U_Q + f), 1)
                    made(U_PV - 1)
                    pe.wait_ge(z["kv_loaded"], (it + 1) * 16 * (2 + GH))

                    def scores(u):
                        t, g = divmod(u, GROUPS)
                        if u >= 2:
                            pe.wait_ge(score.free(u), score.emptyings(it, u))
                        for half in range(2):
                            f = g * CG + half * (CG - 1)
                            h = g * GH + 2 * half
                            last = pe.matmul(score.buf(u)[:, half, 0:2 * CTX], qT[:, f, t * P:(t + 1) * P],
                                             kz[:, h:h + 2, :], start=True, stop=True)
                        last.then_inc(score.full(u), 1)

                    def turn(u):
                        pe.wait_ge(z["exp_done"], (it * UNITS + u + 1) * 2)
                        if u >= 1:
                            pe.wait_ge(pt.free(u), pt.emptyings(it, u))
                        p = probs[u % 4]
                        for j in range(GH):
                            pe.transpose(pt.buf(u)[:, 0, j * P:(j + 1) * P], p[:, j, 0:P], ident[:, :])
                        pe.transpose(pt.buf(u)[0:GH * REM, 1, 0:P], tails[u % 4][:, :], ident[:, :]).then_inc(pt.full(u), 1)

                    def weigh(u):
                        g = u % GROUPS
                        pe.wait_ge(pt.free(u), pt.emptied_by(it, u))
                        bank = take(U_PV + u)
                        pT = ptS[u % 2]
                        pe.matmul(bank[:, 0:GH * VW], pT[0:GH * REM, GH, :], vr[:, g, :, :], start=True, stop=False)
                        for j in range(GH):
                            last = pe.matmul(bank[:, j * VW:(j + 1) * VW], pT[:, j, :], vm[:, g * GH + j, :],
                                             start=False, stop=j == GH - 1)
                        last.then_inc(acc.full(U_PV + u), 1)

                    for u in range(UNITS + 3):
                        if u < UNITS:
                            scores(u)
                        if 2 <= u < UNITS + 2:
                            turn(u - 2)
                        if u >= 3:
                            weigh(u - 3)
                    made(U_OT - 1)
                    hc = P // dk
                    for c in range(FT):
                        bank = take(U_OT + c)
                        for t in range(TILES):
                            last = pe.transpose(bank[:, t * P:(t + 1) * P], o[:, t, c * hc:(c + 1) * hc, :], ident[:, :])
                        last.then_inc(acc.full(U_OT + c), 1)
                    made(U_R - 1)
                    if layer:
                        for f in range(DC):
                            bank = take(U_R + f)
                            for c in range(FT):
                                last = pe.matmul(bank[:, :], wo[:, c, f * P:(f + 1) * P], oT[:, c, :],
                                                 start=c == 0, stop=c == FT - 1)
                            last.then_inc(acc.full(U_R + f), 1)
                        made(U_OUT - 1)
                    src, w, n = (rT, w2, DC) if layer else (oT, wo, FT)
                    for t in range(TILES):
                        bank = take(U_OUT + t)
                        for c in range(n):
                            last = pe.matmul(bank[:, :], src[:, c, t * P:(t + 1) * P], w[:, c, :],
                                             start=c == 0, stop=c == n - 1)
                        last.then_inc(acc.full(U_OUT + t), 1)

            @block.scalar
            def _(act):
                act.wait_ge(z["eps_done"], 1)
                act.wait_ge(z["w_loaded"], 64)
                scale = float(dk) ** -0.5
                if not layer:
                    act.mul(bqs[:, :], bq[:, :], scale).then_inc(z["bqs_done"], 1)
                    act.wait_ge(z["bqs_done"], 1)
                with act.Fori(0, BLOCKS) as it:
                    act.wait_ge(z["var_ready"], (it + 1) * TILES)
                    act.activation(std[:, :], mv[:, :, 1], ACT.Sqrt, bias=eps[:, :]).then_inc(z["std_ready"], 1)

                    def drain(n, out, func=ACT.Copy, **kw):
                        act.wait_ge(acc.full(n), acc.fillings(it, n))
                        act.activation(out, acc.buf(n)[:, :], func, **kw).then_inc(acc.free(n), 1)

                    for c in range(DC):
                        drain(U_XT + c, xnT[:, c, :])
                    for f in range(FT):
                        kw = {"bias": bqs[:, f:f + 1]} if not layer else {}
                        drain(U_Q + f, qT[:, f, :], ACT.Identity, scale=scale, **kw)
                    for u in range(UNITS + 2):
                        if u < UNITS:
                            act.wait_ge(score.free(u), score.emptied_by(it, u))
                            p = probs[u % 4]
                            act.activation(p[:, :, 0:P], p[:, :, 0:P], ACT.Exp).then_inc(z["exp_done"], 1)
                            act.activation(tails[u % 4][:, :].rearrange("p (j k) -> p j k", j=GH), p[:, :, P:CTX],
                                           ACT.Exp).then_inc(z["exp_done"], 1)
                        if u >= 2:
                            n = u - 2
                            act.wait_ge(pt.full(n), pt.fillings(it, n))
                            act.copy(ptS[n % 2][:, 0:GH, :], pt.buf(n)[:, 0, :].rearrange("p (j k) -> p j k", j=GH)).then_inc(pt.free(n), 1)
                            act.copy(ptS[n % 2][0:GH * REM, GH, :], pt.buf(n)[0:GH * REM, 1, 0:P]).then_inc(pt.free(n), 1)
                    for c in range(FT):
                        drain(U_OT + c, oT[:, c, :])
                    if layer:
                        for f in range(DC):
                            drain(U_R + f, rT[:, f, :], ACT.Relu)
                        for t in range(TILES):
                            act.wait_ge(z["y_var"], it * TILES + t + 1)
                            act.activation(bstd[:, t:t + 1], bmv[:, t, 1:2], ACT.Sqrt, bias=eps[:, :]).then_inc(z["y_std"], 1)

            @block.vector
            def _(dve):
                dve.memset(eps[:, :], EPS).then_inc(z["eps_done"], 1)
                dve.memset(vr[:, :, :, :], 0.0).then_inc(z["vr_zeroed"], 1)
                dve.wait_ge(z["w_loaded"], 64)
                with dve.Fori(0, BLOCKS) as it:
                    st = Steps(z["dve_step"], it, DVE_STEPS[layer])
                    dve.wait_ge(z["x_loaded"], (it + 1) * 16)
                    layernorm_stats(dve, st, [xin[:, t, :] for t in range(TILES)], stats, mv, z["var_ready"], z["dve_held"])
                    dve.wait_ge(z["std_ready"], it + 1)
                    st.give(dve.reciprocal(rstd[:, :], std[:, :]))
                    dve.wait_ge(st.sem, st.level())
                    for t in range(TILES):
                        dve.tensor_scalar(xn[:, t, :], xin[:, t, :], mv[:, t, 0:1], rstd[:, t:t + 1],
                                          ALU.subtract, ALU.mult).then_inc(z["xn_ready"], 1)
                    dve.wait_ge(z["res_loaded"], (it + 1) * 16)

                    def shift(u):
                        m = mx[:, u % 2, :]
                        sc = score.buf(u)[:, :, 0:2 * CTX]
                        dve.wait_ge(score.full(u), score.fillings(it, u))
                        st.give(dve.tensor_reduce(m.rearrange("p (a b) -> p a b", a=2),
                                                  sc.rearrange("p a (b k) -> p a b k", b=2), AX.X, ALU.max))
                        dve.wait_ge(st.sem, st.level())
                        out = probs[u % 4][:, :, :].rearrange("p (a b) k -> p a b k", a=2)
                        top = m.rearrange("p (a b) -> p a b", a=2).unsqueeze(3).broadcast_to([P, 2, 2, CTX])
                        dve.tensor_tensor(out, sc.rearrange("p a (b k) -> p a b k", b=2), top,
                                          ALU.subtract).then_inc(score.free(u), 1)

                    def normalise(u):
                        t, g = divmod(u, GROUPS)
                        n = U_PV + u
                        v = acc.buf(n)[:, 0:GH * VW].rearrange("p (j v) -> p j v", v=VW)
                        dve.wait_ge(acc.full(n), acc.fillings(it, n))
                        st.give(dve.reciprocal(rz[:, u % 2, :].unsqueeze(2), v[:, :, dk:VW]))
                        dve.wait_ge(st.sem, st.level())
                        dve.tensor_tensor(o[:, t, g * GH:(g + 1) * GH, :], v[:, :, 0:dk],
                                          rz[:, u % 2, :].unsqueeze(2).broadcast_to([P, GH, dk]), ALU.mult).then_inc(acc.free(n), 1)

                    for u in range(UNITS + 3):
                        if u < UNITS:
                            shift(u)
                        if u >= 3:
                            normalise(u - 3)
                    if not layer:
                        for t in range(TILES):
                            st.give(dve.tensor_tensor(xres[:, t, :], xres[:, t, :], row[:, :], ALU.add))
                        dve.wait_ge(st.sem, st.level())
                    for t in range(TILES):
                        n = U_OUT + t
                        bank = acc.buf(n)
                        dve.wait_ge(acc.full(n), acc.fillings(it, n))
                        if not layer:
                            dve.tensor_tensor(xres[:, t, :], bank[:, :], xres[:, t, :], ALU.add).then_inc(acc.free(n), 1)
                            continue
                        st.give(dve.bn_stats(bst[:, t, :], bank[:, :]))
                        hold(dve, st.sem, st.level(), z["dve_held"])
                        dve.bn_aggr(bmv[:, t, :], bst[:, t, :]).then_inc(z["y_var"], 1)
                        dve.wait_ge(z["y_std"], it * TILES + t + 1)
                        st.give(dve.reciprocal(brstd[:, t:t + 1], bstd[:, t:t + 1]))
                        dve.wait_ge(st.sem, st.level())
                        yt = y[:, t, :]
                        dve.tensor_scalar(yt, bank[:, :], bmv[:, t, 0:1], brstd[:, t:t + 1], ALU.subtract,
                                          ALU.mult).then_inc(acc.free(n), 1)
                        dve.wait_ge(acc.free(n), acc.emptied_by(it, n))
                        st.give(dve.tensor_tensor(yt, yt, row[:, :], ALU.mult))
                        dve.wait_ge(st.sem, st.level())
                        dve.tensor_tensor(xres[:, t, :], xres[:, t, :], yt, ALU.add).then_inc(z["out_ready"], 1)
                    st.end()

            @block.gpsimd
            def _(pool):
                make_identity(pool, ident, z["id_zeroed"], z["id_done"])
                weights = a["down_w"] if layer else a["up_w"]
                pool.dma_start(by[:, :, :], a["W_conT" if layer else "W_exp"].rearrange("(c p) n -> p c n", p=P)).then_inc(z["bf_x"], 16)
                pool.wait_ge(z["bf_x"], 16)
                n_w = 0
                steps = 0
                for k in range(STAGES):
                    sidx = STAGES - 1 - k if layer else k
                    pool.dma_start(bw[:, :, :], weights[sidx].partition_broadcast(P)).then_inc(z["bf_w"], 16)
                    n_w += 16
                    pool.wait_ge(z["bf_w"], n_w)
                    with pool.Fori(0, DC) as r:
                        butterfly_stage(pool, by[:, bass.ds(r, 1), :].rearrange("p a n -> p (a n)"), bw, sidx, bool(layer),
                                        bt, z["bf_step"], r * 6 + steps, z["pool_held"])
                    steps += 6 * DC
                pool.dma_start(s["wcon" if layer else "wexp"], by[:, :, :].rearrange("p c n -> p (c n)")).then_inc(z["bf_out"], 16)
                pool.wait_ge(z["bf_out"], 16)
                if layer:
                    pool.dma_start(bias_row, a["b_exp"]).then_inc(z["bf_x"], 16)
                    pool.dma_start(up_row, a["up_bias"]).then_inc(z["bf_x"], 16)
                    pool.wait_ge(z["bf_x"], 48)
                    for k in range(STAGES):
                        pool.dma_start(bw[0:1, :, :], a["up_w"][k].unsqueeze(0)).then_inc(z["bf_w"], 16)
                        n_w += 16
                        pool.wait_ge(z["bf_w"], n_w)
                        butterfly_stage(pool, bias_row, bw, k, False, bt, z["bf_step"], steps, z["pool_held"])
                        steps += 6
                    pool.tensor_tensor(bias_row, bias_row, up_row, ALU.add).then_inc(z["bf_step"], 1)
                    pool.wait_ge(z["bf_step"], steps + 1)
                    pool.dma_start(s["bexp"], bias_row).then_inc(z["bf_out"], 16)
                    pool.wait_ge(z["bf_out"], 32)


DVE_STEPS = (41, 49)


def ffn0(nc, a, s, x_in, x_out):
    pre = "ff0"
    XH = RH * XROWS
    W_USES = DC + TILES + 2 * FI + 2 * FI
    U_XT, U_SIM, U_GU, U_ST = 0, DC, DC + TILES, DC + TILES + 2 * FI
    with ExitStack() as ctx:
        sem = make_sem(nc, s["sems"], pre)
        sb = lambda name, shape, dt=F32: ctx.enter_context(nc.sbuf_tensor(f"{pre}_{name}", shape, dt))
        ident = sb("ident", [P, P])
        eps = sb("eps", [P, 1])
        downT = sb("downT", [P, DC, NEXP])
        up = sb("up", [P, FI, D])
        fold = sb("fold", [P, DC, D])
        bg, bu, bd = sb("bg", [P, FI]), sb("bu", [P, FI]), sb("bd", [P, D])
        xin, xres, xn = (sb(n, [P, TILES, D]) for n in ("xin", "xres", "xn"))
        xnT = sb("xnT", [P, DC, BLOCK])
        stats, mv = sb("stats", [P, TILES, 6]), sb("mv", [P, TILES, 2])
        std, rstd = sb("std", [P, TILES]), sb("rstd", [P, TILES])
        sim = xn[:, :, :].rearrange("p t (g k) -> p t g k", k=KEYS)
        G = sb("G", [P, TILES, NEXP])
        best = sb("best", [P, 2, 2 * RH, TOPK])
        place = sb("place", [P, 2, 2 * RH, TOPK], U32)
        placef = sb("placef", [P, 2, 2 * RH, TOPK], BF16)
        pair = sb("pair", [P, 2, RH, TOPK, TOPK])
        best2 = sb("best2", [P, 2, RH, TOPK])
        struck = sb("struck", [P, 2, RH, TOPK, TOPK])
        picked = sb("picked", [P, 2, RH, TOPK, TOPK])
        count = sb("count", [P, 2, RH, TOPK], BF16)
        ex = sb("ex", [P, 2, 2 * RH, KEYS])
        ebest = sb("ebest", [P, 2, 2 * RH, TOPK])
        rows_w = sb("rows_w", [P, 2, RH, TOPK])
        norm = sb("norm", [P, 2, 2, RH])
        beyond = sb("beyond", [P, 2, RH, TOPK])
        beyond_w = sb("beyond_w", [P, 2, 1])
        exn = sb("exn", [P, 2, RH, XROWS])
        hot = sb("hot", [P, RH, KEYS, TOPK], BF16)
        cx = sb("cx", [P, 2, RH, XROWS])
        qy = sb("qy", [P, 2, RH, KEYS])
        index = sb("index", [P, KEYS, TOPK], BF16)
        falling = sb("falling", [P, TOPK], BF16)
        ps = lambda name: ctx.enter_context(nc.psum_tensor(f"{pre}_{name}", [P, 512], F32))
        work = Ring(sem, "work", [ps(f"work{i}") for i in range(4)], W_USES)
        MOVED = U_GU // 4
        accs = [ps(f"acc{i}") for i in range(TILES)]
        gu_w = Ring(sem, "gu_w", [sb(f"gu_w{i}", [P, 2, DC, P]) for i in range(2)], FI, parts=32)
        wd_w = Ring(sem, "wd_w", [sb(f"wd_w{i}", [P, D]) for i in range(2)], FI, parts=16)
        silu = Ring(sem, "silu", [sb(f"silu{i}", [P, BLOCK]) for i in range(2)], 2 * FI)
        hid = Ring(sem, "hid", [sb(f"hid{i}", [P, BLOCK]) for i in range(2)], 2 * FI)
        reach = Ring(sem, "reach", [sb(f"reach{i}", [P, XROWS, KEYS], BF16) for i in range(2)], RH * TILES)
        outer = Ring(sem, "outer", [sb(f"outer{i}", [P, XROWS, KEYS]) for i in range(2)], RH * TILES)
        z = Named(sem)

        with nc.Block() as block:
            @block.sync
            def _(sp):
                sp.dma_start(xin[:, :, :], x_in[0].rearrange("p t d -> p (t d)")).then_inc(z["x_loaded"], 16)
                sp.dma_start(fold[:, :, :], s["fold"].rearrange("p (c n) -> p c n", c=DC)).then_inc(z["w_loaded"], 16)
                for t, name in ((bg, "bg"), (bu, "bu")):
                    sp.dma_start(t[:, :], a[name]).then_inc(z["w_loaded"], 16)
                sp.dma_start(bd[:, :], a["bd"].partition_broadcast(P)).then_inc(z["w_loaded"], 16)

                def load_gu(it, i):
                    if i >= 2:
                        n = U_GU + 2 * (i - 2) + 1
                        sp.wait_ge(work.full(n), work.fillings(it, n))
                    elif not isinstance(it, int) or it:
                        n = U_GU + 2 * (FI - 2 + i) + 1
                        sp.wait_ge(work.full(n), work.fillings(it - 1, n))
                    for k, w in enumerate(("Wg", "Wu")):
                        sp.dma_start(gu_w.buf(i)[:, k, :, :], a[w][i]).then_inc(gu_w.full(i), 16)

                def load_wd(it, i):
                    sp.wait_ge(wd_w.free(i), wd_w.emptyings(it, i))
                    sp.dma_start(wd_w.buf(i)[:, :], a["Wd"][i]).then_inc(wd_w.full(i), 16)

                def block_io(it, more):
                    for i in range(2):
                        load_gu(it, i)
                        load_wd(it, i)
                    if isinstance(it, int) and it == 0:
                        sp.dma_start(downT[:, :, :], a["downT"].rearrange("(c p) n -> p c n", p=P)).then_inc(z["w_loaded"], 16)
                        sp.dma_start(up[:, :, :], a["up"].rearrange("(c p) n -> p c n", p=P)).then_inc(z["w_loaded"], 16)
                    sp.wait_ge(z["xn_ready"], (it + 1) * TILES)
                    if more:
                        sp.dma_start(xin[:, :, :], x_in[bass.ds(it + 1, 1)].rearrange("a p t d -> (a p) (t d)")).then_inc(z["x_loaded"], 16)
                    if not isinstance(it, int) or it:
                        sp.wait_ge(z["stored"], it * 16)
                    sp.dma_start(xres[:, :, :], x_in[bass.ds(it, 1)].rearrange("a p t d -> (a p) (t d)")).then_inc(z["res_loaded"], 16)
                    for i in range(2, FI):
                        load_gu(it, i)
                        load_wd(it, i)
                    sp.wait_ge(z["out_ready"], (it + 1) * TILES)
                    sp.dma_start(x_out[bass.ds(it, 1)].rearrange("a p t d -> (a p) (t d)"), xres[:, :, :]).then_inc(z["stored"], 16)

                block_io(0, True)
                with sp.Fori(1, BLOCKS - 1) as it:
                    block_io(it, True)
                block_io(BLOCKS - 1, False)
                sp.wait_ge(z["stored"], BLOCKS * 16)

            @block.tensor
            def _(pe):
                pe.wait_ge(z["w_loaded"], 6 * 16)
                pe.wait_ge(z["id_done"], 1)
                with pe.Fori(0, BLOCKS) as it:
                    def take(n):
                        k = (n - U_GU) // 2 - 2
                        reader = hid if n % 2 else silu
                        if n < DC:
                            pass
                        elif k < 0:
                            pe.wait_ge(work.free(n), it * MOVED + (1 if n < U_GU else MOVED))
                        else:
                            pe.wait_ge(reader.full(k), reader.fillings(it, k))
                        return work.buf(n)

                    pe.wait_ge(z["xn_ready"], (it + 1) * TILES)
                    for c in range(DC):
                        bank = take(U_XT + c)
                        for t in range(TILES):
                            last = pe.transpose(bank[:, t * P:(t + 1) * P], xn[:, t, c * P:(c + 1) * P], ident[:, :])
                        last.then_inc(work.full(U_XT + c), 1)
                    for n in range(U_XT, U_SIM):
                        pe.wait_ge(work.free(n), it * MOVED + 1)
                    for t in range(TILES):
                        bank = take(U_SIM + t)
                        for c in range(DC):
                            last = pe.matmul(bank[:, :], xnT[:, c, t * P:(t + 1) * P], fold[:, c, :],
                                             start=c == 0, stop=c == DC - 1)
                        last.then_inc(work.full(U_SIM + t), 1)

                    def product(n, w):
                        bank = take(n)
                        for c in range(DC):
                            last = pe.matmul(bank[:, :], w(c), xnT[:, c, :], start=c == 0, stop=c == DC - 1)
                        last.then_inc(work.full(n), 1)

                    def accumulate(k, w):
                        pe.wait_ge(hid.full(k), hid.fillings(it, k))
                        h = hid.buf(k)
                        for t in range(TILES):
                            last = pe.matmul(accs[t][:, :], h[:, t * P:(t + 1) * P], w, start=k == 0, stop=k == 2 * FI - 1)
                            if k == 2 * FI - 1:
                                last.then_inc(z["summed"], 1)
                        return last

                    for i in range(FI + 1):
                        if i < FI:
                            pe.wait_ge(gu_w.full(i), gu_w.fillings(it, i))
                            w = gu_w.buf(i)
                            product(U_GU + 2 * i, lambda c: w[:, 0, c, :])
                            bank = take(U_GU + 2 * i + 1)
                            for c in range(DC):
                                last = pe.matmul(bank[:, :], w[:, 1, c, :], xnT[:, c, :], start=c == 0, stop=c == DC - 1)
                            last.then_inc(work.full(U_GU + 2 * i + 1), 1)
                        if i:
                            k = i - 1
                            pe.wait_ge(wd_w.full(k), wd_w.fillings(it, k))
                            accumulate(k, wd_w.buf(k)[:, :]).then_inc(wd_w.free(k), 1)
                    pe.wait_ge(z["G_ready"], (it + 1) * TILES)
                    for i in range(FI + 1):
                        if i < FI:
                            product(U_ST + 2 * i, lambda c: downT[:, c, i * P:(i + 1) * P])
                            bank = take(U_ST + 2 * i + 1)
                            for t in range(TILES):
                                last = pe.transpose(bank[:, t * P:(t + 1) * P], G[:, t, i * P:(i + 1) * P], ident[:, :])
                            last.then_inc(work.full(U_ST + 2 * i + 1), 1)
                        if i:
                            last = accumulate(FI + i - 1, up[:, i - 1, :])
                            if i <= FI - 2:
                                last.then_inc(z["spent"], 1)

            @block.scalar
            def _(act):
                act.wait_ge(z["eps_done"], 1)
                act.wait_ge(z["w_loaded"], 6 * 16)
                with act.Fori(0, BLOCKS) as it:
                    act.wait_ge(z["var_ready"], (it + 1) * TILES)
                    act.activation(std[:, :], mv[:, :, 1], ACT.Sqrt, bias=eps[:, :]).then_inc(z["std_ready"], 1)
                    for c in range(DC):
                        act.wait_ge(work.full(c), work.fillings(it, c))
                        act.copy(xnT[:, c, :], work.buf(c)[:, :]).then_inc(work.free(c), 1)
                    for t in range(TILES):
                        n = U_SIM + t
                        act.wait_ge(work.full(n), work.fillings(it, n))
                        act.copy(sim[:, t, :, :], work.buf(n)[:, :].rearrange("p (g k) -> p g k", k=KEYS)).then_inc(work.free(n), 1)

                    def silu_of(n, k, bias):
                        act.wait_ge(work.full(n), work.fillings(it, n))
                        if k >= 2:
                            act.wait_ge(hid.full(k - 2), hid.fillings(it, k - 2))
                        act.activation(silu.buf(k)[:, :], work.buf(n)[:, :], ACT.Silu, bias=bias).then_inc(silu.full(k), 1)

                    for t in range(TILES):
                        act.wait_ge(z["diff_ready"], (it * TILES + t + 1) * 2)
                        act.activation(ex[:, t % 2, :, :], ex[:, t % 2, :, :], ACT.Exp).then_inc(z["exp_done"], 1)
                        act.activation(ebest[:, t % 2, :, :], ebest[:, t % 2, :, :], ACT.Exp).then_inc(z["exp_done"], 1)
                        for i in range(t * RH, (t + 1) * RH):
                            silu_of(U_GU + 2 * i, i, bg[:, i:i + 1])
                    for i in range(FI):
                        silu_of(U_ST + 2 * i, FI + i, 0.0)

            @block.gpsimd
            def _(pool):
                make_identity(pool, ident, z["id_zeroed"], z["id_done"])
                pool.iota(index[:, :, :], [[1, KEYS], [0, TOPK]], base=0, channel_multiplier=0,
                          allow_small_or_imprecise_dtypes=True).then_inc(z["const_done"], 1)
                pool.iota(falling[:, :], [[-1, TOPK]], base=TOPK, channel_multiplier=0,
                          allow_small_or_imprecise_dtypes=True).then_inc(z["const_done"], 1)
                with pool.Fori(0, BLOCKS) as it:
                    for t in range(TILES):
                        pool.wait_ge(z["sel_ready"], (it * TILES + t + 1) * 3)
                        for h in range(RH):
                            n = t * RH + h
                            wide = lambda v: v.unsqueeze(2).broadcast_to([P, XROWS, KEYS])
                            flat = lambda v: v.unsqueeze(1).broadcast_to([P, XROWS, KEYS])
                            if n >= 2:
                                pool.wait_ge(z["spread"], it * RH * TILES + n - 1)
                            pool.tensor_tensor(reach.buf(n)[:, :, :], wide(cx[:, t % 2, h, :]), flat(qy[:, t % 2, h, :]),
                                               ALU.add).then_inc(reach.full(n), 1)
                            pool.tensor_tensor(outer.buf(n)[:, :, :], wide(exn[:, t % 2, h, :]), flat(ex[:, t % 2, RH + h, :]),
                                               ALU.mult).then_inc(outer.full(n), 1)

            @block.vector
            def _(dve):
                dve.memset(eps[:, :], EPS).then_inc(z["eps_done"], 1)
                dve.wait_ge(z["const_done"], 2)
                dve.wait_ge(z["w_loaded"], 6 * 16)
                with dve.Fori(0, BLOCKS) as it:
                    st = Steps(z["dve_step"], it, FF0_STEPS)
                    dve.wait_ge(z["x_loaded"], (it + 1) * 16)
                    layernorm_stats(dve, st, [xin[:, t, :] for t in range(TILES)], stats, mv, z["var_ready"], z["dve_held"])
                    dve.wait_ge(z["std_ready"], it + 1)
                    st.give(dve.reciprocal(rstd[:, :], std[:, :]))
                    dve.wait_ge(st.sem, st.level())
                    for t in range(TILES):
                        dve.tensor_scalar(xn[:, t, :], xin[:, t, :], mv[:, t, 0:1], rstd[:, t:t + 1],
                                          ALU.subtract, ALU.mult).then_inc(z["xn_ready"], 1)

                    def settle():
                        dve.wait_ge(st.sem, st.level())

                    def select(t):
                        q = t % 2
                        g8 = lambda v: v.rearrange("p g k -> p (g k)")
                        hold(dve, work.free(U_SIM + t), (it + 1) * MOVED, z["dve_held"])
                        for g in range(2 * RH):
                            st.give(dve.max(best[:, q, g, :], sim[:, t, g, :]))
                        hold(dve, st.sem, st.level(), z["dve_held"])
                        for g in range(2 * RH):
                            st.give(dve.max_index(place[:, q, g, :], best[:, q, g, :], sim[:, t, g, :]))
                        b = best[:, q, :, :]
                        top = lambda n: b[:, :, 0:1].broadcast_to([P, 2 * RH, n])
                        dve.tensor_tensor(ex[:, q, :, :], sim[:, t, :, :], top(KEYS), ALU.subtract).then_inc(z["diff_ready"], 1)
                        dve.tensor_tensor(ebest[:, q, :, :], b, top(TOPK), ALU.subtract).then_inc(z["diff_ready"], 1)
                        full = [P, RH, TOPK, TOPK]
                        st.give(dve.tensor_tensor(pair[:, q, :, :, :], b[:, 0:RH, :].unsqueeze(3).broadcast_to(full),
                                                  b[:, RH:, :].unsqueeze(2).broadcast_to(full), ALU.add))
                        hold(dve, st.sem, st.level(), z["dve_held"])
                        for h in range(RH):
                            st.give(dve.max(best2[:, q, h, :], pair[:, q, h, :, :]))
                        st.give(dve.tensor_copy(placef[:, q, :, :], place[:, q, :, :]))
                        st.give(dve.tensor_scalar(beyond[:, q, :, :], place[:, q, 0:RH, :], float(XROWS), None, ALU.is_ge))
                        hold(dve, st.sem, st.level(), z["dve_held"])
                        for h in range(RH):
                            st.give(dve.match_replace(struck[:, q, h, :, :], best2[:, q, h, :], pair[:, q, h, :, :], LOW))
                        px, py = placef[:, q, 0:RH, :], placef[:, q, RH:, :]
                        xs, ys = [P, RH, XROWS, TOPK], [P, RH, KEYS, TOPK]
                        hot_x = hot[:, :, 0:XROWS, :]
                        st.give(dve.tensor_tensor(hot_x, index[:, 0:XROWS, :].unsqueeze(1).broadcast_to(xs),
                                                  px.unsqueeze(2).broadcast_to(xs), ALU.is_equal))
                        settle()
                        st.give(dve.tensor_tensor(picked[:, q], struck[:, q], pair[:, q], ALU.not_equal))
                        settle()
                        with nc.allow_low_precision(reason="counts of at most eight are exact"):
                            st.give(dve.tensor_reduce(count[:, q, :, :], picked[:, q], AX.X, ALU.add))
                        settle()
                        st.give(dve.tensor_tensor(hot_x, hot_x, count[:, q, :, :].unsqueeze(2).broadcast_to(xs), ALU.mult))
                        settle()
                        dve.tensor_reduce(cx[:, q, :, :], hot_x, AX.X, ALU.add).then_inc(z["sel_ready"], 1)
                        dve.wait_ge(z["sel_ready"], (it * TILES + t) * 3 + 1)
                        st.give(dve.tensor_tensor(hot[:, :, :, :], index[:, :, :].unsqueeze(1).broadcast_to(ys),
                                                  py.unsqueeze(2).broadcast_to(ys), ALU.is_equal))
                        settle()
                        fall = falling[:, :].unsqueeze(1).broadcast_to([P, RH * KEYS, TOPK])
                        hy = hot[:, :, :, :].rearrange("p h j b -> p (h j) b")
                        st.give(dve.tensor_tensor(hy, hy, fall, ALU.mult))
                        settle()
                        dve.tensor_reduce(qy[:, q, :, :], hot[:, :, :, :], AX.X, ALU.add).then_inc(z["sel_ready"], 1)
                        dve.wait_ge(z["exp_done"], (it * TILES + t + 1) * 2)
                        e = ebest[:, q, :, :]
                        st.give(dve.tensor_tensor(pair[:, q], e[:, 0:RH, :].unsqueeze(3).broadcast_to(full),
                                                  e[:, RH:, :].unsqueeze(2).broadcast_to(full), ALU.mult))
                        settle()
                        st.give(dve.tensor_tensor(pair[:, q], pair[:, q], picked[:, q], ALU.mult))
                        settle()
                        st.give(dve.tensor_reduce(rows_w[:, q, :, :], pair[:, q], AX.X, ALU.add))
                        settle()
                        st.give(dve.tensor_reduce(norm[:, q, 0, :], rows_w[:, q, :, :], AX.X, ALU.add))
                        settle()
                        st.give(dve.reciprocal(norm[:, q, 1, :], norm[:, q, 0, :]))
                        settle()
                        inv = norm[:, q, 1, :].unsqueeze(2)
                        dve.tensor_tensor(exn[:, q, :, :], ex[:, q, 0:RH, 0:XROWS], inv.broadcast_to([P, RH, XROWS]),
                                          ALU.mult).then_inc(z["sel_ready"], 1)
                        st.give(dve.tensor_tensor(rows_w[:, q, :, :], rows_w[:, q, :, :], inv.broadcast_to([P, RH, TOPK]), ALU.mult))
                        settle()
                        st.give(dve.tensor_tensor(rows_w[:, q, :, :], rows_w[:, q, :, :], beyond[:, q, :, :], ALU.mult))
                        settle()
                        st.give(dve.tensor_reduce(beyond_w[:, q, :], rows_w[:, q, :, :], AX.XY, ALU.add))

                    def spread(t, h):
                        n = t * RH + h
                        g = G[:, t, :].rearrange("p (i j) -> p i j", j=KEYS)
                        dve.wait_ge(reach.full(n), reach.fillings(it, n))
                        dve.wait_ge(outer.full(n), outer.fillings(it, n))
                        r, w = reach.buf(n)[:, :, :], outer.buf(n)[:, :, :]
                        if h == 0:
                            last = dve.scalar_tensor_tensor(out=g, in0=r, scalar=float(TOPK), in1=w, op0=ALU.is_gt, op1=ALU.mult)
                        else:
                            st.give(dve.scalar_tensor_tensor(out=w, in0=r, scalar=float(TOPK), in1=w, op0=ALU.is_gt, op1=ALU.mult))
                            settle()
                            last = dve.tensor_tensor(g, g, w, ALU.add)
                        last.then_inc(z["spread"], 1)
                        if h == RH - 1:
                            dve.wait_ge(z["spread"], it * RH * TILES + n + 1)
                            dve.tensor_tensor(G[:, t, NEXP - 1:], G[:, t, NEXP - 1:], beyond_w[:, t % 2, :],
                                              ALU.add).then_inc(z["G_ready"], 1)

                    def hidden(n, k, bias):
                        dve.wait_ge(work.full(n), work.fillings(it, n))
                        dve.wait_ge(silu.full(k), silu.fillings(it, k))
                        if 2 <= k < FI + 2:
                            dve.wait_ge(wd_w.free(k - 2), wd_w.emptied_by(it, k - 2))
                        elif k >= FI + 2:
                            dve.wait_ge(z["spent"], it * (FI - 2) + k - 2 - FI + 1)
                        if bias is None:
                            dve.tensor_tensor(hid.buf(k)[:, :], work.buf(n)[:, :], silu.buf(k)[:, :], ALU.mult).then_inc(hid.full(k), 1)
                        else:
                            dve.scalar_tensor_tensor(out=hid.buf(k)[:, :], in0=work.buf(n)[:, :], scalar=bias,
                                                     in1=silu.buf(k)[:, :], op0=ALU.add, op1=ALU.mult).then_inc(hid.full(k), 1)

                    for t in range(TILES):
                        select(t)
                        for h in range(RH):
                            spread(t, h)
                            i = t * RH + h
                            hidden(U_GU + 2 * i + 1, i, bu[:, i:i + 1])
                    for i in range(FI):
                        hidden(U_ST + 2 * i + 1, FI + i, None)
                    dve.wait_ge(z["res_loaded"], (it + 1) * 16)
                    for t in range(TILES):
                        st.give(dve.tensor_tensor(xres[:, t, :], xres[:, t, :], bd[:, :], ALU.add))
                    settle()
                    dve.wait_ge(z["summed"], (it + 1) * TILES)
                    for t in range(TILES):
                        dve.tensor_tensor(xres[:, t, :], accs[t][:, :], xres[:, t, :], ALU.add).then_inc(z["out_ready"], 1)
                    st.end()


def ffn1(nc, a, s, x_in, x_out):
    pre = "ff1"
    USES = DC + FI
    with ExitStack() as ctx:
        sem = make_sem(nc, s["sems"], pre)
        sb = lambda name, shape, dt=F32: ctx.enter_context(nc.sbuf_tensor(f"{pre}_{name}", shape, dt))
        ident = sb("ident", [P, P])
        eps = sb("eps", [P, 1])
        wexp = sb("wexp", [P, DC, F])
        wconT = sb("wconT", [P, DC, F])
        wcon = sb("wcon", [P, FI, D])
        bh, bias = sb("bh", [P, FI]), sb("bias", [P, 2, D])
        xin, xres, xn = (sb(n, [P, TILES, D]) for n in ("xin", "xres", "xn"))
        xnT = sb("xnT", [P, DC, BLOCK])
        stats, mv = sb("stats", [P, TILES, 6]), sb("mv", [P, TILES, 2])
        std, rstd = sb("std", [P, TILES]), sb("rstd", [P, TILES])
        ps = lambda name: ctx.enter_context(nc.psum_tensor(f"{pre}_{name}", [P, 512], F32))
        work = Ring(sem, "work", [ps(f"work{i}") for i in range(4)], USES)
        accs = [ps(f"acc{i}") for i in range(TILES)]
        hid = [sb(f"hid{i}", [P, BLOCK]) for i in range(4)]
        z = Named(sem)

        with nc.Block() as block:
            @block.sync
            def _(sp):
                sp.dma_start(wconT[:, :, :], s["wcon"].rearrange("p (c n) -> p c n", c=DC)).then_inc(z["w_loaded"], 16)
                sp.dma_start(xin[:, :, :], x_in[0].rearrange("p t d -> p (t d)")).then_inc(z["x_loaded"], 16)
                sp.dma_start(wexp[:, :, :], s["wexp"].rearrange("p (c n) -> p c n", c=DC)).then_inc(z["w_loaded"], 16)
                sp.dma_start(bh[:, :], s["bexp"].rearrange("a (i p) -> p (a i)", p=P), allow_slow_non_contiguous=True).then_inc(z["w_loaded"], 16)
                for k, name in enumerate(("b_con", "down_bias")):
                    sp.dma_start(bias[:, k, :], a[name].partition_broadcast(P)).then_inc(z["w_loaded"], 16)

                def block_io(it, more):
                    sp.wait_ge(z["xn_ready"], (it + 1) * TILES)
                    if more:
                        sp.dma_start(xin[:, :, :], x_in[bass.ds(it + 1, 1)].rearrange("a p t d -> (a p) (t d)")).then_inc(z["x_loaded"], 16)
                    if not isinstance(it, int) or it:
                        sp.wait_ge(z["stored"], it * 16)
                    sp.dma_start(xres[:, :, :], x_in[bass.ds(it, 1)].rearrange("a p t d -> (a p) (t d)")).then_inc(z["res_loaded"], 16)
                    sp.wait_ge(z["out_ready"], (it + 1) * TILES)
                    sp.dma_start(x_out[bass.ds(it, 1)].rearrange("a p t d -> (a p) (t d)"), xres[:, :, :]).then_inc(z["stored"], 16)

                block_io(0, True)
                with sp.Fori(1, BLOCKS - 1) as it:
                    block_io(it, True)
                block_io(BLOCKS - 1, False)
                sp.wait_ge(z["stored"], BLOCKS * 16)

            @block.tensor
            def _(pe):
                pe.wait_ge(z["w_loaded"], 5 * 16)
                pe.wait_ge(z["id_done"], 1)
                for i in range(FI):
                    if i >= TILES:
                        pe.wait_ge(z["wcon_ready"], i - TILES + 1)
                    for c in range(DC):
                        last = pe.transpose(accs[i % TILES][:, c * P:(c + 1) * P], wconT[:, c, i * P:(i + 1) * P], ident[:, :])
                    last.then_inc(z["turned"], 1)
                pe.wait_ge(z["wcon_ready"], FI)
                with pe.Fori(0, BLOCKS) as it:
                    def take(n):
                        if n >= 4:
                            pe.wait_ge(work.free(n), work.emptyings(it, n))
                        return work.buf(n)

                    pe.wait_ge(z["xn_ready"], (it + 1) * TILES)
                    for c in range(DC):
                        bank = take(c)
                        for t in range(TILES):
                            last = pe.transpose(bank[:, t * P:(t + 1) * P], xn[:, t, c * P:(c + 1) * P], ident[:, :])
                        last.then_inc(work.full(c), 1)
                    for c in range(DC):
                        pe.wait_ge(work.free(c), work.emptied_by(it, c))
                    for i in range(FI + 2):
                        if i < FI:
                            n = DC + i
                            bank = take(n)
                            for c in range(DC):
                                last = pe.matmul(bank[:, :], wexp[:, c, i * P:(i + 1) * P], xnT[:, c, :],
                                                 start=c == 0, stop=c == DC - 1)
                            last.then_inc(work.full(n), 1)
                        if i >= 2:
                            k = i - 2
                            pe.wait_ge(work.free(DC + k), work.emptied_by(it, DC + k))
                            for t in range(TILES):
                                last = pe.matmul(accs[t][:, :], hid[k % 4][:, t * P:(t + 1) * P], wcon[:, k, :],
                                                 start=k == 0, stop=k == FI - 1)
                                if k == FI - 1:
                                    last.then_inc(z["summed"], 1)
                            if k < FI - 1:
                                last.then_inc(z["spent"], 1)

            @block.scalar
            def _(act):
                act.wait_ge(z["eps_done"], 1)
                act.wait_ge(z["w_loaded"], 5 * 16)
                with act.Fori(0, BLOCKS) as it:
                    act.wait_ge(z["var_ready"], (it + 1) * TILES)
                    act.activation(std[:, :], mv[:, :, 1], ACT.Sqrt, bias=eps[:, :]).then_inc(z["std_ready"], 1)
                    for c in range(DC):
                        act.wait_ge(work.full(c), work.fillings(it, c))
                        act.copy(xnT[:, c, :], work.buf(c)[:, :]).then_inc(work.free(c), 1)
                    for i in range(FI):
                        n = DC + i
                        act.wait_ge(work.full(n), work.fillings(it, n))
                        if i >= 4:
                            act.wait_ge(z["spent"], it * (FI - 1) + i - 3)
                        act.activation(hid[i % 4][:, :], work.buf(n)[:, :], ACT.Gelu, bias=bh[:, i:i + 1]).then_inc(work.free(n), 1)

            @block.gpsimd
            def _(pool):
                make_identity(pool, ident, z["id_zeroed"], z["id_done"])

            @block.vector
            def _(dve):
                dve.memset(eps[:, :], EPS).then_inc(z["eps_done"], 1)
                dve.wait_ge(z["w_loaded"], 5 * 16)
                dve.tensor_tensor(bias[:, 0, :], bias[:, 0, :], bias[:, 1, :], ALU.add).then_inc(z["bias_done"], 1)
                for i in range(FI):
                    dve.wait_ge(z["turned"], i + 1)
                    dve.tensor_copy(wcon[:, i, :], accs[i % TILES][:, :]).then_inc(z["wcon_ready"], 1)
                dve.wait_ge(z["bias_done"], 1)
                with dve.Fori(0, BLOCKS) as it:
                    st = Steps(z["dve_step"], it, TILES + 1 + TILES)
                    dve.wait_ge(z["x_loaded"], (it + 1) * 16)
                    layernorm_stats(dve, st, [xin[:, t, :] for t in range(TILES)], stats, mv, z["var_ready"], z["dve_held"])
                    dve.wait_ge(z["std_ready"], it + 1)
                    st.give(dve.reciprocal(rstd[:, :], std[:, :]))
                    dve.wait_ge(st.sem, st.level())
                    for t in range(TILES):
                        dve.tensor_scalar(xn[:, t, :], xin[:, t, :], mv[:, t, 0:1], rstd[:, t:t + 1],
                                          ALU.subtract, ALU.mult).then_inc(z["xn_ready"], 1)
                    dve.wait_ge(z["res_loaded"], (it + 1) * 16)
                    for t in range(TILES):
                        st.give(dve.tensor_tensor(xres[:, t, :], xres[:, t, :], bias[:, 0, :], ALU.add))
                    dve.wait_ge(st.sem, st.level())
                    dve.wait_ge(z["summed"], (it + 1) * TILES)
                    for t in range(TILES):
                        dve.tensor_tensor(xres[:, t, :], accs[t][:, :], xres[:, t, :], ALU.add).then_inc(z["out_ready"], 1)
                    st.end()


FF0_STEPS = 185


PHASES = 5


def build(nc, a, out, sems):
    scratch = lambda name, shape: nc.dram_tensor("scratch_" + name, shape, F32).ap()
    s = {"kz": [scratch(f"kz{i}", (BATCH, P, HEADS * CTX)) for i in range(2)],
         "vm": [scratch(f"vm{i}", (BATCH, P, HEADS * (dk + 1))) for i, dk in enumerate((32, 64))],
         "vr": [scratch(f"vr{i}", (BATCH, REM, HEADS * (dk + 1))) for i, dk in enumerate((32, 64))],
         "fold": scratch("fold", (P, DC * D)), "wexp": scratch("wexp", (P, DC * F)),
         "wcon": scratch("wcon", (P, DC * F)), "bexp": scratch("bexp", (1, F))}
    s["sems"] = sems
    blocks = lambda ap: ap.rearrange("(a p t) d -> a p t d", p=P, t=TILES)
    x = [blocks(a["x"])] + [blocks(scratch(f"x{i}", (TOKENS, D))) for i in (1, 2, 3)] + [blocks(out)]
    prepare(nc, a, s)
    attention(nc, a, s, 0, x[0], x[1])
    if PHASES > 2:
        ffn0(nc, a, s, x[1], x[2])
    if PHASES > 3:
        attention(nc, a, s, 1, x[2], x[3])
    if PHASES > 4:
        ffn1(nc, a, s, x[3], x[4])


def kernel(**inputs):
    import numpy as np
    import concourse.bacc as bacc
    from concourse.bass_utils import run_bass_kernel_spmd

    v = {k: np.asarray(w) for k, w in inputs.items()}
    cols = lambda b: b.reshape(-1, P).T
    tiles = lambda w: w.reshape(DC, P, FI, P).transpose(2, 1, 0, 3)
    laid = {
        "x": v["x"].reshape(TOKENS, D), "ctxT": v["ctx_1024"].transpose(0, 2, 1),
        "wq0": v["L0_xattn_w_q"].T, "wkT0": v["L0_xattn_w_k"].T, "wvT0": v["L0_xattn_w_v"].T, "wo0": v["L0_xattn_w_o"].T,
        "bq0": cols(v["L0_xattn_b_q"]), "bk0": cols(v["L0_xattn_b_k"]), "bv0": v["L0_xattn_b_v"], "bo0": v["L0_xattn_b_o"],
        "Wg": tiles(v["L0_ffn_Wg"]), "Wu": tiles(v["L0_ffn_Wu"]), "Wd": v["L0_ffn_Wd"].reshape(FI, P, D),
        "bg": cols(v["L0_ffn_bg"]), "bu": cols(v["L0_ffn_bu"]), "bd": v["L0_ffn_bd"],
        "WqT": v["L0_ffn_Wq"].T, "keysT": v["L0_ffn_keys"].transpose(2, 0, 3, 1).reshape(2 * RH * KEYS, KEYS),
        "downT": v["L0_ffn_down_embed"].T, "up": v["L0_ffn_up_embed"],
        "wkv1": v["L1_xattn_w_kv"], "wq1": v["L1_xattn_w_q"], "wo1": v["L1_xattn_w_out1"], "w2": v["L1_xattn_w_out2"],
        "gamma": v["L1_xattn_gamma"],
        "W_exp": v["L1_ffn_W_exp"], "b_exp": v["L1_ffn_b_exp"].reshape(1, F), "up_bias": v["L1_ffn_up_bias"].reshape(1, F),
        "up_w": v["L1_ffn_up_weights"].transpose(0, 2, 3, 1).reshape(STAGES, 4, F // 2),
        "down_w": v["L1_ffn_down_weights"].transpose(0, 2, 3, 1).reshape(STAGES, 4, F // 2),
        "W_conT": v["L1_ffn_W_con"].T, "b_con": v["L1_ffn_b_con"], "down_bias": v["L1_ffn_down_bias"],
    }
    nc = bacc.Bacc("TRN2", target_bir_lowering=False, num_devices=1)
    arrays, a = {}, {}
    for name, w in laid.items():
        arrays["in_" + name] = np.ascontiguousarray(w)
        a[name] = nc.dram_tensor("in_" + name, w.shape, mybir.dt.from_np(w.dtype), kind="ExternalInput").ap()
    out = nc.dram_tensor("out_0", (TOKENS, D), F32, kind="ExternalOutput").ap()
    with ExitStack() as sems:
        build(nc, a, out, sems)
    r = run_bass_kernel_spmd(nc, [arrays], core_ids=[0])
    return r.results[0]["out_0"].reshape(BATCH, TOKENS // BATCH, D)
```

```python
import concourse.bass as bass
from concourse import mybir
from contextlib import ExitStack

F32 = mybir.dt.float32
F32R = mybir.dt.float32r
BF16 = mybir.dt.bfloat16
U32 = mybir.dt.uint32
ALU = mybir.AluOpType
ACT = mybir.ActivationFunctionType
AX = mybir.AxisListType

P = 128
D = 512
DC = D // P
TILES = 4
BLOCK = TILES * P
TOKENS = 4096
BLOCKS = TOKENS // BLOCK
BATCH = 2
CTX = 154
REM = CTX - P
HEADS = 16
GH = 4
GROUPS = HEADS // GH
UNITS = TILES * GROUPS
F = 2048
FI = F // P
EPS = 1e-5
KEYS = 64
RH = 4
TOPK = 8
NEXP = 2048
XROWS = NEXP // KEYS
STAGES = 11
LOW = -3.0e38


class Named(dict):

    def __init__(self, make):
        super().__init__()
        self.make = make

    def __missing__(self, name):
        self[name] = self.make(name)
        return self[name]


class Ring:

    def __init__(self, sem, name, buffers, uses, parts=1, drains=1, start=0):
        assert uses % len(buffers) == 0
        self.buffers, self.parts, self.drains, self.each = buffers, parts, drains, uses // len(buffers)
        self.start = start
        self.filled = Named(lambda i: sem(f"{name}_filled{i}"))
        self.emptied = Named(lambda i: sem(f"{name}_emptied{i}"))

    def buf(self, n):
        return self.buffers[n % len(self.buffers)]

    def full(self, n):
        return self.filled[n % len(self.buffers)]

    def free(self, n):
        return self.emptied[n % len(self.buffers)]

    def fillings(self, it, n):
        return it * (self.each * self.parts) + (n // len(self.buffers) + 1) * self.parts

    def emptyings(self, it, n):
        return (it * self.each + n // len(self.buffers)) * self.drains + self.start

    def emptied_by(self, it, n):
        return it * (self.each * self.drains) + (n // len(self.buffers) + 1) * self.drains + self.start


class Steps:

    def __init__(self, sem, it, each):
        self.sem, self.it, self.each, self.n = sem, it, each, 0

    def give(self, ins):
        ins.then_inc(self.sem, 1)
        self.n += 1

    def level(self):
        return self.it * self.each + self.n

    def end(self):
        assert self.n == self.each, f"a pass gives {self.n} steps"


def make_sem(nc, ctx, prefix):
    return lambda name: ctx.enter_context(nc.semaphore(f"{prefix}_{name}"))


def hold(engine, sem, value, held):
    engine.wait_ge(sem, value)
    engine.sem_inc(held, 1)


def make_identity(pool, ident, step):
    pool.memset(ident[:, :], 0.0).then_inc(step, 1)
    pool.wait_ge(step, 1)
    pool.affine_select(out=ident[:, :], in_=ident[:, :], compare_op=ALU.not_equal, fill=1.0, base=0,
                       pattern=[[-1, P]], channel_multiplier=1).then_inc(step, 1)


def prepare(nc, a, s):
    with ExitStack() as ctx:
        sem = make_sem(nc, s["sems"], "prep")
        sb = lambda name, shape, dt=F32: ctx.enter_context(nc.sbuf_tensor("prep_" + name, shape, dt))
        ctxT = sb("ctxT", [P, BATCH, DC, CTX])
        wk0 = sb("wk0", [P, DC, D])
        wv0 = sb("wv0", [P, DC, D])
        wkv1 = sb("wkv1", [P, DC, 2048])
        wqT = sb("wqT", [P, DC, D])
        keyz = sb("keyz", [P, RH, P])
        bk0 = sb("bk0", [P, DC])
        bv0 = sb("bv0", [P, D])
        kz = [sb(f"kz{i}", [P, BATCH, HEADS, CTX]) for i in range(2)]
        dks = (32, 64)
        vm = [sb(f"vm{i}", [P, BATCH, HEADS, dks[i] + 1]) for i in range(2)]
        vr = [sb(f"vr{i}", [REM, BATCH, HEADS, dks[i] + 1]) for i in range(2)]
        fold = sb("fold", [P, DC, D])
        banks = [ctx.enter_context(nc.psum_tensor(f"prep_ps{i}", [P, 512], F32)) for i in range(8)]
        loaded = sem("loaded")
        keys_loaded = sem("keys_loaded")
        zeroed = sem("zeroed")
        stored = sem("stored")

        jobs = [("fold", 0, 0, c) for c in range(DC)]
        for layer in range(2):
            for b in range(BATCH):
                jobs += [("k", layer, b, f) for f in range(HEADS * dks[layer] // P)]
                jobs += [("v", layer, b, (part, n)) for part in range(2) for n in range(HEADS * dks[layer] // 512)]
        made = sem("made")
        k_done, v_done = sem("k_done"), sem("v_done")
        n_k = sum(P // dks[j[1]] for j in jobs if j[0] == "k")
        n_v = sum(j[0] in ("v", "fold") for j in jobs)

        with nc.Block() as block:
            @block.sync
            def _(sp):
                sp.dma_start(ctxT[:, :, :, :], a["ctxT"].rearrange("b (c p) s -> p b c s", p=P)).then_inc(loaded, 16)
                for w, src in ((wk0, a["wkT0"]), (wv0, a["wvT0"]), (wkv1, a["wkv1"]), (wqT, a["WqT"])):
                    sp.dma_start(w[:, :, :], src.rearrange("(c p) n -> p c n", p=P)).then_inc(loaded, 16)
                sp.dma_start(bk0[:, :], a["bk0"]).then_inc(loaded, 16)
                sp.dma_start(bv0[:, :], a["bv0"].partition_broadcast(P)).then_inc(loaded, 16)
                sp.wait_ge(zeroed, 1)
                src = a["keysT"].rearrange("(g q n) k -> q n g k", q=2, n=KEYS)
                for q in range(2):
                    rows = slice(q * KEYS, (q + 1) * KEYS)
                    sp.dma_start(keyz[rows, :, rows], src[q]).then_inc(keys_loaded, 16)
                sp.wait_ge(k_done, n_k)
                sp.wait_ge(v_done, n_v)
                for layer in range(2):
                    sp.dma_start(s["kz"][layer].rearrange("b p n -> p b n"),
                                 kz[layer][:, :, :, :].rearrange("p b h k -> p b (h k)")).then_inc(stored, 16)
                    sp.dma_start(s["vm"][layer].rearrange("b p n -> p b n"),
                                 vm[layer][:, :, :, :].rearrange("p b h k -> p b (h k)")).then_inc(stored, 16)
                    sp.dma_start(s["vr"][layer].rearrange("b p n -> p b n"),
                                 vr[layer][:, :, :, :].rearrange("p b h k -> p b (h k)")).then_inc(stored, 16)
                sp.dma_start(s["fold"], fold[:, :, :].rearrange("p c n -> p (c n)")).then_inc(stored, 16)
                sp.wait_ge(stored, 7 * 16)

            @block.gpsimd
            def _(pool):
                pool.memset(keyz[:, :, :], 0.0).then_inc(zeroed, 1)
                for layer in range(2):
                    pool.memset(kz[layer][:, :, :, :], 0.0).then_inc(zeroed, 1)
                    pool.memset(vm[layer][:, :, :, dks[layer]:], 1.0).then_inc(zeroed, 1)
                    pool.memset(vr[layer][:, :, :, dks[layer]:], 1.0).then_inc(zeroed, 1)

            @block.tensor
            def _(pe):
                pe.wait_ge(loaded, 7 * 16)
                pe.wait_ge(keys_loaded, 32)
                for n, (kind, layer, b, i) in enumerate(jobs):
                    bank = banks[n % 8]
                    if n >= 8:
                        before = jobs[n - 8][0]
                        if before == "k":
                            pe.wait_ge(k_done, sum(P // dks[q[1]] for q in jobs[:n - 7] if q[0] == "k"))
                        else:
                            pe.wait_ge(v_done, sum(q[0] != "k" for q in jobs[:n - 7]))
                    if kind == "fold":
                        for g in range(RH):
                            last = pe.matmul(bank[:, g * P:(g + 1) * P], wqT[:, g, i * P:(i + 1) * P],
                                             keyz[:, g, :], start=True, stop=True)
                    elif kind == "k":
                        w = wkv1 if layer else wk0
                        for c in range(DC):
                            last = pe.matmul(bank[:, 0:CTX], w[:, c, i * P:(i + 1) * P], ctxT[:, b, c, :],
                                             start=c == 0, stop=c == DC - 1)
                    elif kind == "v":
                        part, m = i
                        rows = slice(0, P) if part == 0 else slice(P, CTX)
                        for c in range(DC):
                            w = wkv1[:, c, 1024 + m * 512:1024 + m * 512 + 512] if layer else wv0[:, c, :]
                            last = pe.matmul(bank[0:rows.stop - rows.start, :], ctxT[:, b, c, rows], w,
                                             start=c == 0, stop=c == DC - 1)
                    last.then_inc(made, 1)

            @block.scalar
            def _(act):
                act.wait_ge(loaded, 7 * 16)
                act.wait_ge(zeroed, 7)
                for n, (kind, layer, b, i) in enumerate(jobs):
                    if kind != "k":
                        continue
                    dk = dks[layer]
                    per = P // dk
                    act.wait_ge(made, n + 1)
                    for j in range(per):
                        rows = slice(j * dk, (j + 1) * dk)
                        bias = bk0[rows, i:i + 1] if layer == 0 else 0.0
                        last = act.activation(kz[layer][rows, b, i * per + j, :], banks[n % 8][rows, 0:CTX],
                                              ACT.Identity, bias=bias)
                        last.then_inc(k_done, 1)

            @block.vector
            def _(dve):
                dve.wait_ge(loaded, 7 * 16)
                for n, (kind, layer, b, i) in enumerate(jobs):
                    if kind == "fold":
                        dve.wait_ge(made, n + 1)
                        last = dve.tensor_copy(fold[:, i, :], banks[n % 8][:, :])
                    elif kind == "v":
                        part, m = i
                        dk = dks[layer]
                        heads = slice(m * (512 // dk), (m + 1) * (512 // dk))
                        rows = P if part == 0 else REM
                        dve.wait_ge(made, n + 1)
                        out = (vr if part else vm)[layer][0:rows, b, heads, 0:dk]
                        src = banks[n % 8][0:rows, :].rearrange("p (h d) -> p h d", d=dk)
                        if layer == 0:
                            last = dve.tensor_tensor(out, src, bv0[0:rows, :].rearrange("p (h d) -> p h d", d=dk), ALU.add)
                        else:
                            last = dve.tensor_copy(out, src)
                    else:
                        continue
                    last.then_inc(v_done, 1)


def layernorm(dve, z, nth, xin, stats, mv, std, rstd, xn):
    st = Steps(z["ln_step"], nth, TILES + 1)
    dve.wait_ge(z["x_loaded"], (nth + 1) * 16)
    for t in range(TILES):
        st.give(dve.bn_stats(stats[:, t, :], xin[:, t, :]))
    hold(dve, st.sem, st.level(), z["held"])
    for t in range(TILES):
        dve.bn_aggr(mv[:, t, :], stats[:, t, :]).then_inc(z["var_ready"], 1)
    dve.wait_ge(z["std_ready"], nth + 1)
    st.give(dve.reciprocal(rstd[:, :], std[:, :]))
    dve.wait_ge(st.sem, st.level())
    for t in range(TILES):
        dve.tensor_scalar(xn[:, t, :], xin[:, t, :], mv[:, t, 0:1], rstd[:, t:t + 1],
                          ALU.subtract, ALU.mult).then_inc(z["xn_ready"], 1)
    st.end()


def deviations(act, z, nth, std, mv, eps):
    act.wait_ge(z["var_ready"], (nth + 1) * TILES)
    act.activation(std[:, :], mv[:, :, 1], ACT.Sqrt, bias=eps[:, :]).then_inc(z["std_ready"], 1)


def butterfly_stage(pool, y, w, s, transposed, t, done, base, held):
    st = 2 ** s
    v = y.rearrange("p (n two s) -> p n two s", two=2, s=st)
    lo, hi = v[:, :, 0, :], v[:, :, 1, :]
    rows = y.shape[0]
    wv = lambda i, j: w[0:rows, 2 * i + j, :].rearrange("p (n s) -> p n s", s=st)
    tv = lambda k: t[0:rows, k, :].rearrange("p (n s) -> p n s", s=st)
    w01, w10 = (wv(1, 0), wv(0, 1)) if transposed else (wv(0, 1), wv(1, 0))
    pool.tensor_tensor(tv(0), lo, wv(0, 0), ALU.mult).then_inc(done, 1)
    pool.tensor_tensor(tv(1), hi, w01, ALU.mult).then_inc(done, 1)
    pool.tensor_tensor(tv(2), lo, w10, ALU.mult).then_inc(done, 1)
    pool.tensor_tensor(tv(3), hi, wv(1, 1), ALU.mult).then_inc(done, 1)
    hold(pool, done, base + 4, held)
    pool.tensor_tensor(lo, tv(0), tv(1), ALU.add).then_inc(done, 1)
    pool.tensor_tensor(hi, tv(2), tv(3), ALU.add).then_inc(done, 1)
    hold(pool, done, base + 6, held)


def attention(nc, a, s, layer, x_in, x_out):
    dk = (32, 64)[layer]
    FT = HEADS * dk // P
    CG = FT // GROUPS
    VW = dk + 1
    pre = f"at{layer}"
    U_XT, U_Q = 0, DC
    U_PV = U_Q + FT
    U_OT = U_PV + UNITS
    U_R = U_OT + FT
    U_OUT = U_R + (DC if layer else 0)
    USES = U_OUT + TILES
    with ExitStack() as ctx:
        sem = make_sem(nc, s["sems"], pre)
        sb = lambda name, shape, dt=F32: ctx.enter_context(nc.sbuf_tensor(f"{pre}_{name}", shape, dt))
        ident = sb("ident", [P, P])
        eps = sb("eps", [P, 1])
        wq = sb("wq", [P, DC, HEADS * dk])
        wo = sb("wo", [P, FT, D])
        xin = sb("xin", [P, TILES, D])
        xres = sb("xres", [P, TILES, D])
        xn = sb("xn", [P, TILES, D])
        xnT = sb("xnT", [P, DC, BLOCK])
        qT = sb("qT", [P, FT, BLOCK])
        kz = sb("kz", [P, HEADS, CTX])
        vm = sb("vm", [P, HEADS, VW])
        vr = sb("vr", [GH * REM, GROUPS, GH, VW])
        probs = [sb(f"probs{i}", [P, GH, CTX]) for i in range(4)]
        tails = [sb(f"tails{i}", [P, GH * REM]) for i in range(4)]
        ptS = [sb(f"ptS{i}", [P, GH + 1, P]) for i in range(2)]
        o = sb("o", [P, TILES, HEADS, dk])
        oT = qT
        stats, mv = sb("stats", [P, TILES, 6]), sb("mv", [P, TILES, 2])
        std, rstd = sb("std", [P, TILES]), sb("rstd", [P, TILES])
        mx, rz = sb("mx", [P, 2, GH]), sb("rz", [P, 2, GH])
        if layer:
            w2 = sb("w2", [P, DC, D])
            rT = xnT
            row = sb("gamma", [P, D])
            y = sb("y", [P, D])
            bst, bmv = sb("bst", [P, TILES, 6]), sb("bmv", [P, TILES, 2])
            bstd, brstd = sb("bstd", [P, TILES]), sb("brstd", [P, TILES])
        else:
            bq = sb("bq", [P, FT])
            bqs = sb("bqs", [P, FT])
            row = sb("bo", [P, D])
        bw = sb("bw", [P, 4, 1024])
        bt = sb("bt", [P, 4, 1024])
        by = sb("by", [P, DC, F])
        bias_row, up_row = by[0:1, 0, :], by[0:1, 1, :]

        ps = lambda name, shape: ctx.enter_context(nc.psum_tensor(f"{pre}_{name}", shape, F32))
        score = Ring(sem, "score", [ps(f"score{i}", [P, 2, 512]) for i in range(2)], UNITS)
        pt = Ring(sem, "pt", [ps("pt", [P, 2, 512])], UNITS, drains=2)
        acc = Ring(sem, "acc", [ps(f"acc{i}", [P, 512]) for i in range(2)], USES, start=1)

        z = Named(sem)
        z["held"] = s["held"]

        with nc.Block() as block:
            @block.sync
            def _(sp):
                sp.dma_start(xin[:, :, :], x_in[0].rearrange("p t d -> p (t d)")).then_inc(z["x_loaded"], 16)
                sp.dma_start(wq[:, :, :], a[f"wq{layer}"].rearrange("(c p) n -> p c n", p=P)).then_inc(z["w_loaded"], 16)
                sp.dma_start(row[:, :], a["gamma" if layer else "bo0"].partition_broadcast(P)).then_inc(z["w_loaded"], 16)
                if not layer:
                    sp.dma_start(bq[:, :], a["bq0"]).then_inc(z["w_loaded"], 16)
                sp.wait_ge(z["vr_zeroed"], 1)

                def load_kv(b):
                    sp.dma_start(kz[:, :, :], s["kz"][layer][b].rearrange("a p n -> (a p) n")).then_inc(z["kv_loaded"], 16)
                    sp.dma_start(vm[:, :, :], s["vm"][layer][b].rearrange("a p n -> (a p) n")).then_inc(z["kv_loaded"], 16)
                    src = s["vr"][layer][b].rearrange("a p (g j v) -> (a p) g j v", g=GROUPS, j=GH)
                    for j in range(GH):
                        sp.dma_start(vr[REM * j:REM * (j + 1), :, j, :], src[:, :, j, :]).then_inc(z["kv_loaded"], 16)

                load_kv(slice(0, 1))
                sp.dma_start(wo[:, :, :], a[f"wo{layer}"].rearrange("(c p) n -> p c n", p=P)).then_inc(z["wo_loaded"], 16)
                if layer:
                    sp.dma_start(w2[:, :, :], a["w2"].rearrange("(c p) n -> p c n", p=P)).then_inc(z["wo_loaded"], 16)

                def block_io(it, more):
                    sp.wait_ge(z["xn_ready"], (it + 1) * TILES)
                    nxt = bass.ds(it + 1, 1) if more else slice(it, it + 1)
                    sp.dma_start(xin[:, :, :], x_in[nxt].rearrange("a p t d -> (a p) (t d)")).then_inc(z["x_loaded"], 16)
                    if not isinstance(it, int) or it:
                        sp.wait_ge(z["stored"], it * 16)
                    sp.dma_start(xres[:, :, :], x_in[bass.ds(it, 1)].rearrange("a p t d -> (a p) (t d)")).then_inc(z["res_loaded"], 16)
                    if more:
                        sp.wait_ge(acc.free(U_OT - 1), acc.emptied_by(it, U_OT - 1))
                        load_kv(bass.ds((it + 1) // (BLOCKS // BATCH), 1))
                    if layer:
                        sp.wait_ge(z["out_ready"], (it + 1) * TILES)
                    else:
                        for n in (USES - 2, USES - 1):
                            sp.wait_ge(acc.free(n), acc.emptied_by(it, n))
                    sp.dma_start(x_out[bass.ds(it, 1)].rearrange("a p t d -> (a p) (t d)"), xres[:, :, :]).then_inc(z["stored"], 16)

                block_io(0, True)
                with sp.Fori(1, BLOCKS - 1) as it:
                    block_io(it, True)
                block_io(BLOCKS - 1, False)
                sp.wait_ge(z["stored"], BLOCKS * 16)
                sp.wait_ge(z["x_loaded"], (BLOCKS + 1) * 16)

            @block.tensor
            def _(pe):
                pe.wait_ge(z["w_loaded"], 48 - 16 * layer)
                pe.wait_ge(z["id_step"], 2)
                with pe.Fori(0, BLOCKS) as it:
                    def take(n):
                        pe.wait_ge(acc.free(n), acc.emptyings(it, n))
                        return acc.buf(n)

                    def made(n):
                        for m in (n - 1, n):
                            pe.wait_ge(acc.free(m), acc.emptied_by(it, m))

                    pe.wait_ge(z["xn_ready"], (it + 1) * TILES)
                    for c in range(DC):
                        bank = take(U_XT + c)
                        for t in range(TILES):
                            last = pe.transpose(bank[:, t * P:(t + 1) * P], xn[:, t, c * P:(c + 1) * P], ident[:, :])
                        last.then_inc(acc.full(U_XT + c), 1)
                    made(U_Q - 1)
                    for f in range(FT):
                        bank = take(U_Q + f)
                        for c in range(DC):
                            last = pe.matmul(bank[:, :], wq[:, c, f * P:(f + 1) * P], xnT[:, c, :],
                                             start=c == 0, stop=c == DC - 1)
                        last.then_inc(acc.full(U_Q + f), 1)
                    made(U_PV - 1)
                    pe.wait_ge(z["kv_loaded"], (it + 1) * 16 * (2 + GH))

                    def scores(u):
                        t, g = divmod(u, GROUPS)
                        if u >= 2:
                            pe.wait_ge(score.free(u), score.emptyings(it, u))
                        for half in range(2):
                            f = g * CG + half * (CG - 1)
                            h = g * GH + 2 * half
                            last = pe.matmul(score.buf(u)[:, half, 0:2 * CTX], qT[:, f, t * P:(t + 1) * P],
                                             kz[:, h:h + 2, :], start=True, stop=True)
                        last.then_inc(score.full(u), 1)

                    def turn(u):
                        pe.wait_ge(z["exp_done"], (it * UNITS + u + 1) * 2)
                        if u >= 1:
                            pe.wait_ge(pt.free(u), pt.emptyings(it, u))
                        p = probs[u % 4]
                        for j in range(GH):
                            pe.transpose(pt.buf(u)[:, 0, j * P:(j + 1) * P], p[:, j, 0:P], ident[:, :])
                        pe.transpose(pt.buf(u)[0:GH * REM, 1, 0:P], tails[u % 4][:, :], ident[:, :]).then_inc(pt.full(u), 1)

                    def weigh(u):
                        g = u % GROUPS
                        pe.wait_ge(pt.free(u), pt.emptied_by(it, u))
                        bank = take(U_PV + u)
                        pT = ptS[u % 2]
                        pe.matmul(bank[:, 0:GH * VW], pT[0:GH * REM, GH, :], vr[:, g, :, :], start=True, stop=False)
                        for j in range(GH):
                            last = pe.matmul(bank[:, j * VW:(j + 1) * VW], pT[:, j, :], vm[:, g * GH + j, :],
                                             start=False, stop=j == GH - 1)
                        last.then_inc(acc.full(U_PV + u), 1)

                    for u in range(UNITS + 3):
                        if u < UNITS:
                            scores(u)
                        if 2 <= u < UNITS + 2:
                            turn(u - 2)
                        if u >= 3:
                            weigh(u - 3)
                    made(U_OT - 1)
                    hc = P // dk
                    for c in range(FT):
                        bank = take(U_OT + c)
                        for t in range(TILES):
                            last = pe.transpose(bank[:, t * P:(t + 1) * P], o[:, t, c * hc:(c + 1) * hc, :], ident[:, :])
                        last.then_inc(acc.full(U_OT + c), 1)
                    made(U_R - 1)
                    pe.wait_ge(z["wo_loaded"], 16 + 16 * layer)
                    if layer:
                        for f in range(DC):
                            bank = take(U_R + f)
                            for c in range(FT):
                                last = pe.matmul(bank[:, :], wo[:, c, f * P:(f + 1) * P], oT[:, c, :],
                                                 start=c == 0, stop=c == FT - 1)
                            last.then_inc(acc.full(U_R + f), 1)
                        made(U_OUT - 1)
                    src, w, n = (rT, w2, DC) if layer else (oT, wo, FT)
                    for t in range(TILES):
                        bank = take(U_OUT + t)
                        for c in range(n):
                            last = pe.matmul(bank[:, :], src[:, c, t * P:(t + 1) * P], w[:, c, :],
                                             start=c == 0, stop=c == n - 1)
                        last.then_inc(acc.full(U_OUT + t), 1)

            @block.scalar
            def _(act):
                act.wait_ge(z["eps_done"], 1)
                act.wait_ge(z["w_loaded"], 48 - 16 * layer)
                scale = float(dk) ** -0.5
                if not layer:
                    act.mul(bqs[:, :], bq[:, :], scale).then_inc(z["bqs_done"], 1)
                    act.wait_ge(z["bqs_done"], 1)
                deviations(act, z, 0, std, mv, eps)
                with act.Fori(0, BLOCKS) as it:

                    def drain(n, out, func=ACT.Copy, **kw):
                        act.wait_ge(acc.full(n), acc.fillings(it, n))
                        act.activation(out, acc.buf(n)[:, :], func, **kw).then_inc(acc.free(n), 1)

                    for c in range(DC):
                        drain(U_XT + c, xnT[:, c, :])
                    for f in range(FT):
                        kw = {"bias": bqs[:, f:f + 1]} if not layer else {}
                        drain(U_Q + f, qT[:, f, :], ACT.Identity, scale=scale, **kw)
                    for u in range(UNITS + 2):
                        if u >= 2:
                            n = u - 2
                            act.wait_ge(pt.full(n), pt.fillings(it, n))
                            act.copy(ptS[n % 2][:, 0:GH, :], pt.buf(n)[:, 0, :].rearrange("p (j k) -> p j k", j=GH)).then_inc(pt.free(n), 1)
                            act.copy(ptS[n % 2][0:GH * REM, GH, :], pt.buf(n)[0:GH * REM, 1, 0:P]).then_inc(pt.free(n), 1)
                        if u < UNITS:
                            act.wait_ge(score.free(u), score.emptied_by(it, u))
                            p = probs[u % 4]
                            act.activation(p[:, :, 0:P], p[:, :, 0:P], ACT.Exp).then_inc(z["exp_done"], 1)
                            act.activation(tails[u % 4][:, :].rearrange("p (j k) -> p j k", j=GH), p[:, :, P:CTX],
                                           ACT.Exp).then_inc(z["exp_done"], 1)
                    for c in range(FT):
                        drain(U_OT + c, oT[:, c, :])
                    deviations(act, z, it + 1, std, mv, eps)
                    if layer:
                        for f in range(DC):
                            drain(U_R + f, rT[:, f, :], ACT.Relu)
                        for t in range(TILES):
                            act.wait_ge(z["y_var"], it * TILES + t + 1)
                            act.activation(bstd[:, t:t + 1], bmv[:, t, 1:2], ACT.Sqrt, bias=eps[:, :]).then_inc(z["y_std"], 1)

            @block.vector
            def _(dve):
                dve.memset(eps[:, :], EPS).then_inc(z["eps_done"], 1)
                dve.memset(vr[:, :, :, :], 0.0).then_inc(z["vr_zeroed"], 1)
                for n in range(2):
                    dve.sem_inc(acc.free(n), 1)
                dve.wait_ge(z["w_loaded"], 48 - 16 * layer)
                layernorm(dve, z, 0, xin, stats, mv, std, rstd, xn)
                with dve.Fori(0, BLOCKS) as it:
                    st = Steps(z["dve_step"], it, DVE_STEPS[layer])
                    dve.wait_ge(z["res_loaded"], (it + 1) * 16)

                    def shift(u):
                        m = mx[:, u % 2, :]
                        sc = score.buf(u)[:, :, 0:2 * CTX]
                        dve.wait_ge(score.full(u), score.fillings(it, u))
                        st.give(dve.tensor_reduce(m.rearrange("p (a b) -> p a b", a=2),
                                                  sc.rearrange("p a (b k) -> p a b k", b=2), AX.X, ALU.max))
                        dve.wait_ge(st.sem, st.level())
                        out = probs[u % 4][:, :, :].rearrange("p (a b) k -> p a b k", a=2)
                        top = m.rearrange("p (a b) -> p a b", a=2).unsqueeze(3).broadcast_to([P, 2, 2, CTX])
                        dve.tensor_tensor(out, sc.rearrange("p a (b k) -> p a b k", b=2), top,
                                          ALU.subtract).then_inc(score.free(u), 1)

                    def normalise(u):
                        t, g = divmod(u, GROUPS)
                        n = U_PV + u
                        v = acc.buf(n)[:, 0:GH * VW].rearrange("p (j v) -> p j v", v=VW)
                        dve.wait_ge(acc.full(n), acc.fillings(it, n))
                        st.give(dve.reciprocal(rz[:, u % 2, :].unsqueeze(2), v[:, :, dk:VW]))
                        dve.wait_ge(st.sem, st.level())
                        dve.tensor_tensor(o[:, t, g * GH:(g + 1) * GH, :], v[:, :, 0:dk],
                                          rz[:, u % 2, :].unsqueeze(2).broadcast_to([P, GH, dk]), ALU.mult).then_inc(acc.free(n), 1)

                    for u in range(UNITS + 3):
                        if u < UNITS:
                            shift(u)
                        if u >= 3:
                            normalise(u - 3)
                    layernorm(dve, z, it + 1, xin, stats, mv, std, rstd, xn)
                    if not layer:
                        for t in range(TILES):
                            st.give(dve.tensor_tensor(xres[:, t, :], xres[:, t, :], row[:, :], ALU.add))
                        dve.wait_ge(st.sem, st.level())
                    for t in range(TILES):
                        n = U_OUT + t
                        bank = acc.buf(n)
                        dve.wait_ge(acc.full(n), acc.fillings(it, n))
                        if not layer:
                            dve.tensor_tensor(xres[:, t, :], bank[:, :], xres[:, t, :], ALU.add).then_inc(acc.free(n), 1)
                            continue
                        st.give(dve.bn_stats(bst[:, t, :], bank[:, :]))
                        hold(dve, st.sem, st.level(), z["held"])
                        dve.bn_aggr(bmv[:, t, :], bst[:, t, :]).then_inc(z["y_var"], 1)
                        dve.wait_ge(z["y_std"], it * TILES + t + 1)
                        st.give(dve.reciprocal(brstd[:, t:t + 1], bstd[:, t:t + 1]))
                        dve.wait_ge(st.sem, st.level())
                        yt = y[:, :]
                        dve.tensor_scalar(yt, bank[:, :], bmv[:, t, 0:1], brstd[:, t:t + 1], ALU.subtract,
                                          ALU.mult).then_inc(acc.free(n), 1)
                        dve.wait_ge(acc.free(n), acc.emptied_by(it, n))
                        st.give(dve.tensor_tensor(yt, yt, row[:, :], ALU.mult))
                        dve.wait_ge(st.sem, st.level())
                        dve.tensor_tensor(xres[:, t, :], xres[:, t, :], yt, ALU.add).then_inc(z["out_ready"], 1)
                    st.end()

            @block.gpsimd
            def _(pool):
                make_identity(pool, ident, z["id_step"])
                weights = a["down_w"] if layer else a["up_w"]
                pool.dma_start(by[:, :, :], a["W_conT" if layer else "W_exp"].rearrange("(c p) n -> p c n", p=P)).then_inc(z["bf_x"], 16)
                pool.wait_ge(z["bf_x"], 16)
                n_w = 0
                steps = 0
                for k in range(STAGES):
                    sidx = STAGES - 1 - k if layer else k
                    pool.dma_start(bw[:, :, :], weights[sidx].partition_broadcast(P)).then_inc(z["bf_w"], 16)
                    n_w += 16
                    pool.wait_ge(z["bf_w"], n_w)
                    with pool.Fori(0, DC) as r:
                        butterfly_stage(pool, by[:, bass.ds(r, 1), :].rearrange("p a n -> p (a n)"), bw, sidx, bool(layer),
                                        bt, z["bf_step"], r * 6 + steps, z["held"])
                    steps += 6 * DC
                pool.dma_start(s["wcon" if layer else "wexp"], by[:, :, :].rearrange("p c n -> p (c n)")).then_inc(z["bf_out"], 16)
                pool.wait_ge(z["bf_out"], 16)
                if layer:
                    pool.dma_start(bias_row, a["b_exp"]).then_inc(z["bf_x"], 16)
                    pool.dma_start(up_row, a["up_bias"]).then_inc(z["bf_x"], 16)
                    pool.wait_ge(z["bf_x"], 48)
                    for k in range(STAGES):
                        pool.dma_start(bw[0:1, :, :], a["up_w"][k].unsqueeze(0)).then_inc(z["bf_w"], 16)
                        n_w += 16
                        pool.wait_ge(z["bf_w"], n_w)
                        butterfly_stage(pool, bias_row, bw, k, False, bt, z["bf_step"], steps, z["held"])
                        steps += 6
                    pool.tensor_tensor(bias_row, bias_row, up_row, ALU.add).then_inc(z["bf_step"], 1)
                    pool.wait_ge(z["bf_step"], steps + 1)
                    pool.dma_start(s["bexp"], bias_row).then_inc(z["bf_out"], 16)
                    pool.wait_ge(z["bf_out"], 32)


DVE_STEPS = (36, 44)


def ffn0(nc, a, s, x_in, x_out):
    pre = "ff0"
    SPREADS = RH * TILES
    HALF = XROWS // 2
    LN_AT = 9
    W_USES = DC + TILES + 2 * FI + 2 * FI
    U_XT, U_SIM, U_GU, U_ST = 0, DC, DC + TILES, DC + TILES + 2 * FI
    with ExitStack() as ctx:
        sem = make_sem(nc, s["sems"], pre)
        sb = lambda name, shape, dt=F32: ctx.enter_context(nc.sbuf_tensor(f"{pre}_{name}", shape, dt))
        ident = sb("ident", [P, P])
        eps = sb("eps", [P, 1])
        downT = sb("downT", [P, DC, NEXP])
        up = sb("up", [P, FI, D])
        fold = sb("fold", [P, DC, D])
        bg, bu, bd = sb("bg", [P, FI]), sb("bu", [P, FI]), sb("bd", [P, D])
        xin, xres, xn = (sb(n, [P, TILES, D]) for n in ("xin", "xres", "xn"))
        xnT = sb("xnT", [P, DC, BLOCK])
        stats, mv = sb("stats", [P, TILES, 6]), sb("mv", [P, TILES, 2])
        std, rstd = sb("std", [P, TILES]), sb("rstd", [P, TILES])
        sim = xn[:, :, :].rearrange("p t (g k) -> p t g k", k=KEYS)
        G = sb("G", [P, TILES, NEXP])
        best = sb("best", [P, 1, 2 * RH, TOPK])
        place = sb("place", [P, 1, 2 * RH, TOPK], U32)
        placef = sb("placef", [P, 1, 2 * RH, TOPK], BF16)
        pair = sb("pair", [P, 1, RH, TOPK, TOPK])
        best2 = sb("best2", [P, 1, RH, TOPK])
        picked = sb("picked", [P, 1, RH, TOPK, TOPK])
        count = sb("count", [P, 1, RH, TOPK], BF16)
        ex = sb("ex", [P, TILES, 2 * RH, KEYS])
        ebest = sb("ebest", [P, 1, 2 * RH, TOPK])
        rows_w = sb("rows_w", [P, 1, RH, TOPK])
        norm = sb("norm", [P, 1, 2, RH])
        beyond = sb("beyond", [P, 1, RH, TOPK])
        beyond_w = sb("beyond_w", [P, TILES, 1])
        exn = sb("exn", [P, TILES, RH, XROWS])
        hot = sb("hot", [P, RH, KEYS, TOPK], BF16)
        cx = sb("cx", [P, TILES, RH, XROWS])
        qy = sb("qy", [P, TILES, RH, KEYS])
        index = sb("index", [P, KEYS, TOPK], BF16)
        falling = sb("falling", [P, TOPK], BF16)
        ps = lambda name: ctx.enter_context(nc.psum_tensor(f"{pre}_{name}", [P, 512], F32))
        work = Ring(sem, "work", [ps(f"work{i}") for i in range(4)], W_USES)
        MOVED = U_GU // 4
        accs = [ps(f"acc{i}") for i in range(TILES)]
        gu_w = Ring(sem, "gu_w", [sb(f"gu_w{i}", [P, 2, DC, P]) for i in range(2)], FI, parts=32)
        wd_w = Ring(sem, "wd_w", [sb(f"wd_w{i}", [P, D]) for i in range(2)], FI, parts=16)
        silu = Ring(sem, "silu", [sb(f"silu{i}", [P, BLOCK]) for i in range(2)], 2 * FI)
        hid = Ring(sem, "hid", [sb(f"hid{i}", [P, BLOCK]) for i in range(2)], 2 * FI)
        reach = [sb(f"reach{i}", [P, HALF, KEYS], BF16) for i in range(4)]
        outer = [sb(f"outer{i}", [P, HALF, KEYS]) for i in range(4)]
        z = Named(sem)
        z["held"] = s["held"]

        with nc.Block() as block:
            @block.sync
            def _(sp):
                sp.dma_start(xin[:, :, :], x_in[0].rearrange("p t d -> p (t d)")).then_inc(z["x_loaded"], 16)
                sp.dma_start(fold[:, :, :], s["fold"].rearrange("p (c n) -> p c n", c=DC)).then_inc(z["w_loaded"], 16)
                for t, name in ((bg, "bg"), (bu, "bu")):
                    sp.dma_start(t[:, :], a[name]).then_inc(z["w_loaded"], 16)
                sp.dma_start(bd[:, :], a["bd"].partition_broadcast(P)).then_inc(z["w_loaded"], 16)

                def load_gu(it, i):
                    if i >= 2:
                        n = U_GU + 2 * (i - 2) + 1
                        sp.wait_ge(work.full(n), work.fillings(it, n))
                    elif not isinstance(it, int) or it:
                        n = U_GU + 2 * (FI - 2 + i) + 1
                        sp.wait_ge(work.full(n), work.fillings(it - 1, n))
                    for k, w in enumerate(("Wg", "Wu")):
                        sp.dma_start(gu_w.buf(i)[:, k, :, :], a[w][i]).then_inc(gu_w.full(i), 16)

                def load_wd(it, i):
                    sp.wait_ge(wd_w.free(i), wd_w.emptyings(it, i))
                    sp.dma_start(wd_w.buf(i)[:, :], a["Wd"][i]).then_inc(wd_w.full(i), 16)

                def block_io(it, more):
                    for i in range(2):
                        load_gu(it, i)
                        load_wd(it, i)
                    sp.wait_ge(z["xn_ready"], (it + 1) * TILES)
                    nxt = bass.ds(it + 1, 1) if more else slice(it, it + 1)
                    sp.dma_start(xin[:, :, :], x_in[nxt].rearrange("a p t d -> (a p) (t d)")).then_inc(z["x_loaded"], 16)
                    if not isinstance(it, int) or it:
                        sp.wait_ge(z["stored"], it * 16)
                    sp.dma_start(xres[:, :, :], x_in[bass.ds(it, 1)].rearrange("a p t d -> (a p) (t d)")).then_inc(z["res_loaded"], 16)
                    for i in range(2, FI):
                        load_gu(it, i)
                        load_wd(it, i)
                        if isinstance(it, int) and it == 0 and i % 4 == 3:
                            c = i // 4
                            sp.dma_start(downT[:, c, :], a["downT"][c * P:(c + 1) * P, :]).then_inc(z["experts_loaded"], 16)
                            part = slice(c * 4, (c + 1) * 4)
                            sp.dma_start(up[:, part, :], a["up"].rearrange("(c p) n -> p c n", p=P)[:, part, :]).then_inc(z["experts_loaded"], 16)
                    sp.wait_ge(z["out_ready"], (it + 1) * TILES)
                    sp.dma_start(x_out[bass.ds(it, 1)].rearrange("a p t d -> (a p) (t d)"), xres[:, :, :]).then_inc(z["stored"], 16)

                block_io(0, True)
                with sp.Fori(1, BLOCKS - 1) as it:
                    block_io(it, True)
                block_io(BLOCKS - 1, False)
                sp.wait_ge(z["stored"], BLOCKS * 16)
                sp.wait_ge(z["x_loaded"], (BLOCKS + 1) * 16)

            @block.tensor
            def _(pe):
                pe.wait_ge(z["w_loaded"], 4 * 16)
                pe.wait_ge(z["id_step"], 2)
                with pe.Fori(0, BLOCKS) as it:
                    def take(n):
                        k = (n - U_GU) // 2 - 2
                        reader = hid if n % 2 else silu
                        if n < DC:
                            pass
                        elif k < 0:
                            pe.wait_ge(work.free(n), it * MOVED + (1 if n < U_GU else MOVED))
                        else:
                            pe.wait_ge(reader.full(k), reader.fillings(it, k))
                        return work.buf(n)

                    pe.wait_ge(z["xn_ready"], (it + 1) * TILES)
                    for c in range(DC):
                        bank = take(U_XT + c)
                        for t in range(TILES):
                            last = pe.transpose(bank[:, t * P:(t + 1) * P], xn[:, t, c * P:(c + 1) * P], ident[:, :])
                        last.then_inc(work.full(U_XT + c), 1)
                    for n in range(U_XT, U_SIM):
                        pe.wait_ge(work.free(n), it * MOVED + 1)
                    for t in range(TILES):
                        bank = take(U_SIM + t)
                        for c in range(DC):
                            last = pe.matmul(bank[:, :], xnT[:, c, t * P:(t + 1) * P], fold[:, c, :],
                                             start=c == 0, stop=c == DC - 1)
                        last.then_inc(work.full(U_SIM + t), 1)

                    def product(n, w):
                        bank = take(n)
                        for c in range(DC):
                            last = pe.matmul(bank[:, :], w(c), xnT[:, c, :], start=c == 0, stop=c == DC - 1)
                        last.then_inc(work.full(n), 1)

                    def accumulate(k, w):
                        pe.wait_ge(hid.full(k), hid.fillings(it, k))
                        h = hid.buf(k)
                        for t in range(TILES):
                            last = pe.matmul(accs[t][:, :], h[:, t * P:(t + 1) * P], w, start=k == 0, stop=k == 2 * FI - 1)
                            if k == 2 * FI - 1:
                                last.then_inc(z["summed"], 1)
                        return last

                    for i in range(FI + 1):
                        if i < FI:
                            pe.wait_ge(gu_w.full(i), gu_w.fillings(it, i))
                            w = gu_w.buf(i)
                            product(U_GU + 2 * i, lambda c: w[:, 0, c, :])
                            bank = take(U_GU + 2 * i + 1)
                            for c in range(DC):
                                last = pe.matmul(bank[:, :], w[:, 1, c, :], xnT[:, c, :], start=c == 0, stop=c == DC - 1)
                            last.then_inc(work.full(U_GU + 2 * i + 1), 1)
                        if i:
                            k = i - 1
                            pe.wait_ge(wd_w.full(k), wd_w.fillings(it, k))
                            accumulate(k, wd_w.buf(k)[:, :]).then_inc(wd_w.free(k), 1)
                    pe.wait_ge(z["experts_loaded"], 8 * 16)
                    for i in range(FI + 1):
                        if i < FI:
                            product(U_ST + 2 * i, lambda c: downT[:, c, i * P:(i + 1) * P])
                            if i == 0:
                                pe.wait_ge(z["spread"], it * 2 * SPREADS + SPREADS)
                            if i == FI // 2:
                                pe.wait_ge(z["G_ready"], (it + 1) * TILES)
                            bank = take(U_ST + 2 * i + 1)
                            for t in range(TILES):
                                last = pe.transpose(bank[:, t * P:(t + 1) * P], G[:, t, i * P:(i + 1) * P], ident[:, :])
                            last.then_inc(work.full(U_ST + 2 * i + 1), 1)
                        if i:
                            last = accumulate(FI + i - 1, up[:, i - 1, :])
                            if i <= FI - 2:
                                last.then_inc(z["spent"], 1)

            @block.scalar
            def _(act):
                act.wait_ge(z["eps_done"], 1)
                act.wait_ge(z["w_loaded"], 4 * 16)
                deviations(act, z, 0, std, mv, eps)
                with act.Fori(0, BLOCKS) as it:
                    for c in range(DC):
                        act.wait_ge(work.full(c), work.fillings(it, c))
                        act.copy(xnT[:, c, :], work.buf(c)[:, :]).then_inc(work.free(c), 1)
                    for t in range(TILES):
                        n = U_SIM + t
                        act.wait_ge(work.full(n), work.fillings(it, n))
                        act.copy(sim[:, t, :, :], work.buf(n)[:, :].rearrange("p (g k) -> p g k", k=KEYS)).then_inc(work.free(n), 1)

                    def silu_of(n, k, bias):
                        act.wait_ge(work.full(n), work.fillings(it, n))
                        if k >= 2:
                            act.wait_ge(hid.full(k - 2), hid.fillings(it, k - 2))
                        act.activation(silu.buf(k)[:, :], work.buf(n)[:, :], ACT.Silu, bias=bias).then_inc(silu.full(k), 1)

                    for i in range(FI):
                        silu_of(U_GU + 2 * i, i, bg[:, i:i + 1])
                        if i % RH == 0:
                            t = i // RH
                            act.wait_ge(z["diff_ready"], (it * TILES + t + 1) * 2)
                            act.activation(ex[:, t, :, :], ex[:, t, :, :], ACT.Exp).then_inc(z["exp_done"], 1)
                            act.activation(ebest[:, 0, :, :], ebest[:, 0, :, :], ACT.Exp).then_inc(z["exp_done"], 1)
                    for i in range(FI):
                        silu_of(U_ST + 2 * i, FI + i, 0.0)
                        if i == LN_AT:
                            deviations(act, z, it + 1, std, mv, eps)

            @block.gpsimd
            def _(pool):
                make_identity(pool, ident, z["id_step"])
                pool.iota(index[:, :, :], [[1, KEYS], [0, TOPK]], base=0, channel_multiplier=0,
                          allow_small_or_imprecise_dtypes=True).then_inc(z["const_done"], 1)
                pool.iota(falling[:, :], [[-1, TOPK]], base=TOPK, channel_multiplier=0,
                          allow_small_or_imprecise_dtypes=True).then_inc(z["const_done"], 1)
                with pool.Fori(0, BLOCKS) as it:
                    for m in range(2 * SPREADS):
                        half, t, h = m // SPREADS, m % SPREADS // RH, m % RH
                        if half == 0 and h == 0:
                            pool.wait_ge(z["sel_ready"], (it * TILES + t + 1) * 3)
                        if m >= 4:
                            pool.wait_ge(z["spread"], it * 2 * SPREADS + m - 3)
                        i = slice(half * HALF, (half + 1) * HALF)
                        wide = lambda v: v.unsqueeze(2).broadcast_to([P, HALF, KEYS])
                        flat = lambda v: v.unsqueeze(1).broadcast_to([P, HALF, KEYS])
                        pool.tensor_tensor(reach[m % 4][:, :, :], wide(cx[:, t, h, i]), flat(qy[:, t, h, :]),
                                           ALU.add).then_inc(z["paired"], 1)
                        pool.tensor_tensor(outer[m % 4][:, :, :], wide(exn[:, t, h, i]), flat(ex[:, t, RH + h, :]),
                                           ALU.mult).then_inc(z["paired"], 1)

            @block.vector
            def _(dve):
                dve.memset(eps[:, :], EPS).then_inc(z["eps_done"], 1)
                dve.wait_ge(z["const_done"], 2)
                dve.wait_ge(z["w_loaded"], 4 * 16)
                layernorm(dve, z, 0, xin, stats, mv, std, rstd, xn)
                with dve.Fori(0, BLOCKS) as it:
                    st = Steps(z["dve_step"], it, FF0_STEPS)

                    def settle():
                        dve.wait_ge(st.sem, st.level())

                    full = [P, RH, TOPK, TOPK]
                    own = 0

                    def candidates(t):
                        hold(dve, work.free(U_SIM + t), (it + 1) * MOVED, z["held"])
                        for g in range(2 * RH):
                            st.give(dve.max(best[:, own, g, :], sim[:, t, g, :]))
                        hold(dve, st.sem, st.level(), z["held"])
                        for g in range(2 * RH):
                            st.give(dve.max_index(place[:, own, g, :], best[:, own, g, :], sim[:, t, g, :]))
                        b = best[:, own, :, :]
                        top = lambda n: b[:, :, 0:1].broadcast_to([P, 2 * RH, n])
                        dve.tensor_tensor(ex[:, t, :, :], sim[:, t, :, :], top(KEYS), ALU.subtract).then_inc(z["diff_ready"], 1)
                        dve.tensor_tensor(ebest[:, own, :, :], b, top(TOPK), ALU.subtract).then_inc(z["diff_ready"], 1)

                    def pairs(t):
                        b = best[:, own, :, :]
                        st.give(dve.tensor_tensor(pair[:, own, :, :, :], b[:, 0:RH, :].unsqueeze(3).broadcast_to(full),
                                                  b[:, RH:, :].unsqueeze(2).broadcast_to(full), ALU.add))
                        hold(dve, st.sem, st.level(), z["held"])
                        for h in range(RH):
                            st.give(dve.max(best2[:, own, h, :], pair[:, own, h, :, :]))
                        st.give(dve.tensor_copy(placef[:, own, :, :], place[:, own, :, :]))
                        st.give(dve.tensor_scalar(beyond[:, own, :, :], place[:, own, 0:RH, :], float(XROWS), None, ALU.is_ge))
                        hold(dve, st.sem, st.level(), z["held"])
                        for h in range(RH):
                            st.give(dve.match_replace(picked[:, own, h, :, :], best2[:, own, h, :], pair[:, own, h, :, :], LOW))
                        settle()
                        st.give(dve.tensor_tensor(picked[:, own], picked[:, own], pair[:, own], ALU.not_equal))
                        settle()
                        with nc.allow_low_precision(reason="counts of at most eight are exact"):
                            st.give(dve.tensor_reduce(count[:, own, :, :], picked[:, own], AX.X, ALU.add))

                    def rows(t):
                        xs = [P, RH, XROWS, TOPK]
                        px, hot_x = placef[:, own, 0:RH, :], hot[:, :, 0:XROWS, :]
                        st.give(dve.tensor_tensor(hot_x, index[:, 0:XROWS, :].unsqueeze(1).broadcast_to(xs),
                                                  px.unsqueeze(2).broadcast_to(xs), ALU.is_equal))
                        dve.wait_ge(z["exp_done"], (it * TILES + t + 1) * 2)
                        e = ebest[:, own, :, :]
                        st.give(dve.tensor_tensor(pair[:, own], e[:, 0:RH, :].unsqueeze(3).broadcast_to(full),
                                                  e[:, RH:, :].unsqueeze(2).broadcast_to(full), ALU.mult))
                        settle()
                        st.give(dve.tensor_tensor(hot_x, hot_x, count[:, own, :, :].unsqueeze(2).broadcast_to(xs), ALU.mult))
                        st.give(dve.tensor_tensor(pair[:, own], pair[:, own], picked[:, own], ALU.mult))
                        settle()
                        dve.tensor_reduce(cx[:, t, :, :], hot_x, AX.X, ALU.add).then_inc(z["sel_ready"], 1)
                        st.give(dve.tensor_reduce(rows_w[:, own, :, :], pair[:, own], AX.X, ALU.add))
                        settle()
                        st.give(dve.tensor_reduce(norm[:, own, 0, :], rows_w[:, own, :, :], AX.X, ALU.add))
                        settle()
                        st.give(dve.reciprocal(norm[:, own, 1, :], norm[:, own, 0, :]))
                        settle()
                        inv = norm[:, own, 1, :].unsqueeze(2)
                        dve.tensor_tensor(exn[:, t, :, :], ex[:, t, 0:RH, 0:XROWS], inv.broadcast_to([P, RH, XROWS]),
                                          ALU.mult).then_inc(z["sel_ready"], 1)
                        st.give(dve.tensor_tensor(rows_w[:, own, :, :], rows_w[:, own, :, :], inv.broadcast_to([P, RH, TOPK]), ALU.mult))
                        settle()
                        st.give(dve.tensor_tensor(rows_w[:, own, :, :], rows_w[:, own, :, :], beyond[:, own, :, :], ALU.mult))
                        settle()
                        st.give(dve.tensor_reduce(beyond_w[:, t, :], rows_w[:, own, :, :], AX.XY, ALU.add))

                    def columns(t):
                        ys = [P, RH, KEYS, TOPK]
                        st.give(dve.tensor_tensor(hot[:, :, :, :], index[:, :, :].unsqueeze(1).broadcast_to(ys),
                                                  placef[:, own, RH:, :].unsqueeze(2).broadcast_to(ys), ALU.is_equal))
                        settle()
                        fall = falling[:, :].unsqueeze(1).broadcast_to([P, RH * KEYS, TOPK])
                        hy = hot[:, :, :, :].rearrange("p h j b -> p (h j) b")
                        st.give(dve.tensor_tensor(hy, hy, fall, ALU.mult))
                        settle()
                        dve.tensor_reduce(qy[:, t, :, :], hot[:, :, :, :], AX.X, ALU.add).then_inc(z["sel_ready"], 1)

                    def spread(m):
                        half, t, h = m // SPREADS, m % SPREADS // RH, m % RH
                        g = G[:, t, half * NEXP // 2:(half + 1) * NEXP // 2].rearrange("p (i j) -> p i j", j=KEYS)
                        dve.wait_ge(z["paired"], (it * 2 * SPREADS + m + 1) * 2)
                        r, w = reach[m % 4][:, :, :], outer[m % 4][:, :, :]
                        if h == 0:
                            last = dve.scalar_tensor_tensor(out=g, in0=r, scalar=float(TOPK), in1=w, op0=ALU.is_gt, op1=ALU.mult)
                        else:
                            st.give(dve.scalar_tensor_tensor(out=w, in0=r, scalar=float(TOPK), in1=w, op0=ALU.is_gt, op1=ALU.mult))
                            settle()
                            last = dve.tensor_tensor(g, g, w, ALU.add)
                        last.then_inc(z["spread"], 1)
                        if half and h == RH - 1:
                            dve.wait_ge(z["spread"], it * 2 * SPREADS + m + 1)
                            dve.tensor_tensor(G[:, t, NEXP - 1:], G[:, t, NEXP - 1:], beyond_w[:, t, :],
                                              ALU.add).then_inc(z["G_ready"], 1)

                    def hidden(n, k, bias):
                        dve.wait_ge(work.full(n), work.fillings(it, n))
                        dve.wait_ge(silu.full(k), silu.fillings(it, k))
                        if 2 <= k < FI + 2:
                            dve.wait_ge(wd_w.free(k - 2), wd_w.emptied_by(it, k - 2))
                        elif k >= FI + 2:
                            dve.wait_ge(z["spent"], it * (FI - 2) + k - 2 - FI + 1)
                        if bias is None:
                            dve.tensor_tensor(hid.buf(k)[:, :], work.buf(n)[:, :], silu.buf(k)[:, :], ALU.mult).then_inc(hid.full(k), 1)
                        else:
                            dve.scalar_tensor_tensor(out=hid.buf(k)[:, :], in0=work.buf(n)[:, :], scalar=bias,
                                                     in1=silu.buf(k)[:, :], op0=ALU.add, op1=ALU.mult).then_inc(hid.full(k), 1)

                    for i in range(FI):
                        t = i // 4
                        (candidates, pairs, rows, columns)[i % 4](t)
                        if t:
                            spread(i - 4)
                        hidden(U_GU + 2 * i + 1, i, bu[:, i:i + 1])
                    for m in range(SPREADS - 4, SPREADS):
                        spread(m)
                    for i in range(FI):
                        if i < FI // 2:
                            spread(SPREADS + 2 * i)
                            spread(SPREADS + 2 * i + 1)
                        hidden(U_ST + 2 * i + 1, FI + i, None)
                        if i == LN_AT:
                            layernorm(dve, z, it + 1, xin, stats, mv, std, rstd, xn)
                    dve.wait_ge(z["res_loaded"], (it + 1) * 16)
                    for t in range(TILES):
                        st.give(dve.tensor_tensor(xres[:, t, :], xres[:, t, :], bd[:, :], ALU.add))
                    settle()
                    dve.wait_ge(z["summed"], (it + 1) * TILES)
                    for t in range(TILES):
                        dve.tensor_tensor(xres[:, t, :], accs[t][:, :], xres[:, t, :], ALU.add).then_inc(z["out_ready"], 1)
                    st.end()


def split_product(pe, out, lhsT, rhs, start, stop):
    for k, (x, y) in enumerate(((0, 0), (0, 1), (1, 0))):
        last = pe.matmul(out, lhsT(x), rhs(y), start=start and k == 0, stop=stop and k == 2)
    return last


def ffn1(nc, a, s, x_in, x_out):
    pre = "ff1"
    USES = DC + FI
    LAG = 2
    with ExitStack() as ctx:
        sem = make_sem(nc, s["sems"], pre)
        sb = lambda name, shape, dt=F32: ctx.enter_context(nc.sbuf_tensor(f"{pre}_{name}", shape, dt))
        ident = sb("ident", [P, P])
        eps = sb("eps", [P, 1])
        wexp = sb("wexp", [P, 2, DC, F], F32R)
        wcon = sb("wcon", [P, 2, FI, D], F32R)
        room = sb("room", [P, 4, F])
        stage = Ring(sem, "stage", [room[:, i, :] for i in range(4)], 2 * DC, parts=16)
        xnT = room[:, 0:2, :].bitcast(F32R).rearrange("p h (c b) -> p h c b", c=DC)
        hid = [room[:, 2 + i // 2, i % 2 * 2 * BLOCK:(i % 2 + 1) * 2 * BLOCK].bitcast(F32R).rearrange("p (h b) -> p h b", h=2)
               for i in range(4)]
        bh, bias = sb("bh", [P, FI]), sb("bias", [P, 2, D])
        xin, xres, xn = (sb(n, [P, TILES, D]) for n in ("xin", "xres", "xn"))
        act_out = [sb(f"act{i}", [P, BLOCK]) for i in range(2)]
        stats, mv = sb("stats", [P, TILES, 6]), sb("mv", [P, TILES, 2])
        std, rstd = sb("std", [P, TILES]), sb("rstd", [P, TILES])
        ps = lambda name: ctx.enter_context(nc.psum_tensor(f"{pre}_{name}", [P, 512], F32))
        work = Ring(sem, "work", [ps(f"work{i}") for i in range(4)], USES)
        accs = [ps(f"acc{i}") for i in range(TILES)]
        z = Named(sem)
        z["held"] = s["held"]

        with nc.Block() as block:
            @block.sync
            def _(sp):
                for n in range(2 * DC):
                    c = n % DC
                    if n >= 4:
                        sp.wait_ge(stage.free(n), stage.emptyings(0, n))
                    src = s["wcon" if n >= DC else "wexp"].rearrange("p (c n) -> p c n", c=DC)[:, c, :]
                    sp.dma_start(stage.buf(n), src).then_inc(stage.full(n), 16)
                    if n == 0:
                        sp.dma_start(xin[:, :, :], x_in[0].rearrange("p t d -> p (t d)")).then_inc(z["x_loaded"], 16)
                sp.dma_start(bh[:, :], s["bexp"].rearrange("a (i p) -> p (a i)", p=P), allow_slow_non_contiguous=True).then_inc(z["b_loaded"], 16)
                for k, name in enumerate(("b_con", "down_bias")):
                    sp.dma_start(bias[:, k, :], a[name].partition_broadcast(P)).then_inc(z["b_loaded"], 16)

                def block_io(it, more):
                    sp.wait_ge(z["xn_ready"], (it + 1) * TILES)
                    nxt = bass.ds(it + 1, 1) if more else slice(it, it + 1)
                    sp.dma_start(xin[:, :, :], x_in[nxt].rearrange("a p t d -> (a p) (t d)")).then_inc(z["x_loaded"], 16)
                    if not isinstance(it, int) or it:
                        sp.wait_ge(z["stored"], it * 16)
                    sp.dma_start(xres[:, :, :], x_in[bass.ds(it, 1)].rearrange("a p t d -> (a p) (t d)")).then_inc(z["res_loaded"], 16)
                    sp.wait_ge(z["out_ready"], (it + 2) * TILES)
                    sp.dma_start(x_out[bass.ds(it, 1)].rearrange("a p t d -> (a p) (t d)"), xres[:, :, :]).then_inc(z["stored"], 16)

                block_io(0, True)
                with sp.Fori(1, BLOCKS - 1) as it:
                    block_io(it, True)
                block_io(BLOCKS - 1, False)
                sp.wait_ge(z["stored"], BLOCKS * 16)
                sp.wait_ge(z["x_loaded"], (BLOCKS + 1) * 16)

            @block.tensor
            def _(pe):
                pe.wait_ge(z["id_step"], 2)
                for c in range(DC):
                    n = DC + c
                    pe.wait_ge(stage.full(n), stage.fillings(0, n))
                    for q in range(4):
                        if c:
                            pe.wait_ge(z["wcon_ready"], (c - 1) * 4 + q + 1)
                        for j in range(4):
                            i = 4 * q + j
                            last = pe.transpose(accs[q][:, j * P:(j + 1) * P], stage.buf(n)[:, i * P:(i + 1) * P], ident[:, :])
                        last.then_inc(z["turned"], 1)
                pe.wait_ge(z["wcon_ready"], FI)
                with pe.Fori(0, BLOCKS) as it:
                    def take(n):
                        if n >= 4:
                            pe.wait_ge(work.free(n), work.emptyings(it, n))
                        return work.buf(n)

                    pe.wait_ge(z["xn_ready"], (it + 1) * TILES)
                    for c in range(DC):
                        bank = take(c)
                        for t in range(TILES):
                            last = pe.transpose(bank[:, t * P:(t + 1) * P], xn[:, t, c * P:(c + 1) * P], ident[:, :])
                        last.then_inc(work.full(c), 1)
                    for c in range(DC):
                        pe.wait_ge(work.free(c), work.emptied_by(it, c))
                    for i in range(FI + LAG):
                        if i < FI:
                            n = DC + i
                            bank = take(n)
                            for c in range(DC):
                                last = split_product(pe, bank[:, :], lambda x: wexp[:, x, c, i * P:(i + 1) * P],
                                                     lambda y: xnT[:, y, c, :], c == 0, c == DC - 1)
                            last.then_inc(work.full(n), 1)
                        if i >= LAG:
                            k = i - LAG
                            pe.wait_ge(z["hid_ready"], it * FI + k + 1)
                            for t in range(TILES):
                                if k == 0:
                                    pe.wait_ge(z["out_ready"], it * TILES + t + 1)
                                last = split_product(pe, accs[t][:, :], lambda x: hid[k % 4][:, x, t * P:(t + 1) * P],
                                                     lambda y: wcon[:, y, k, :], k == 0, k == FI - 1)
                                if k == FI - 1:
                                    last.then_inc(z["summed"], 1)
                            if k < FI - 1:
                                last.then_inc(z["spent"], 1)

            @block.scalar
            def _(act):
                for c in range(DC):
                    act.wait_ge(stage.full(c), stage.fillings(0, c))
                    act.copy(wexp[:, 0, c, :], stage.buf(c)).then_inc(z["high"], 1)
                for c in range(DC):
                    for q in range(4):
                        act.wait_ge(z["turned"], c * 4 + q + 1)
                        act.copy(wcon[:, 0, 4 * q:4 * q + 4, c * P:(c + 1) * P],
                                 accs[q][:, :].rearrange("p (j n) -> p j n", j=4)).then_inc(z["high"], 1)
                act.wait_ge(z["eps_done"], 1)
                act.wait_ge(z["b_loaded"], 3 * 16)
                deviations(act, z, 0, std, mv, eps)
                with act.Fori(0, BLOCKS) as it:
                    for c in range(DC):
                        act.wait_ge(work.full(c), work.fillings(it, c))
                        act.copy(xnT[:, 0, c, :], work.buf(c)[:, :]).then_inc(z["x_high"], 1)
                    for i in range(FI):
                        n = DC + i
                        act.wait_ge(work.full(n), work.fillings(it, n))
                        if i >= 2:
                            act.wait_ge(z["hid_ready"], it * FI + i - 1)
                        act.activation(act_out[i % 2][:, :], work.buf(n)[:, :], ACT.Gelu, bias=bh[:, i:i + 1]).then_inc(work.free(n), 1)
                        act.wait_ge(work.free(n), work.emptied_by(it, n))
                        if i >= 4:
                            act.wait_ge(z["spent"], it * (FI - 1) + i - 3)
                        act.copy(hid[i % 4][:, 0, :], act_out[i % 2][:, :]).then_inc(z["hid_high"], 1)
                        if i == FI // 2:
                            deviations(act, z, it + 1, std, mv, eps)

            @block.gpsimd
            def _(pool):
                make_identity(pool, ident, z["id_step"])

            @block.vector
            def _(dve):
                dve.memset(eps[:, :], EPS).then_inc(z["eps_done"], 1)
                dve.sem_inc(z["out_ready"], TILES)
                for c in range(DC):
                    dve.wait_ge(z["high"], c + 1)
                    dve.tensor_tensor(wexp[:, 1, c, :], stage.buf(c), wexp[:, 0, c, :].bitcast(F32),
                                      ALU.subtract).then_inc(stage.free(c), 1)
                for c in range(DC):
                    for q in range(4):
                        dve.wait_ge(z["high"], DC + c * 4 + q + 1)
                        part = lambda h: wcon[:, h, 4 * q:4 * q + 4, c * P:(c + 1) * P]
                        dve.tensor_tensor(part(1), accs[q][:, :].rearrange("p (j n) -> p j n", j=4), part(0).bitcast(F32),
                                          ALU.subtract).then_inc(z["wcon_ready"], 1)
                dve.wait_ge(z["b_loaded"], 3 * 16)
                dve.tensor_tensor(bias[:, 0, :], bias[:, 0, :], bias[:, 1, :], ALU.add).then_inc(z["bias_done"], 1)
                dve.wait_ge(z["bias_done"], 1)
                layernorm(dve, z, 0, xin, stats, mv, std, rstd, xn)
                with dve.Fori(0, BLOCKS) as it:
                    st = Steps(z["dve_step"], it, TILES)
                    for c in range(DC):
                        dve.wait_ge(z["x_high"], it * DC + c + 1)
                        dve.tensor_tensor(xnT[:, 1, c, :], work.buf(c)[:, :], xnT[:, 0, c, :].bitcast(F32),
                                          ALU.subtract).then_inc(work.free(c), 1)
                    for i in range(FI):
                        dve.wait_ge(z["hid_high"], it * FI + i + 1)
                        h = hid[i % 4]
                        dve.tensor_tensor(h[:, 1, :], act_out[i % 2][:, :], h[:, 0, :].bitcast(F32),
                                          ALU.subtract).then_inc(z["hid_ready"], 1)
                        if i == FI // 2:
                            layernorm(dve, z, it + 1, xin, stats, mv, std, rstd, xn)
                    dve.wait_ge(z["res_loaded"], (it + 1) * 16)
                    for t in range(TILES):
                        st.give(dve.tensor_tensor(xres[:, t, :], xres[:, t, :], bias[:, 0, :], ALU.add))
                    dve.wait_ge(st.sem, st.level())
                    dve.wait_ge(z["summed"], (it + 1) * TILES)
                    for t in range(TILES):
                        dve.tensor_tensor(xres[:, t, :], accs[t][:, :], xres[:, t, :], ALU.add).then_inc(z["out_ready"], 1)
                    st.end()


FF0_STEPS = 192


PHASES = 5


def build(nc, a, out, sems):
    scratch = lambda name, shape: nc.dram_tensor("scratch_" + name, shape, F32).ap()
    s = {"kz": [scratch(f"kz{i}", (BATCH, P, HEADS * CTX)) for i in range(2)],
         "vm": [scratch(f"vm{i}", (BATCH, P, HEADS * (dk + 1))) for i, dk in enumerate((32, 64))],
         "vr": [scratch(f"vr{i}", (BATCH, REM, HEADS * (dk + 1))) for i, dk in enumerate((32, 64))],
         "fold": scratch("fold", (P, DC * D)), "wexp": scratch("wexp", (P, DC * F)),
         "wcon": scratch("wcon", (P, DC * F)), "bexp": scratch("bexp", (1, F))}
    s["sems"] = sems
    s["held"] = sems.enter_context(nc.semaphore("held"))
    blocks = lambda ap: ap.rearrange("(a p t) d -> a p t d", p=P, t=TILES)
    x = [blocks(a["x"])] + [blocks(scratch(f"x{i}", (TOKENS, D))) for i in (1, 2, 3)] + [blocks(out)]
    prepare(nc, a, s)
    attention(nc, a, s, 0, x[0], x[1])
    if PHASES > 2:
        ffn0(nc, a, s, x[1], x[2])
    if PHASES > 3:
        attention(nc, a, s, 1, x[2], x[3])
    if PHASES > 4:
        ffn1(nc, a, s, x[3], x[4])


def kernel(**inputs):
    import numpy as np
    import concourse.bacc as bacc
    from concourse.bass_utils import run_bass_kernel_spmd

    v = {k: np.asarray(w) for k, w in inputs.items()}
    cols = lambda b: b.reshape(-1, P).T
    tiles = lambda w: w.reshape(DC, P, FI, P).transpose(2, 1, 0, 3)
    laid = {
        "x": v["x"].reshape(TOKENS, D), "ctxT": v["ctx_1024"].transpose(0, 2, 1),
        "wq0": v["L0_xattn_w_q"].T, "wkT0": v["L0_xattn_w_k"].T, "wvT0": v["L0_xattn_w_v"].T, "wo0": v["L0_xattn_w_o"].T,
        "bq0": cols(v["L0_xattn_b_q"]), "bk0": cols(v["L0_xattn_b_k"]), "bv0": v["L0_xattn_b_v"], "bo0": v["L0_xattn_b_o"],
        "Wg": tiles(v["L0_ffn_Wg"]), "Wu": tiles(v["L0_ffn_Wu"]), "Wd": v["L0_ffn_Wd"].reshape(FI, P, D),
        "bg": cols(v["L0_ffn_bg"]), "bu": cols(v["L0_ffn_bu"]), "bd": v["L0_ffn_bd"],
        "WqT": v["L0_ffn_Wq"].T, "keysT": v["L0_ffn_keys"].transpose(2, 0, 3, 1).reshape(2 * RH * KEYS, KEYS),
        "downT": v["L0_ffn_down_embed"].T, "up": v["L0_ffn_up_embed"],
        "wkv1": v["L1_xattn_w_kv"], "wq1": v["L1_xattn_w_q"], "wo1": v["L1_xattn_w_out1"], "w2": v["L1_xattn_w_out2"],
        "gamma": v["L1_xattn_gamma"],
        "W_exp": v["L1_ffn_W_exp"], "b_exp": v["L1_ffn_b_exp"].reshape(1, F), "up_bias": v["L1_ffn_up_bias"].reshape(1, F),
        "up_w": v["L1_ffn_up_weights"].transpose(0, 2, 3, 1).reshape(STAGES, 4, F // 2),
        "down_w": v["L1_ffn_down_weights"].transpose(0, 2, 3, 1).reshape(STAGES, 4, F // 2),
        "W_conT": v["L1_ffn_W_con"].T, "b_con": v["L1_ffn_b_con"], "down_bias": v["L1_ffn_down_bias"],
    }
    nc = bacc.Bacc("TRN2", target_bir_lowering=False, num_devices=1)
    arrays, a = {}, {}
    for name, w in laid.items():
        arrays["in_" + name] = np.ascontiguousarray(w)
        a[name] = nc.dram_tensor("in_" + name, w.shape, mybir.dt.from_np(w.dtype), kind="ExternalInput").ap()
    out = nc.dram_tensor("out_0", (TOKENS, D), F32, kind="ExternalOutput").ap()
    with ExitStack() as sems:
        build(nc, a, out, sems)
    r = run_bass_kernel_spmd(nc, [arrays], core_ids=[0])
    return r.results[0]["out_0"].reshape(BATCH, TOKENS // BATCH, D)
```

```python
import concourse.bass as bass
from concourse import mybir
from contextlib import ExitStack

F32 = mybir.dt.float32
F32R = mybir.dt.float32r
BF16 = mybir.dt.bfloat16
U32 = mybir.dt.uint32
ALU = mybir.AluOpType
ACT = mybir.ActivationFunctionType
AX = mybir.AxisListType

P = 128
D = 512
DC = D // P
TILES = 4
BLOCK = TILES * P
TOKENS = 4096
BLOCKS = TOKENS // BLOCK
BATCH = 2
CTX = 154
REM = CTX - P
HEADS = 16
GH = 4
GROUPS = HEADS // GH
UNITS = TILES * GROUPS
F = 2048
FI = F // P
EPS = 1e-5
KEYS = 64
RH = 4
TOPK = 8
NEXP = 2048
XROWS = NEXP // KEYS
STAGES = 11
LOW = -3.0e38


class Named(dict):

    def __init__(self, make):
        super().__init__()
        self.make = make

    def __missing__(self, name):
        self[name] = self.make(name)
        return self[name]


class Ring:

    def __init__(self, sem, name, buffers, uses, parts=1, drains=1, start=0, before=0):
        assert uses % len(buffers) == 0
        self.buffers, self.parts, self.drains, self.each = buffers, parts, drains, uses // len(buffers)
        self.start = start
        self.before = before
        self.filled = Named(lambda i: sem(f"{name}_filled{i}"))
        self.emptied = Named(lambda i: sem(f"{name}_emptied{i}"))

    def buf(self, n):
        return self.buffers[n % len(self.buffers)]

    def full(self, n):
        return self.filled[n % len(self.buffers)]

    def free(self, n):
        return self.emptied[n % len(self.buffers)]

    def fillings(self, it, n):
        return it * (self.each * self.parts) + (n // len(self.buffers) + 1) * self.parts + self.before

    def emptyings(self, it, n):
        return (it * self.each + n // len(self.buffers)) * self.drains + self.start

    def emptied_by(self, it, n):
        return it * (self.each * self.drains) + (n // len(self.buffers) + 1) * self.drains + self.start


class Steps:

    def __init__(self, sem, it, each):
        self.sem, self.it, self.each, self.n = sem, it, each, 0

    def give(self, ins):
        ins.then_inc(self.sem, 1)
        self.n += 1

    def level(self):
        return self.it * self.each + self.n

    def end(self):
        assert self.n == self.each, f"a pass gives {self.n} steps"


def make_sem(nc, ctx, prefix):
    return lambda name: ctx.enter_context(nc.semaphore(f"{prefix}_{name}"))


def hold(engine, sem, value, held):
    engine.wait_ge(sem, value)
    engine.sem_inc(held, 1)


def make_identity(pool, ident, step):
    pool.memset(ident[:, :], 0.0).then_inc(step, 1)
    pool.wait_ge(step, 1)
    pool.affine_select(out=ident[:, :], in_=ident[:, :], compare_op=ALU.not_equal, fill=1.0, base=0,
                       pattern=[[-1, P]], channel_multiplier=1).then_inc(step, 1)


def prepare(nc, a, s):
    with ExitStack() as ctx:
        sem = make_sem(nc, s["sems"], "prep")
        sb = lambda name, shape, dt=F32: ctx.enter_context(nc.sbuf_tensor("prep_" + name, shape, dt))
        ctxT = sb("ctxT", [P, BATCH, DC, CTX])
        wk0 = sb("wk0", [P, DC, D])
        wv0 = sb("wv0", [P, DC, D])
        wkv1 = sb("wkv1", [P, DC, 2048])
        wqT = sb("wqT", [P, DC, D])
        keyz = sb("keyz", [P, RH, P])
        bk0 = sb("bk0", [P, DC])
        bv0 = sb("bv0", [P, D])
        kz = [sb(f"kz{i}", [P, BATCH, HEADS, CTX]) for i in range(2)]
        dks = (32, 64)
        vm = [sb(f"vm{i}", [P, BATCH, HEADS, dks[i] + 1]) for i in range(2)]
        vr = [sb(f"vr{i}", [REM, BATCH, HEADS, dks[i] + 1]) for i in range(2)]
        fold = sb("fold", [P, DC, D])
        banks = [ctx.enter_context(nc.psum_tensor(f"prep_ps{i}", [P, 512], F32)) for i in range(8)]
        loaded = sem("loaded")
        keys_loaded = sem("keys_loaded")
        later_loaded = sem("later_loaded")
        zeroed = sem("zeroed")
        stored = sem("stored")

        jobs = []
        for layer in range(2):
            for b in range(BATCH):
                jobs += [("k", layer, b, f) for f in range(HEADS * dks[layer] // P)]
                jobs += [("v", layer, b, (part, n)) for part in range(2) for n in range(HEADS * dks[layer] // 512)]
            if layer == 0:
                jobs += [("fold", 0, 0, c) for c in range(DC)]
        k_steps = lambda n: sum(P // dks[q[1]] for q in jobs[:n] if q[0] == "k")
        v_steps = lambda n: sum(q[0] != "k" for q in jobs[:n])
        made = sem("made")
        k_done, v_done = sem("k_done"), sem("v_done")

        with nc.Block() as block:
            @block.sync
            def _(sp):
                sp.dma_start(ctxT[:, :, :, :], a["ctxT"].rearrange("b (c p) s -> p b c s", p=P)).then_inc(loaded, 16)
                load = lambda w, src, to: sp.dma_start(w[:, :, :], src.rearrange("(c p) n -> p c n", p=P)).then_inc(to, 16)
                load(wk0, a["wkT0"], loaded)
                load(wv0, a["wvT0"], loaded)
                sp.dma_start(bk0[:, :], a["bk0"]).then_inc(loaded, 16)
                sp.dma_start(bv0[:, :], a["bv0"].partition_broadcast(P)).then_inc(loaded, 16)
                load(wqT, a["WqT"], keys_loaded)
                sp.wait_ge(zeroed, 1)
                src = a["keysT"].rearrange("(g q n) k -> q n g k", q=2, n=KEYS)
                for q in range(2):
                    rows = slice(q * KEYS, (q + 1) * KEYS)
                    sp.dma_start(keyz[rows, :, rows], src[q]).then_inc(keys_loaded, 16)
                load(wkv1, a["wkv1"], later_loaded)
                for layer in range(2):
                    for b in range(BATCH):
                        n = max(n for n, q in enumerate(jobs) if q[0] == "v" and q[1:3] == (layer, b)) + 1
                        sp.wait_ge(k_done, k_steps(n))
                        sp.wait_ge(v_done, v_steps(n))
                        for name, t in (("kz", kz), ("vm", vm), ("vr", vr)):
                            sp.dma_start(s[name][layer][b], t[layer][:, b, :, :].rearrange("p h k -> p (h k)")).then_inc(stored, 16)
                    if layer == 0:
                        n = max(n for n, q in enumerate(jobs) if q[0] == "fold") + 1
                        sp.wait_ge(v_done, v_steps(n))
                        sp.dma_start(s["fold"], fold[:, :, :].rearrange("p c n -> p (c n)")).then_inc(stored, 16)
                sp.wait_ge(stored, 13 * 16)

            @block.gpsimd
            def _(pool):
                pool.memset(keyz[:, :, :], 0.0).then_inc(zeroed, 1)
                for layer in range(2):
                    pool.memset(kz[layer][:, :, :, :], 0.0).then_inc(zeroed, 1)
                    pool.memset(vm[layer][:, :, :, dks[layer]:], 1.0).then_inc(zeroed, 1)
                    pool.memset(vr[layer][:, :, :, dks[layer]:], 1.0).then_inc(zeroed, 1)

            @block.tensor
            def _(pe):
                pe.wait_ge(loaded, 5 * 16)
                for n, (kind, layer, b, i) in enumerate(jobs):
                    bank = banks[n % 8]
                    if kind == "fold" and i == 0:
                        pe.wait_ge(keys_loaded, 3 * 16)
                    if layer == 1:
                        pe.wait_ge(later_loaded, 16)
                    if n >= 8:
                        before = jobs[n - 8][0]
                        if before == "k":
                            pe.wait_ge(k_done, k_steps(n - 7))
                        else:
                            pe.wait_ge(v_done, v_steps(n - 7))
                    if kind == "fold":
                        for g in range(RH):
                            last = pe.matmul(bank[:, g * P:(g + 1) * P], wqT[:, g, i * P:(i + 1) * P],
                                             keyz[:, g, :], start=True, stop=True)
                    elif kind == "k":
                        w = wkv1 if layer else wk0
                        for c in range(DC):
                            last = pe.matmul(bank[:, 0:CTX], w[:, c, i * P:(i + 1) * P], ctxT[:, b, c, :],
                                             start=c == 0, stop=c == DC - 1)
                    elif kind == "v":
                        part, m = i
                        rows = slice(0, P) if part == 0 else slice(P, CTX)
                        for c in range(DC):
                            w = wkv1[:, c, 1024 + m * 512:1024 + m * 512 + 512] if layer else wv0[:, c, :]
                            last = pe.matmul(bank[0:rows.stop - rows.start, :], ctxT[:, b, c, rows], w,
                                             start=c == 0, stop=c == DC - 1)
                    last.then_inc(made, 1)

            @block.scalar
            def _(act):
                act.wait_ge(loaded, 5 * 16)
                act.wait_ge(zeroed, 7)
                for n, (kind, layer, b, i) in enumerate(jobs):
                    if kind != "k":
                        continue
                    dk = dks[layer]
                    per = P // dk
                    act.wait_ge(made, n + 1)
                    for j in range(per):
                        rows = slice(j * dk, (j + 1) * dk)
                        bias = bk0[rows, i:i + 1] if layer == 0 else 0.0
                        last = act.activation(kz[layer][rows, b, i * per + j, :], banks[n % 8][rows, 0:CTX],
                                              ACT.Identity, bias=bias)
                        last.then_inc(k_done, 1)

            @block.vector
            def _(dve):
                dve.wait_ge(loaded, 5 * 16)
                for n, (kind, layer, b, i) in enumerate(jobs):
                    if kind == "fold":
                        dve.wait_ge(made, n + 1)
                        last = dve.tensor_copy(fold[:, i, :], banks[n % 8][:, :])
                    elif kind == "v":
                        part, m = i
                        dk = dks[layer]
                        heads = slice(m * (512 // dk), (m + 1) * (512 // dk))
                        rows = P if part == 0 else REM
                        dve.wait_ge(made, n + 1)
                        out = (vr if part else vm)[layer][0:rows, b, heads, 0:dk]
                        src = banks[n % 8][0:rows, :].rearrange("p (h d) -> p h d", d=dk)
                        if layer == 0:
                            last = dve.tensor_tensor(out, src, bv0[0:rows, :].rearrange("p (h d) -> p h d", d=dk), ALU.add)
                        else:
                            last = dve.tensor_copy(out, src)
                    else:
                        continue
                    last.then_inc(v_done, 1)


def layernorm(dve, z, nth, xin, stats, mv, std, rstd, xn):
    st = Steps(z["ln_step"], nth, TILES + 1)
    dve.wait_ge(z["x_loaded"], (nth + 1) * 16)
    for t in range(TILES):
        st.give(dve.bn_stats(stats[:, t, :], xin[:, t, :]))
    hold(dve, st.sem, st.level(), z["held"])
    for t in range(TILES):
        dve.bn_aggr(mv[:, t, :], stats[:, t, :]).then_inc(z["var_ready"], 1)
    dve.wait_ge(z["std_ready"], nth + 1)
    st.give(dve.reciprocal(rstd[:, :], std[:, :]))
    dve.wait_ge(st.sem, st.level())
    for t in range(TILES):
        dve.tensor_scalar(xn[:, t, :], xin[:, t, :], mv[:, t, 0:1], rstd[:, t:t + 1],
                          ALU.subtract, ALU.mult).then_inc(z["xn_ready"], 1)
    st.end()


def deviations(act, z, nth, std, mv, eps):
    act.wait_ge(z["var_ready"], (nth + 1) * TILES)
    act.activation(std[:, :], mv[:, :, 1], ACT.Sqrt, bias=eps[:, :]).then_inc(z["std_ready"], 1)


def split_product(pe, out, lhsT, rhs, start, stop):
    for k, (x, y) in enumerate(((0, 0), (0, 1), (1, 0))):
        last = pe.matmul(out, lhsT(x), rhs(y), start=start and k == 0, stop=stop and k == 2)
    return last


def butterfly_stage(pool, y, w, s, t, done, base, held):
    st = 2 ** s
    rows = y.shape[0]
    v = y.rearrange("p (n two s) -> p n two s", two=2, s=st)
    both = lambda tile, k: tile[0:rows, k:k + 2, :].rearrange("p two (n s) -> p n two s", s=st)
    one = lambda k: t[0:rows, k, :].rearrange("p (n s) -> p n s", s=st)
    pool.tensor_tensor(both(t, 0), v, both(w, 0), ALU.mult).then_inc(done, 1)
    pool.tensor_tensor(both(t, 2), v, both(w, 2), ALU.mult).then_inc(done, 1)
    hold(pool, done, base + 2, held)
    pool.tensor_tensor(v[:, :, 0, :], one(0), one(3), ALU.add).then_inc(done, 1)
    pool.tensor_tensor(v[:, :, 1, :], one(1), one(2), ALU.add).then_inc(done, 1)
    hold(pool, done, base + 4, held)


def attention(nc, a, s, layer, x_in, x_out):
    dk = (32, 64)[layer]
    FT = HEADS * dk // P
    CG = FT // GROUPS
    VW = dk + 1
    pre = f"at{layer}"
    U_XT, U_Q = 0, DC
    U_PV = U_Q + FT
    U_OT = U_PV + UNITS
    U_R = U_OT + FT
    U_OUT = U_R + (DC if layer else 0)
    USES = U_OUT + TILES
    with ExitStack() as ctx:
        sem = make_sem(nc, s["sems"], pre)
        sb = lambda name, shape, dt=F32: ctx.enter_context(nc.sbuf_tensor(f"{pre}_{name}", shape, dt))
        ident = sb("ident", [P, P])
        eps = sb("eps", [P, 1])
        if layer:
            wq = sb("wq", [P, DC, HEADS * dk])
            wo = sb("wo", [P, FT, D])
            xnT = sb("xnT", [P, DC, BLOCK])
        else:
            wq_s, wo_s = (sb(n, [P, 2, DC, D], F32R) for n in ("wq_s", "wo_s"))
            xnT_s = sb("xnT_s", [P, 2, DC, BLOCK], F32R)
            oT_s = xnT_s
        xin = sb("xin", [P, TILES, D])
        xres = sb("xres", [P, TILES, D])
        xn = sb("xn", [P, TILES, D])
        qT = sb("qT", [P, FT, BLOCK])
        kz = sb("kz", [P, HEADS, CTX])
        vm = sb("vm", [P, HEADS, VW])
        vr = sb("vr", [GH * REM, GROUPS, GH, VW])
        probs = [sb(f"probs{i}", [P, GH, CTX]) for i in range(4)]
        tails = [sb(f"tails{i}", [P, GH * REM]) for i in range(4)]
        ptS = [sb(f"ptS{i}", [P, GH + 1, P]) for i in range(2)]
        o = sb("o", [P, TILES, HEADS, dk])
        if layer:
            oT = qT
        else:
            wq, wo = o[:, :, :, :].rearrange("p t h k -> p t (h k)"), xres
        stats, mv = sb("stats", [P, TILES, 6]), sb("mv", [P, TILES, 2])
        std, rstd = sb("std", [P, TILES]), sb("rstd", [P, TILES])
        mx, rz = sb("mx", [P, 2, GH]), sb("rz", [P, 2, GH])
        if layer:
            w2 = sb("w2", [P, DC, D])
            rT = xnT
            row = sb("gamma", [P, D])
            y = sb("y", [P, D])
            bst, bmv = sb("bst", [P, TILES, 6]), sb("bmv", [P, TILES, 2])
            bstd, brstd = sb("bstd", [P, TILES]), sb("brstd", [P, TILES])
        else:
            bq = sb("bq", [P, FT])
            bqs = sb("bqs", [P, FT])
            row = sb("bo", [P, D])
        bw = [sb(f"bw{i}", [P, 4, 1024]) for i in range(2 - layer)]
        bt = sb("bt", [P, 4, 1024])
        by = sb("by", [P, DC, F])
        bias_row, up_row = by[0:1, 0, :], by[0:1, 1, :]

        ps = lambda name, shape: ctx.enter_context(nc.psum_tensor(f"{pre}_{name}", shape, F32))
        score = Ring(sem, "score", [ps(f"score{i}", [P, 2, 512]) for i in range(2)], UNITS)
        pt = Ring(sem, "pt", [ps("pt", [P, 2, 512])], UNITS, drains=2)
        acc = Ring(sem, "acc", [ps(f"acc{i}", [P, 512]) for i in range(2)], USES, start=1)

        z = Named(sem)
        z["held"] = s["held"]

        with nc.Block() as block:
            @block.sync
            def _(sp):
                sp.dma_start(xin[:, :, :], x_in[0].rearrange("p t d -> p (t d)")).then_inc(z["x_loaded"], 16)
                sp.dma_start(row[:, :], a["gamma" if layer else "bo0"].partition_broadcast(P)).then_inc(z["w_loaded"], 16)
                if not layer:
                    sp.dma_start(bq[:, :], a["bq0"]).then_inc(z["w_loaded"], 16)
                sp.dma_start(wq[:, :, :], a[f"wq{layer}"].rearrange("(c p) n -> p c n", p=P)).then_inc(z["w_loaded"], 16)
                if not layer:
                    sp.dma_start(wo[:, :, :], a["wo0"].rearrange("(c p) n -> p c n", p=P)).then_inc(z["wo_loaded"], 16)
                sp.wait_ge(z["vr_zeroed"], 1)

                def load_kv(b):
                    sp.dma_start(kz[:, :, :], s["kz"][layer][b].rearrange("a p n -> (a p) n")).then_inc(z["kv_loaded"], 16)
                    sp.dma_start(vm[:, :, :], s["vm"][layer][b].rearrange("a p n -> (a p) n")).then_inc(z["kv_loaded"], 16)
                    src = s["vr"][layer][b].rearrange("a p (g j v) -> (a p) g j v", g=GROUPS, j=GH)
                    for j in range(GH):
                        sp.dma_start(vr[REM * j:REM * (j + 1), :, j, :], src[:, :, j, :]).then_inc(z["kv_loaded"], 16)

                load_kv(slice(0, 1))
                if layer:
                    sp.dma_start(wo[:, :, :], a["wo1"].rearrange("(c p) n -> p c n", p=P)).then_inc(z["wo_loaded"], 16)
                    sp.dma_start(w2[:, :, :], a["w2"].rearrange("(c p) n -> p c n", p=P)).then_inc(z["wo_loaded"], 16)

                def block_io(it, more):
                    sp.wait_ge(z["xn_ready"], (it + 1) * TILES)
                    nxt = bass.ds(it + 1, 1) if more else slice(it, it + 1)
                    sp.dma_start(xin[:, :, :], x_in[nxt].rearrange("a p t d -> (a p) (t d)")).then_inc(z["x_loaded"], 16)
                    if not isinstance(it, int) or it:
                        sp.wait_ge(z["stored"], it * 16)
                    elif not layer:
                        sp.wait_ge(z["w_low"], 2)
                    sp.dma_start(xres[:, :, :], x_in[bass.ds(it, 1)].rearrange("a p t d -> (a p) (t d)")).then_inc(z["res_loaded"], 16)
                    if more:
                        sp.wait_ge(acc.free(U_OT - 1), acc.emptied_by(it, U_OT - 1))
                        load_kv(bass.ds((it + 1) // (BLOCKS // BATCH), 1))
                    if layer:
                        sp.wait_ge(z["out_ready"], (it + 1) * TILES)
                    else:
                        for n in (USES - 2, USES - 1):
                            sp.wait_ge(acc.free(n), acc.emptied_by(it, n))
                    sp.dma_start(x_out[bass.ds(it, 1)].rearrange("a p t d -> (a p) (t d)"), xres[:, :, :]).then_inc(z["stored"], 16)

                block_io(0, True)
                with sp.Fori(1, BLOCKS - 1) as it:
                    block_io(it, True)
                block_io(BLOCKS - 1, False)
                sp.wait_ge(z["stored"], BLOCKS * 16)
                sp.wait_ge(z["x_loaded"], (BLOCKS + 1) * 16)

            @block.tensor
            def _(pe):
                pe.wait_ge(z["id_step"], 2)
                with pe.Fori(0, BLOCKS) as it:
                    def take(n):
                        pe.wait_ge(acc.free(n), acc.emptyings(it, n))
                        return acc.buf(n)

                    def made(n):
                        for m in (n - 1, n):
                            pe.wait_ge(acc.free(m), acc.emptied_by(it, m))

                    pe.wait_ge(z["xn_ready"], (it + 1) * TILES)
                    for c in range(DC):
                        bank = take(U_XT + c)
                        for t in range(TILES):
                            last = pe.transpose(bank[:, t * P:(t + 1) * P], xn[:, t, c * P:(c + 1) * P], ident[:, :])
                        last.then_inc(acc.full(U_XT + c), 1)
                    made(U_Q - 1)
                    if layer:
                        pe.wait_ge(z["w_loaded"], 32)
                    else:
                        pe.wait_ge(z["w_low"], 2)
                    for f in range(FT):
                        bank = take(U_Q + f)
                        for c in range(DC):
                            if layer:
                                last = pe.matmul(bank[:, :], wq[:, c, f * P:(f + 1) * P], xnT[:, c, :],
                                                 start=c == 0, stop=c == DC - 1)
                            else:
                                last = split_product(pe, bank[:, :], lambda x: wq_s[:, x, c, f * P:(f + 1) * P],
                                                     lambda y: xnT_s[:, y, c, :], c == 0, c == DC - 1)
                        last.then_inc(acc.full(U_Q + f), 1)
                    made(U_PV - 1)
                    pe.wait_ge(z["kv_loaded"], (it + 1) * 16 * (2 + GH))

                    def scores(u):
                        t, g = divmod(u, GROUPS)
                        if u >= 2:
                            pe.wait_ge(score.free(u), score.emptyings(it, u))
                        for half in range(2):
                            f = g * CG + half * (CG - 1)
                            h = g * GH + 2 * half
                            last = pe.matmul(score.buf(u)[:, half, 0:2 * CTX], qT[:, f, t * P:(t + 1) * P],
                                             kz[:, h:h + 2, :], start=True, stop=True)
                        last.then_inc(score.full(u), 1)

                    def turn(u):
                        pe.wait_ge(z["exp_done"], (it * UNITS + u + 1) * 2)
                        if u >= 1:
                            pe.wait_ge(pt.free(u), pt.emptyings(it, u))
                        p = probs[u % 4]
                        for j in range(GH):
                            pe.transpose(pt.buf(u)[:, 0, j * P:(j + 1) * P], p[:, j, 0:P], ident[:, :])
                        pe.transpose(pt.buf(u)[0:GH * REM, 1, 0:P], tails[u % 4][:, :], ident[:, :]).then_inc(pt.full(u), 1)

                    def weigh(u):
                        g = u % GROUPS
                        pe.wait_ge(pt.free(u), pt.emptied_by(it, u))
                        bank = take(U_PV + u)
                        pT = ptS[u % 2]
                        pe.matmul(bank[:, 0:GH * VW], pT[0:GH * REM, GH, :], vr[:, g, :, :], start=True, stop=False)
                        for j in range(GH):
                            last = pe.matmul(bank[:, j * VW:(j + 1) * VW], pT[:, j, :], vm[:, g * GH + j, :],
                                             start=False, stop=j == GH - 1)
                        last.then_inc(acc.full(U_PV + u), 1)

                    for u in range(UNITS + 3):
                        if u < UNITS:
                            scores(u)
                        if 2 <= u < UNITS + 2:
                            turn(u - 2)
                        if u >= 3:
                            weigh(u - 3)
                    made(U_OT - 1)
                    hc = P // dk
                    for c in range(FT):
                        bank = take(U_OT + c)
                        for t in range(TILES):
                            last = pe.transpose(bank[:, t * P:(t + 1) * P], o[:, t, c * hc:(c + 1) * hc, :], ident[:, :])
                        last.then_inc(acc.full(U_OT + c), 1)
                    made(U_R - 1)
                    if layer:
                        pe.wait_ge(z["wo_loaded"], 32)
                        for f in range(DC):
                            bank = take(U_R + f)
                            for c in range(FT):
                                last = pe.matmul(bank[:, :], wo[:, c, f * P:(f + 1) * P], oT[:, c, :],
                                                 start=c == 0, stop=c == FT - 1)
                            last.then_inc(acc.full(U_R + f), 1)
                        made(U_OUT - 1)
                    for t in range(TILES):
                        bank = take(U_OUT + t)
                        for c in range(DC):
                            if layer:
                                last = pe.matmul(bank[:, :], rT[:, c, t * P:(t + 1) * P], w2[:, c, :],
                                                 start=c == 0, stop=c == DC - 1)
                            else:
                                last = split_product(pe, bank[:, :], lambda x: oT_s[:, x, c, t * P:(t + 1) * P],
                                                     lambda y: wo_s[:, y, c, :], c == 0, c == DC - 1)
                        last.then_inc(acc.full(U_OUT + t), 1)

            @block.scalar
            def _(act):
                act.wait_ge(z["eps_done"], 1)
                scale = float(dk) ** -0.5
                deviations(act, z, 0, std, mv, eps)
                if not layer:
                    act.wait_ge(z["w_loaded"], 48)
                    act.mul(bqs[:, :], bq[:, :], scale).then_inc(z["bqs_done"], 1)
                    act.copy(wq_s[:, 0, :, :], wq).then_inc(z["w_high"], 1)
                    act.wait_ge(z["wo_loaded"], 16)
                    act.copy(wo_s[:, 0, :, :], wo[:, :, :]).then_inc(z["w_high"], 1)
                    act.wait_ge(z["bqs_done"], 1)
                with act.Fori(0, BLOCKS) as it:

                    def drain(n, out, func=ACT.Copy, **kw):
                        act.wait_ge(acc.full(n), acc.fillings(it, n))
                        act.activation(out, acc.buf(n)[:, :], func, **kw).then_inc(acc.free(n), 1)

                    def high(n, out, k):
                        act.wait_ge(acc.full(n), acc.fillings(it, n))
                        act.copy(out[:, 0, k % DC, :], acc.buf(n)[:, :]).then_inc(z["high"], 1)

                    for c in range(DC):
                        if layer:
                            drain(U_XT + c, xnT[:, c, :])
                        else:
                            high(U_XT + c, xnT_s, c)
                    for f in range(FT):
                        kw = {"bias": bqs[:, f:f + 1]} if not layer else {}
                        drain(U_Q + f, qT[:, f, :], ACT.Identity, scale=scale, **kw)
                    for u in range(UNITS + 2):
                        if u >= 2:
                            n = u - 2
                            act.wait_ge(pt.full(n), pt.fillings(it, n))
                            act.copy(ptS[n % 2][:, 0:GH, :], pt.buf(n)[:, 0, :].rearrange("p (j k) -> p j k", j=GH)).then_inc(pt.free(n), 1)
                            act.copy(ptS[n % 2][0:GH * REM, GH, :], pt.buf(n)[0:GH * REM, 1, 0:P]).then_inc(pt.free(n), 1)
                        if u < UNITS:
                            act.wait_ge(score.free(u), score.emptied_by(it, u))
                            p = probs[u % 4]
                            act.activation(p[:, :, 0:P], p[:, :, 0:P], ACT.Exp).then_inc(z["exp_done"], 1)
                            act.activation(tails[u % 4][:, :].rearrange("p (j k) -> p j k", j=GH), p[:, :, P:CTX],
                                           ACT.Exp).then_inc(z["exp_done"], 1)
                    for c in range(FT):
                        if layer:
                            drain(U_OT + c, oT[:, c, :])
                        else:
                            high(U_OT + c, oT_s, DC + c)
                    deviations(act, z, it + 1, std, mv, eps)
                    if layer:
                        for f in range(DC):
                            drain(U_R + f, rT[:, f, :], ACT.Relu)
                        for t in range(TILES):
                            act.wait_ge(z["y_var"], it * TILES + t + 1)
                            act.activation(bstd[:, t:t + 1], bmv[:, t, 1:2], ACT.Sqrt, bias=eps[:, :]).then_inc(z["y_std"], 1)

            @block.vector
            def _(dve):
                dve.memset(eps[:, :], EPS).then_inc(z["eps_done"], 1)
                dve.memset(vr[:, :, :, :], 0.0).then_inc(z["vr_zeroed"], 1)
                for n in range(2):
                    dve.sem_inc(acc.free(n), 1)
                layernorm(dve, z, 0, xin, stats, mv, std, rstd, xn)
                if not layer:
                    for k, (w, w_s) in enumerate(((wq, wq_s), (wo, wo_s))):
                        dve.wait_ge(z["w_high"], k + 1)
                        dve.tensor_tensor(w_s[:, 1, :, :], w[:, :, :], w_s[:, 0, :, :].bitcast(F32),
                                          ALU.subtract).then_inc(z["w_low"], 1)
                with dve.Fori(0, BLOCKS) as it:
                    st = Steps(z["dve_step"], it, DVE_STEPS[layer])

                    def low(n, out, k):
                        dve.wait_ge(z["high"], it * 2 * DC + k + 1)
                        dve.tensor_tensor(out[:, 1, k % DC, :], acc.buf(n)[:, :], out[:, 0, k % DC, :].bitcast(F32),
                                          ALU.subtract).then_inc(acc.free(n), 1)

                    if not layer:
                        for c in range(DC):
                            low(U_XT + c, xnT_s, c)
                    dve.wait_ge(z["w_loaded"], 48 - 16 * layer)
                    dve.wait_ge(z["res_loaded"], (it + 1) * 16)

                    def shift(u):
                        m = mx[:, u % 2, :]
                        sc = score.buf(u)[:, :, 0:2 * CTX]
                        dve.wait_ge(score.full(u), score.fillings(it, u))
                        st.give(dve.tensor_reduce(m.rearrange("p (a b) -> p a b", a=2),
                                                  sc.rearrange("p a (b k) -> p a b k", b=2), AX.X, ALU.max))
                        dve.wait_ge(st.sem, st.level())
                        out = probs[u % 4][:, :, :].rearrange("p (a b) k -> p a b k", a=2)
                        top = m.rearrange("p (a b) -> p a b", a=2).unsqueeze(3).broadcast_to([P, 2, 2, CTX])
                        dve.tensor_tensor(out, sc.rearrange("p a (b k) -> p a b k", b=2), top,
                                          ALU.subtract).then_inc(score.free(u), 1)

                    def normalise(u):
                        t, g = divmod(u, GROUPS)
                        n = U_PV + u
                        v = acc.buf(n)[:, 0:GH * VW].rearrange("p (j v) -> p j v", v=VW)
                        dve.wait_ge(acc.full(n), acc.fillings(it, n))
                        st.give(dve.reciprocal(rz[:, u % 2, :].unsqueeze(2), v[:, :, dk:VW]))
                        dve.wait_ge(st.sem, st.level())
                        dve.tensor_tensor(o[:, t, g * GH:(g + 1) * GH, :], v[:, :, 0:dk],
                                          rz[:, u % 2, :].unsqueeze(2).broadcast_to([P, GH, dk]), ALU.mult).then_inc(acc.free(n), 1)

                    for u in range(UNITS + 3):
                        if u < UNITS:
                            shift(u)
                        if u >= 3:
                            normalise(u - 3)
                    if not layer:
                        for c in range(DC):
                            low(U_OT + c, oT_s, DC + c)
                    if layer:
                        layernorm(dve, z, it + 1, xin, stats, mv, std, rstd, xn)
                    else:
                        for t in range(TILES):
                            st.give(dve.tensor_tensor(xres[:, t, :], xres[:, t, :], row[:, :], ALU.add))
                        dve.wait_ge(st.sem, st.level())
                    for t in range(TILES):
                        n = U_OUT + t
                        bank = acc.buf(n)
                        dve.wait_ge(acc.full(n), acc.fillings(it, n))
                        if not layer:
                            dve.tensor_tensor(xres[:, t, :], bank[:, :], xres[:, t, :], ALU.add).then_inc(acc.free(n), 1)
                            if t == 1:
                                layernorm(dve, z, it + 1, xin, stats, mv, std, rstd, xn)
                            continue
                        st.give(dve.bn_stats(bst[:, t, :], bank[:, :]))
                        hold(dve, st.sem, st.level(), z["held"])
                        dve.bn_aggr(bmv[:, t, :], bst[:, t, :]).then_inc(z["y_var"], 1)
                        dve.wait_ge(z["y_std"], it * TILES + t + 1)
                        st.give(dve.reciprocal(brstd[:, t:t + 1], bstd[:, t:t + 1]))
                        dve.wait_ge(st.sem, st.level())
                        yt = y[:, :]
                        dve.tensor_scalar(yt, bank[:, :], bmv[:, t, 0:1], brstd[:, t:t + 1], ALU.subtract,
                                          ALU.mult).then_inc(acc.free(n), 1)
                        dve.wait_ge(acc.free(n), acc.emptied_by(it, n))
                        st.give(dve.tensor_tensor(yt, yt, row[:, :], ALU.mult))
                        dve.wait_ge(st.sem, st.level())
                        dve.tensor_tensor(xres[:, t, :], xres[:, t, :], yt, ALU.add).then_inc(z["out_ready"], 1)
                    st.end()

            @block.gpsimd
            def _(pool):
                make_identity(pool, ident, z["id_step"])
                weights = a["down_w"] if layer else a["up_w"]
                moved = 0

                def move(out, src):
                    nonlocal moved
                    pool.dma_start(out, src).then_inc(z["bf_moved"], 16)
                    moved += 16

                def arrived():
                    pool.wait_ge(z["bf_moved"], moved)

                source = a["W_conT" if layer else "W_exp"].rearrange("(c p) n -> c p n", p=P)
                result = s["wcon" if layer else "wexp"].rearrange("p (c n) -> c p n", c=DC)
                strides = range(STAGES)[::-1] if layer else range(STAGES - 1)
                last_stage = len(strides) - 1
                load = lambda k: move(bw[k % len(bw)][:, :, :], weights[strides[k]].partition_broadcast(P))
                steps = 0

                def stage(k, c, before):
                    butterfly_stage(pool, by[:, bass.ds(c, 1), :].rearrange("p a n -> p (a n)"), bw[k % len(bw)], strides[k],
                                    bt, z["bf_step"], before, z["held"])

                load(0)
                move(by[:, 0, :], source[0])
                arrived()
                for c in range(DC):
                    if c + 1 < DC:
                        move(by[:, c + 1, :], source[c + 1])
                    stage(0, c, steps)
                    steps += 4
                    arrived()
                for k in range(1, last_stage):
                    if k == 1 or layer:
                        load(k)
                    arrived()
                    if not layer:
                        load(k + 1)
                    with pool.Fori(0, DC) as c:
                        stage(k, c, c * 4 + steps)
                    steps += 4 * DC
                if layer:
                    load(last_stage)
                arrived()
                for c in range(DC):
                    stage(last_stage, c, steps)
                    steps += 4
                    move(result[c], by[:, c, :])
                arrived()
                if layer:
                    up_source = s["wexp"].rearrange("p (c n) -> c p n", c=DC)
                    move(bw[0][:, :, :], a["up_w"][STAGES - 1].partition_broadcast(P))
                    for c in range(DC):
                        move(by[:, c, :], up_source[c])
                    arrived()
                    for c in range(DC):
                        butterfly_stage(pool, by[:, c, :], bw[0], STAGES - 1, bt, z["bf_step"], steps, z["held"])
                        steps += 4
                        move(up_source[c], by[:, c, :])
                    arrived()
                    move(bias_row, a["b_exp"])
                    move(up_row, a["up_bias"])
                    load_row = lambda k: move(bw[k % len(bw)][0:1, :, :], a["up_w"][k].unsqueeze(0))
                    for k in range(STAGES):
                        load_row(k)
                        arrived()
                        butterfly_stage(pool, bias_row, bw[k % len(bw)], k, bt, z["bf_step"], steps, z["held"])
                        steps += 4
                    pool.tensor_tensor(bias_row, bias_row, up_row, ALU.add).then_inc(z["bf_step"], 1)
                    pool.wait_ge(z["bf_step"], steps + 1)
                    move(s["bexp"], bias_row)
                    arrived()


DVE_STEPS = (36, 44)


def ffn0(nc, a, s, x_in, x_out):
    pre = "ff0"
    SPREADS = RH * TILES
    PARTS = 4
    ROWS = XROWS // PARTS
    JOBS = PARTS * SPREADS
    job = lambda m: (m // SPREADS, m % SPREADS // RH, m % RH)
    pool_reaches = lambda m: m >= SPREADS and m % 2 == 1
    pool_made = lambda m: m + sum(pool_reaches(q) for q in range(m))
    LAG = 2
    LN_AT = 12
    W_USES = DC + TILES + 2 * FI + 2 * FI
    U_XT, U_SIM, U_GU, U_ST = 0, DC, DC + TILES, DC + TILES + 2 * FI
    with ExitStack() as ctx:
        sem = make_sem(nc, s["sems"], pre)
        sb = lambda name, shape, dt=F32: ctx.enter_context(nc.sbuf_tensor(f"{pre}_{name}", shape, dt))
        ident = sb("ident", [P, P])
        eps = sb("eps", [P, 1])
        fold = sb("fold", [P, DC, D])
        bg, bu, bd = sb("bg", [P, FI]), sb("bu", [P, FI]), sb("bd", [P, D])
        xin, xres, xn = (sb(n, [P, TILES, D]) for n in ("xin", "xres", "xn"))
        xnT = sb("xnT", [P, DC, BLOCK])
        xnT_s = sb("xnT_s", [P, 2, DC, BLOCK], F32R)
        gu_s = [sb(f"gu_s{i}", [P, 2, 2, DC, P], F32R) for i in range(3)]
        wd_s = [sb(f"wd_s{i}", [P, 2, D], F32R) for i in range(2)]
        hid_s = [sb(f"hid_s{i}", [P, 2, BLOCK], F32R) for i in range(3)]
        stats, mv = sb("stats", [P, TILES, 6]), sb("mv", [P, TILES, 2])
        std, rstd = sb("std", [P, TILES]), sb("rstd", [P, TILES])
        sim = xn[:, :, :].rearrange("p t (g k) -> p t g k", k=KEYS)
        G = sb("G", [P, TILES, NEXP])
        best = sb("best", [P, 1, 2 * RH, TOPK])
        place = sb("place", [P, 1, 2 * RH, TOPK], U32)
        placef = sb("placef", [P, 1, 2 * RH, TOPK], BF16)
        pair = sb("pair", [P, 1, RH, TOPK, TOPK])
        best2 = sb("best2", [P, 1, RH, TOPK])
        picked = sb("picked", [P, 1, RH, TOPK, TOPK])
        count = sb("count", [P, 1, RH, TOPK], BF16)
        ex = sb("ex", [P, TILES, 2 * RH, KEYS])
        ebest = sb("ebest", [P, 1, 2 * RH, TOPK])
        rows_w = sb("rows_w", [P, 1, RH, TOPK])
        norm = sb("norm", [P, 1, 2, RH])
        beyond = sb("beyond", [P, 1, RH, TOPK])
        beyond_w = sb("beyond_w", [P, TILES, 1])
        exn = sb("exn", [P, TILES, RH, XROWS])
        hot = sb("hot", [P, RH, KEYS, TOPK], BF16)
        cx = sb("cx", [P, TILES, RH, XROWS], BF16)
        qy = sb("qy", [P, TILES, RH, KEYS], BF16)
        index = sb("index", [P, KEYS], BF16)
        falling = sb("falling", [P, TOPK], BF16)
        ps = lambda name: ctx.enter_context(nc.psum_tensor(f"{pre}_{name}", [P, 512], F32))
        work = Ring(sem, "work", [ps(f"work{i}") for i in range(4)], W_USES)
        MOVED = U_GU // 4
        accs = [ps(f"acc{i}") for i in range(TILES)]
        gu_w = Ring(sem, "gu_w", [sb(f"gu_w{i}", [P, 2, DC, P]) for i in range(4)], 2 * FI, parts=32)
        wd_w = Ring(sem, "wd_w", [sb(f"wd_w{i}", [P, D]) for i in range(2)], FI, parts=16)
        silu = Ring(sem, "silu", [sb(f"silu{i}", [P, BLOCK]) for i in range(2)], 2 * FI)
        hid = Ring(sem, "hid", [sb(f"hid{i}", [P, BLOCK]) for i in range(2)], 2 * FI)
        reach = [sb(f"reach{i}", [P, ROWS, KEYS], BF16) for i in range(4)]
        outer = [sb(f"outer{i}", [P, ROWS, KEYS]) for i in range(8)]
        wide = lambda v: v.unsqueeze(2).broadcast_to([P, ROWS, KEYS])
        flat = lambda v: v.unsqueeze(1).broadcast_to([P, ROWS, KEYS])
        z = Named(sem)
        z["held"] = s["held"]

        with nc.Block() as block:
            @block.sync
            def _(sp):
                sp.dma_start(xin[:, :, :], x_in[0].rearrange("p t d -> p (t d)")).then_inc(z["x_loaded"], 16)
                sp.dma_start(fold[:, :, :], s["fold"].rearrange("p (c n) -> p c n", c=DC)).then_inc(z["w_loaded"], 16)
                for t, name in ((bg, "bg"), (bu, "bu")):
                    sp.dma_start(t[:, :], a[name]).then_inc(z["w_loaded"], 16)
                sp.dma_start(bd[:, :], a["bd"].partition_broadcast(P)).then_inc(z["w_loaded"], 16)

                def load_gu(it, n):
                    if n >= 4 or not isinstance(it, int) or it:
                        sp.wait_ge(gu_w.free(n), gu_w.emptyings(it, n))
                    w = gu_w.buf(n)
                    if n < FI:
                        for k, name in enumerate(("Wg", "Wu")):
                            sp.dma_start(w[:, k, :, :], a[name][n]).then_inc(gu_w.full(n), 16)
                    else:
                        sp.dma_start(w[:, 0, :, :], a["downT"][n - FI]).then_inc(gu_w.full(n), 16)
                        sp.dma_start(w[:, 1, :, :].rearrange("p c n -> p (c n)"), a["up"][n - FI]).then_inc(gu_w.full(n), 16)

                def load_wd(it, i):
                    if i >= 2 or not isinstance(it, int) or it:
                        sp.wait_ge(wd_w.free(i), wd_w.emptyings(it, i))
                    sp.dma_start(wd_w.buf(i)[:, :], a["Wd"][i]).then_inc(wd_w.full(i), 16)

                def load_first(it):
                    for i in range(4):
                        load_gu(it, i)
                    for i in range(2):
                        load_wd(it, i)

                def block_io(it, more):
                    sp.wait_ge(z["xn_ready"], (it + 1) * TILES)
                    nxt = bass.ds(it + 1, 1) if more else slice(it, it + 1)
                    sp.dma_start(xin[:, :, :], x_in[nxt].rearrange("a p t d -> (a p) (t d)")).then_inc(z["x_loaded"], 16)
                    if not isinstance(it, int) or it:
                        sp.wait_ge(z["stored"], it * 16)
                    sp.dma_start(xres[:, :, :], x_in[bass.ds(it, 1)].rearrange("a p t d -> (a p) (t d)")).then_inc(z["res_loaded"], 16)
                    for i in range(2, FI):
                        load_gu(it, i + 2)
                        load_wd(it, i)
                    for n in range(FI + 2, 2 * FI):
                        load_gu(it, n)
                    if more:
                        load_first(it + 1)
                    sp.wait_ge(z["out_ready"], (it + 1) * TILES)
                    sp.dma_start(x_out[bass.ds(it, 1)].rearrange("a p t d -> (a p) (t d)"), xres[:, :, :]).then_inc(z["stored"], 16)

                load_first(0)
                block_io(0, True)
                with sp.Fori(1, BLOCKS - 1) as it:
                    block_io(it, True)
                block_io(BLOCKS - 1, False)
                sp.wait_ge(z["stored"], BLOCKS * 16)
                sp.wait_ge(z["x_loaded"], (BLOCKS + 1) * 16)

            @block.tensor
            def _(pe):
                pe.wait_ge(z["id_step"], 2)
                with pe.Fori(0, BLOCKS) as it:
                    def take(n):
                        k = (n - U_GU) // 2 - 2
                        reader = hid if n % 2 else silu
                        if n < DC:
                            pass
                        elif k < 0:
                            pe.wait_ge(work.free(n), it * MOVED + (1 if n < U_GU else MOVED))
                        else:
                            pe.wait_ge(reader.full(k), reader.fillings(it, k))
                        return work.buf(n)

                    pe.wait_ge(z["xn_ready"], (it + 1) * TILES)
                    for c in range(DC):
                        bank = take(U_XT + c)
                        for t in range(TILES):
                            last = pe.transpose(bank[:, t * P:(t + 1) * P], xn[:, t, c * P:(c + 1) * P], ident[:, :])
                        last.then_inc(work.full(U_XT + c), 1)
                    pe.wait_ge(z["w_loaded"], 4 * 16)
                    for n in range(U_XT, U_SIM):
                        pe.wait_ge(work.free(n), it * MOVED + 1)
                    for t in range(TILES):
                        bank = take(U_SIM + t)
                        for c in range(DC):
                            last = pe.matmul(bank[:, :], xnT[:, c, t * P:(t + 1) * P], fold[:, c, :],
                                             start=c == 0, stop=c == DC - 1)
                        last.then_inc(work.full(U_SIM + t), 1)

                    def product(n, w):
                        bank = take(n)
                        for c in range(DC):
                            last = pe.matmul(bank[:, :], w(c), xnT[:, c, :], start=c == 0, stop=c == DC - 1)
                        last.then_inc(work.full(n), 1)

                    pe.wait_ge(z["x_low"], (it + 1) * DC)
                    for i in range(FI + LAG):
                        if i < FI:
                            pe.wait_ge(gu_w.free(i), gu_w.emptied_by(it, i))
                            for k in range(2):
                                n = U_GU + 2 * i + k
                                bank = take(n)
                                for c in range(DC):
                                    last = split_product(pe, bank[:, :], lambda x: gu_s[i % 3][:, x, k, c, :],
                                                         lambda y: xnT_s[:, y, c, :], c == 0, c == DC - 1)
                                last.then_inc(work.full(n), 1)
                        if i >= LAG:
                            k = i - LAG
                            pe.wait_ge(wd_w.free(k), wd_w.emptied_by(it, k))
                            pe.wait_ge(z["hid_ready"], it * FI + k + 1)
                            for t in range(TILES):
                                last = split_product(pe, accs[t][:, :], lambda x: hid_s[k % 3][:, x, t * P:(t + 1) * P],
                                                     lambda y: wd_s[k % 2][:, y, :], k == 0, False)
                            last.then_inc(z["spent"], 1)
                    def down(i):
                        pe.wait_ge(gu_w.full(FI + i), gu_w.fillings(it, FI + i))
                        product(U_ST + 2 * i, lambda c: gu_w.buf(FI + i)[:, 0, c, :])

                    down(0)
                    for i in range(FI + 1):
                        if i + 1 < FI:
                            down(i + 1)
                        if i < FI:
                            if i == FI - FI // PARTS:
                                pe.wait_ge(z["G_ready"], (it + 1) * TILES)
                            elif i % (FI // PARTS) == 0:
                                pe.wait_ge(z["spread"], it * JOBS + (i * PARTS // FI + 1) * SPREADS)
                            bank = take(U_ST + 2 * i + 1)
                            for t in range(TILES):
                                last = pe.transpose(bank[:, t * P:(t + 1) * P], G[:, t, i * P:(i + 1) * P], ident[:, :])
                            last.then_inc(work.full(U_ST + 2 * i + 1), 1)
                        if i:
                            k = FI + i - 1
                            pe.wait_ge(hid.full(k), hid.fillings(it, k))
                            for t in range(TILES):
                                last = pe.matmul(accs[t][:, :], hid.buf(k)[:, t * P:(t + 1) * P],
                                                 gu_w.buf(k)[:, 1, :, :], start=False, stop=k == 2 * FI - 1)
                            last.then_inc(gu_w.free(k), 1)

            @block.scalar
            def _(act):
                act.wait_ge(z["eps_done"], 1)
                deviations(act, z, 0, std, mv, eps)
                act.wait_ge(z["w_loaded"], 4 * 16)
                with act.Fori(0, BLOCKS) as it:
                    def high_gu(i):
                        act.wait_ge(gu_w.full(i), gu_w.fillings(it, i))
                        if i >= 3:
                            n = U_GU + 2 * (i - 3) + 1
                            act.wait_ge(work.full(n), work.fillings(it, n))
                        act.copy(gu_s[i % 3][:, 0, :, :, :], gu_w.buf(i)[:, :, :, :]).then_inc(z["gu_high"], 1)

                    def high_wd(i):
                        act.wait_ge(wd_w.full(i), wd_w.fillings(it, i))
                        if i >= 2:
                            act.wait_ge(z["spent"], it * FI + i - 1)
                        act.copy(wd_s[i % 2][:, 0, :], wd_w.buf(i)[:, :]).then_inc(z["wd_high"], 1)

                    def high_hid(i):
                        act.wait_ge(hid.full(i), hid.fillings(it, i))
                        if i >= 3:
                            act.wait_ge(z["spent"], it * FI + i - 2)
                        act.copy(hid_s[i % 3][:, 0, :], hid.buf(i)[:, :]).then_inc(z["hid_high"], 1)

                    for c in range(DC):
                        act.wait_ge(work.full(c), work.fillings(it, c))
                        act.copy(xnT[:, c, :], work.buf(c)[:, :]).then_inc(work.free(c), 1)
                    for c in range(DC):
                        act.wait_ge(work.free(c), it * MOVED + 1)
                        act.copy(xnT_s[:, 0, c, :], xnT[:, c, :]).then_inc(z["x_high"], 1)
                    for i in range(2):
                        high_gu(i)
                        high_wd(i)
                    for t in range(TILES):
                        n = U_SIM + t
                        act.wait_ge(work.full(n), work.fillings(it, n))
                        act.copy(sim[:, t, :, :], work.buf(n)[:, :].rearrange("p (g k) -> p g k", k=KEYS)).then_inc(work.free(n), 1)

                    def silu_of(n, k, bias):
                        act.wait_ge(work.full(n), work.fillings(it, n))
                        if k >= 2:
                            act.wait_ge(hid.full(k - 2), hid.fillings(it, k - 2))
                        act.activation(silu.buf(k)[:, :], work.buf(n)[:, :], ACT.Silu, bias=bias).then_inc(silu.full(k), 1)

                    for i in range(FI):
                        silu_of(U_GU + 2 * i, i, bg[:, i:i + 1])
                        if i % RH == 0:
                            t = i // RH
                            act.wait_ge(z["diff_ready"], (it * TILES + t + 1) * 2)
                            act.activation(ex[:, t, :, :], ex[:, t, :, :], ACT.Exp).then_inc(z["exp_done"], 1)
                            act.activation(ebest[:, 0, :, :], ebest[:, 0, :, :], ACT.Exp).then_inc(z["exp_done"], 1)
                        if i:
                            high_hid(i - 1)
                        if i + 2 < FI:
                            high_gu(i + 2)
                        if i >= 2:
                            high_wd(i)
                    high_hid(FI - 1)
                    for i in range(FI):
                        silu_of(U_ST + 2 * i, FI + i, 0.0)
                        if i == LN_AT:
                            deviations(act, z, it + 1, std, mv, eps)

            @block.gpsimd
            def _(pool):
                make_identity(pool, ident, z["id_step"])
                pool.iota(index[:, :], [[1, KEYS]], base=0, channel_multiplier=0,
                          allow_small_or_imprecise_dtypes=True).then_inc(z["id_step"], 1)
                pool.iota(falling[:, :], [[-1, TOPK]], base=TOPK, channel_multiplier=0,
                          allow_small_or_imprecise_dtypes=True).then_inc(z["id_step"], 1)
                with pool.Fori(0, BLOCKS) as it:
                    def low_gu(i):
                        pool.wait_ge(z["gu_high"], it * FI + i + 1)
                        pool.tensor_tensor(gu_s[i % 3][:, 1, :, :, :], gu_w.buf(i)[:, :, :, :], gu_s[i % 3][:, 0, :, :, :].bitcast(F32),
                                           ALU.subtract).then_inc(gu_w.free(i), 1)

                    def low_wd(i):
                        pool.wait_ge(z["wd_high"], it * FI + i + 1)
                        pool.tensor_tensor(wd_s[i % 2][:, 1, :], wd_w.buf(i)[:, :], wd_s[i % 2][:, 0, :].bitcast(F32),
                                           ALU.subtract).then_inc(wd_w.free(i), 1)

                    def pair_up(m):
                        part, t, h = job(m)
                        if part == 0 and h == 0:
                            pool.wait_ge(z["sel_ready"], it * TILES + t + 1)
                        if m >= 8 or pool_reaches(m):
                            pool.wait_ge(z["spread"], it * JOBS + m - (3 if pool_reaches(m) else 7))
                        i = slice(part * ROWS, (part + 1) * ROWS)
                        if pool_reaches(m):
                            pool.tensor_tensor(reach[m % 4][:, :, :], wide(cx[:, t, h, i]), flat(qy[:, t, h, :]),
                                               ALU.add).then_inc(z["paired"], 1)
                        pool.tensor_tensor(outer[m % 8][:, :, :], wide(exn[:, t, h, i]), flat(ex[:, t, RH + h, :]),
                                           ALU.mult).then_inc(z["paired"], 1)

                    for c in range(DC):
                        pool.wait_ge(z["x_high"], it * DC + c + 1)
                        pool.tensor_tensor(xnT_s[:, 1, c, :], xnT[:, c, :], xnT_s[:, 0, c, :].bitcast(F32),
                                          ALU.subtract).then_inc(z["x_low"], 1)
                    low_gu(0)
                    low_gu(1)
                    for i in range(FI):
                        if i >= RH:
                            pair_up(i - RH)
                        if i + 2 < FI:
                            low_gu(i + 2)
                        low_wd(i)
                    for m in range(FI - RH, JOBS):
                        pair_up(m)

            @block.vector
            def _(dve):
                dve.memset(eps[:, :], EPS).then_inc(z["eps_done"], 1)
                dve.wait_ge(z["id_step"], 4)
                layernorm(dve, z, 0, xin, stats, mv, std, rstd, xn)
                dve.wait_ge(z["w_loaded"], 4 * 16)
                with dve.Fori(0, BLOCKS) as it:
                    st = Steps(z["dve_step"], it, FF0_STEPS)

                    def settle():
                        dve.wait_ge(st.sem, st.level())

                    full = [P, RH, TOPK, TOPK]
                    own = 0

                    def candidates(t):
                        hold(dve, work.free(U_SIM + t), (it + 1) * MOVED, z["held"])
                        for g in range(2 * RH):
                            st.give(dve.max(best[:, own, g, :], sim[:, t, g, :]))
                        hold(dve, st.sem, st.level(), z["held"])
                        for g in range(2 * RH):
                            st.give(dve.max_index(place[:, own, g, :], best[:, own, g, :], sim[:, t, g, :]))
                        b = best[:, own, :, :]
                        top = lambda n: b[:, :, 0:1].broadcast_to([P, 2 * RH, n])
                        dve.tensor_tensor(ex[:, t, :, :], sim[:, t, :, :], top(KEYS), ALU.subtract).then_inc(z["diff_ready"], 1)
                        dve.tensor_tensor(ebest[:, own, :, :], b, top(TOPK), ALU.subtract).then_inc(z["diff_ready"], 1)

                    def pairs(t):
                        b = best[:, own, :, :]
                        st.give(dve.tensor_tensor(pair[:, own, :, :, :], b[:, 0:RH, :].unsqueeze(3).broadcast_to(full),
                                                  b[:, RH:, :].unsqueeze(2).broadcast_to(full), ALU.add))
                        hold(dve, st.sem, st.level(), z["held"])
                        for h in range(RH):
                            st.give(dve.max(best2[:, own, h, :], pair[:, own, h, :, :]))
                        st.give(dve.tensor_copy(placef[:, own, :, :], place[:, own, :, :]))
                        st.give(dve.tensor_scalar(beyond[:, own, :, :], place[:, own, 0:RH, :], float(XROWS), None, ALU.is_ge))
                        hold(dve, st.sem, st.level(), z["held"])
                        for h in range(RH):
                            st.give(dve.match_replace(picked[:, own, h, :, :], best2[:, own, h, :], pair[:, own, h, :, :], LOW))
                        settle()
                        st.give(dve.tensor_tensor(picked[:, own], picked[:, own], pair[:, own], ALU.not_equal))
                        settle()
                        with nc.allow_low_precision(reason="counts of at most eight are exact"):
                            st.give(dve.tensor_reduce(count[:, own, :, :], picked[:, own], AX.X, ALU.add))

                    def rows(t):
                        xs = [P, RH, XROWS, TOPK]
                        px, hot_x = placef[:, own, 0:RH, :], hot[:, :, 0:XROWS, :]
                        st.give(dve.tensor_tensor(hot_x, index[:, 0:XROWS].unsqueeze(1).unsqueeze(3).broadcast_to(xs),
                                                  px.unsqueeze(2).broadcast_to(xs), ALU.is_equal))
                        dve.wait_ge(z["exp_done"], (it * TILES + t + 1) * 2)
                        e = ebest[:, own, :, :]
                        st.give(dve.tensor_tensor(pair[:, own], e[:, 0:RH, :].unsqueeze(3).broadcast_to(full),
                                                  e[:, RH:, :].unsqueeze(2).broadcast_to(full), ALU.mult))
                        settle()
                        st.give(dve.tensor_tensor(hot_x, hot_x, count[:, own, :, :].unsqueeze(2).broadcast_to(xs), ALU.mult))
                        st.give(dve.tensor_tensor(pair[:, own], pair[:, own], picked[:, own], ALU.mult))
                        settle()
                        with nc.allow_low_precision(reason="counts of at most eight are exact"):
                            st.give(dve.tensor_reduce(cx[:, t, :, :], hot_x, AX.X, ALU.add))
                        st.give(dve.tensor_reduce(rows_w[:, own, :, :], pair[:, own], AX.X, ALU.add))
                        settle()
                        st.give(dve.tensor_reduce(norm[:, own, 0, :], rows_w[:, own, :, :], AX.X, ALU.add))
                        settle()
                        st.give(dve.reciprocal(norm[:, own, 1, :], norm[:, own, 0, :]))
                        settle()
                        inv = norm[:, own, 1, :].unsqueeze(2)
                        dve.tensor_tensor(exn[:, t, :, :], ex[:, t, 0:RH, 0:XROWS], inv.broadcast_to([P, RH, XROWS]),
                                          ALU.mult).then_inc(z["sel_ready"], 1)
                        st.give(dve.tensor_tensor(rows_w[:, own, :, :], rows_w[:, own, :, :], inv.broadcast_to([P, RH, TOPK]), ALU.mult))
                        settle()
                        st.give(dve.tensor_tensor(rows_w[:, own, :, :], rows_w[:, own, :, :], beyond[:, own, :, :], ALU.mult))
                        settle()
                        st.give(dve.tensor_reduce(beyond_w[:, t, :], rows_w[:, own, :, :], AX.XY, ALU.add))

                    def columns(t):
                        ys = [P, RH, KEYS, TOPK]
                        st.give(dve.tensor_tensor(hot[:, :, :, :], index[:, :].unsqueeze(1).unsqueeze(3).broadcast_to(ys),
                                                  placef[:, own, RH:, :].unsqueeze(2).broadcast_to(ys), ALU.is_equal))
                        settle()
                        fall = falling[:, :].unsqueeze(1).broadcast_to([P, RH * KEYS, TOPK])
                        hy = hot[:, :, :, :].rearrange("p h j b -> p (h j) b")
                        st.give(dve.tensor_tensor(hy, hy, fall, ALU.mult))
                        settle()
                        with nc.allow_low_precision(reason="ranks of at most eight are exact"):
                            st.give(dve.tensor_reduce(qy[:, t, :, :], hot[:, :, :, :], AX.X, ALU.add))

                    def spread(m):
                        part, t, h = job(m)
                        i = slice(part * ROWS, (part + 1) * ROWS)
                        g = G[:, t, i.start * KEYS:i.stop * KEYS].rearrange("p (i j) -> p i j", j=KEYS)
                        r, w = reach[m % 4][:, :, :], outer[m % 8][:, :, :]
                        if not pool_reaches(m):
                            settle()
                            st.give(dve.tensor_tensor(r, wide(cx[:, t, h, i]), flat(qy[:, t, h, :]), ALU.add))
                            settle()
                        dve.wait_ge(z["paired"], it * pool_made(JOBS) + pool_made(m + 1))
                        if h == 0:
                            last = dve.scalar_tensor_tensor(out=g, in0=r, scalar=float(TOPK), in1=w, op0=ALU.is_gt, op1=ALU.mult)
                        else:
                            st.give(dve.scalar_tensor_tensor(out=w, in0=r, scalar=float(TOPK), in1=w, op0=ALU.is_gt, op1=ALU.mult))
                            settle()
                            last = dve.tensor_tensor(g, g, w, ALU.add)
                        last.then_inc(z["spread"], 1)
                        if part == PARTS - 1 and h == RH - 1:
                            dve.wait_ge(z["spread"], it * JOBS + m + 1)
                            dve.tensor_tensor(G[:, t, NEXP - 1:], G[:, t, NEXP - 1:], beyond_w[:, t, :],
                                              ALU.add).then_inc(z["G_ready"], 1)

                    def hidden(n, k, bias):
                        dve.wait_ge(work.full(n), work.fillings(it, n))
                        dve.wait_ge(silu.full(k), silu.fillings(it, k))
                        if 2 <= k < FI + 2:
                            dve.wait_ge(z["hid_ready"], it * FI + k - 1)
                        elif k >= FI + 2:
                            dve.wait_ge(gu_w.free(k - 2), gu_w.emptied_by(it, k - 2))
                        if bias is None:
                            dve.tensor_tensor(hid.buf(k)[:, :], work.buf(n)[:, :], silu.buf(k)[:, :], ALU.mult).then_inc(hid.full(k), 1)
                        else:
                            dve.scalar_tensor_tensor(out=hid.buf(k)[:, :], in0=work.buf(n)[:, :], scalar=bias,
                                                     in1=silu.buf(k)[:, :], op0=ALU.add, op1=ALU.mult).then_inc(hid.full(k), 1)

                    def low_hid(i):
                        dve.wait_ge(z["hid_high"], it * FI + i + 1)
                        dve.tensor_tensor(hid_s[i % 3][:, 1, :], hid.buf(i)[:, :], hid_s[i % 3][:, 0, :].bitcast(F32),
                                          ALU.subtract).then_inc(z["hid_ready"], 1)

                    for i in range(FI):
                        t = i // 4
                        (candidates, pairs, rows, columns)[i % 4](t)
                        if i:
                            low_hid(i - 1)
                        hidden(U_GU + 2 * i + 1, i, bu[:, i:i + 1])
                        if t:
                            spread(i - 4)
                    low_hid(FI - 1)
                    for m in range(SPREADS - 4, SPREADS):
                        spread(m)
                    for i in range(FI):
                        if i < FI - FI // PARTS:
                            for m in range(4):
                                spread(SPREADS + 4 * i + m)
                        hidden(U_ST + 2 * i + 1, FI + i, None)
                        if i == LN_AT:
                            layernorm(dve, z, it + 1, xin, stats, mv, std, rstd, xn)
                    dve.wait_ge(z["res_loaded"], (it + 1) * 16)
                    for t in range(TILES):
                        st.give(dve.tensor_tensor(xres[:, t, :], xres[:, t, :], bd[:, :], ALU.add))
                    settle()
                    dve.wait_ge(gu_w.free(2 * FI - 1), gu_w.emptied_by(it, 2 * FI - 1))
                    for t in range(TILES):
                        dve.tensor_tensor(xres[:, t, :], accs[t][:, :], xres[:, t, :], ALU.add).then_inc(z["out_ready"], 1)
                    st.end()


def ffn1(nc, a, s, x_in, x_out):
    pre = "ff1"
    USES = FI + DC
    LN_AT = FI // 2
    LAG = 2
    with ExitStack() as ctx:
        sem = make_sem(nc, s["sems"], pre)
        sb = lambda name, shape, dt=F32: ctx.enter_context(nc.sbuf_tensor(f"{pre}_{name}", shape, dt))
        ident = sb("ident", [P, P])
        eps = sb("eps", [P, 1])
        wexp = sb("wexp", [P, 2, DC, F], F32R)
        wcon = sb("wcon", [P, 2, FI, D], F32R)
        room = sb("room", [P, 4, F])
        stage = Ring(sem, "stage", [room[:, i, :] for i in range(4)], 2 * DC, parts=16)
        xnT = room[:, 0:2, :].bitcast(F32R).rearrange("p h (c b) -> p h c b", c=DC)
        hid = [room[:, 2 + i // 2, i % 2 * 2 * BLOCK:(i % 2 + 1) * 2 * BLOCK].bitcast(F32R).rearrange("p (h b) -> p h b", h=2)
               for i in range(4)]
        bh, bias = sb("bh", [P, FI]), sb("bias", [P, 2, D])
        xin, xres, xn = (sb(n, [P, TILES, D]) for n in ("xin", "xres", "xn"))
        act_out = [sb(f"act{i}", [P, BLOCK]) for i in range(2)]
        stats, mv = sb("stats", [P, TILES, 6]), sb("mv", [P, TILES, 2])
        std, rstd = sb("std", [P, TILES]), sb("rstd", [P, TILES])
        ps = lambda name: ctx.enter_context(nc.psum_tensor(f"{pre}_{name}", [P, 512], F32))
        work = Ring(sem, "work", [ps(f"work{i}") for i in range(4)], USES, start=1, before=1)
        accs = [ps(f"acc{i}") for i in range(TILES)]
        z = Named(sem)
        z["held"] = s["held"]

        with nc.Block() as block:
            @block.sync
            def _(sp):
                sp.dma_start(xin[:, :, :], x_in[0].rearrange("p t d -> p (t d)")).then_inc(z["x_loaded"], 16)
                for n in range(2 * DC):
                    c = n % DC
                    if n >= 4:
                        sp.wait_ge(stage.free(n), stage.emptyings(0, n))
                    src = s["wcon" if n >= DC else "wexp"].rearrange("p (c n) -> p c n", c=DC)[:, c, :]
                    sp.dma_start(stage.buf(n), src).then_inc(stage.full(n), 16)
                sp.dma_start(bh[:, :], s["bexp"].rearrange("a (i p) -> p (a i)", p=P), allow_slow_non_contiguous=True).then_inc(z["b_loaded"], 16)
                for k, name in enumerate(("b_con", "down_bias")):
                    sp.dma_start(bias[:, k, :], a[name].partition_broadcast(P)).then_inc(z["b_loaded"], 16)

                def block_io(it, more):
                    sp.wait_ge(z["xn_ready"], (it + 1) * TILES)
                    nxt = bass.ds(it + 1, 1) if more else slice(it, it + 1)
                    sp.dma_start(xin[:, :, :], x_in[nxt].rearrange("a p t d -> (a p) (t d)")).then_inc(z["x_loaded"], 16)
                    if not isinstance(it, int) or it:
                        sp.wait_ge(z["stored"], it * 16)
                    sp.dma_start(xres[:, :, :], x_in[bass.ds(it, 1)].rearrange("a p t d -> (a p) (t d)")).then_inc(z["res_loaded"], 16)
                    sp.wait_ge(z["out_ready"], (it + 2) * TILES)
                    sp.dma_start(x_out[bass.ds(it, 1)].rearrange("a p t d -> (a p) (t d)"), xres[:, :, :]).then_inc(z["stored"], 16)

                block_io(0, True)
                with sp.Fori(1, BLOCKS - 1) as it:
                    block_io(it, True)
                block_io(BLOCKS - 1, False)
                sp.wait_ge(z["stored"], BLOCKS * 16)
                sp.wait_ge(z["x_loaded"], (BLOCKS + 1) * 16)

            @block.tensor
            def _(pe):
                pe.wait_ge(z["id_step"], 2)
                for c in range(DC):
                    n = DC + c
                    pe.wait_ge(stage.full(n), stage.fillings(0, n))
                    for q in range(4):
                        if c:
                            pe.wait_ge(z["wcon_ready"], (c - 1) * 4 + q + 1)
                        for j in range(4):
                            i = 4 * q + j
                            last = pe.transpose(accs[q][:, j * P:(j + 1) * P], stage.buf(n)[:, i * P:(i + 1) * P], ident[:, :])
                        last.then_inc(z["turned"], 1)
                pe.wait_ge(z["wcon_ready"], FI)

                def turn_rows(nth):
                    pe.wait_ge(z["xn_ready"], (nth + 1) * TILES)
                    for c in range(DC):
                        n = FI + c
                        bank = work.buf(n)
                        if not isinstance(nth, int):
                            pe.wait_ge(work.free(n), work.emptyings(nth - 1, n))
                        for t in range(TILES):
                            last = pe.transpose(bank[:, t * P:(t + 1) * P], xn[:, t, c * P:(c + 1) * P], ident[:, :])
                        last.then_inc(work.full(n), 1)

                turn_rows(0)
                with pe.Fori(0, BLOCKS) as it:
                    for i in range(FI + LAG):
                        if i < FI:
                            bank = work.buf(i)
                            if i == 0:
                                for n in range(4):
                                    pe.wait_ge(work.free(n), work.emptyings(it, n))
                            elif i >= 4:
                                pe.wait_ge(work.free(i), work.emptyings(it, i))
                            for c in range(DC):
                                last = split_product(pe, bank[:, :], lambda x: wexp[:, x, c, i * P:(i + 1) * P],
                                                     lambda y: xnT[:, y, c, :], c == 0, c == DC - 1)
                            last.then_inc(work.full(i), 1)
                        if i == FI:
                            turn_rows(it + 1)
                        if i >= LAG:
                            k = i - LAG
                            pe.wait_ge(z["hid_ready"], it * FI + k + 1)
                            for t in range(TILES):
                                if k == 0:
                                    pe.wait_ge(z["out_ready"], it * TILES + t + 1)
                                last = split_product(pe, accs[t][:, :], lambda x: hid[k % 4][:, x, t * P:(t + 1) * P],
                                                     lambda y: wcon[:, y, k, :], k == 0, k == FI - 1)
                                if k == FI - 1:
                                    last.then_inc(z["summed"], 1)
                            if k < FI - 1:
                                last.then_inc(z["spent"], 1)
                for n in range(FI, FI + DC):
                    pe.wait_ge(work.free(n), work.emptied_by(BLOCKS - 1, n))

            @block.scalar
            def _(act):
                for c in range(DC):
                    act.wait_ge(stage.full(c), stage.fillings(0, c))
                    act.copy(wexp[:, 0, c, :], stage.buf(c)).then_inc(z["high"], 1)
                act.wait_ge(z["eps_done"], 1)
                deviations(act, z, 0, std, mv, eps)
                for c in range(DC):
                    for q in range(4):
                        act.wait_ge(z["turned"], c * 4 + q + 1)
                        act.copy(wcon[:, 0, 4 * q:4 * q + 4, c * P:(c + 1) * P],
                                 accs[q][:, :].rearrange("p (j n) -> p j n", j=4)).then_inc(z["high"], 1)
                act.wait_ge(z["b_loaded"], 3 * 16)

                def high_rows(nth):
                    for c in range(DC):
                        n = FI + c
                        act.wait_ge(work.full(n), work.fillings(nth - 1, n))
                        act.copy(xnT[:, 0, c, :], work.buf(n)[:, :]).then_inc(z["x_high"], 1)

                high_rows(0)
                with act.Fori(0, BLOCKS) as it:
                    for i in range(FI):
                        act.wait_ge(work.full(i), work.fillings(it, i))
                        if i >= 2:
                            act.wait_ge(z["hid_ready"], it * FI + i - 1)
                        act.activation(act_out[i % 2][:, :], work.buf(i)[:, :], ACT.Gelu, bias=bh[:, i:i + 1]).then_inc(work.free(i), 1)
                        act.wait_ge(work.free(i), work.emptied_by(it, i))
                        if i >= 4:
                            act.wait_ge(z["spent"], it * (FI - 1) + i - 3)
                        act.copy(hid[i % 4][:, 0, :], act_out[i % 2][:, :]).then_inc(z["hid_high"], 1)
                        if i == LN_AT:
                            deviations(act, z, it + 1, std, mv, eps)
                    high_rows(it + 1)

            @block.gpsimd
            def _(pool):
                make_identity(pool, ident, z["id_step"])

            @block.vector
            def _(dve):
                dve.memset(eps[:, :], EPS).then_inc(z["eps_done"], 1)
                dve.sem_inc(z["out_ready"], TILES)
                for c in range(DC):
                    dve.wait_ge(z["high"], c + 1)
                    dve.tensor_tensor(wexp[:, 1, c, :], stage.buf(c), wexp[:, 0, c, :].bitcast(F32),
                                      ALU.subtract).then_inc(stage.free(c), 1)
                layernorm(dve, z, 0, xin, stats, mv, std, rstd, xn)
                for c in range(DC):
                    for q in range(4):
                        dve.wait_ge(z["high"], DC + c * 4 + q + 1)
                        part = lambda h: wcon[:, h, 4 * q:4 * q + 4, c * P:(c + 1) * P]
                        dve.tensor_tensor(part(1), accs[q][:, :].rearrange("p (j n) -> p j n", j=4), part(0).bitcast(F32),
                                          ALU.subtract).then_inc(z["wcon_ready"], 1)
                dve.wait_ge(z["b_loaded"], 3 * 16)
                dve.tensor_tensor(bias[:, 0, :], bias[:, 0, :], bias[:, 1, :], ALU.add).then_inc(z["bias_done"], 1)
                dve.wait_ge(z["bias_done"], 1)

                def low_rows(nth):
                    for c in range(DC):
                        dve.wait_ge(z["x_high"], nth * DC + c + 1)
                        dve.tensor_tensor(xnT[:, 1, c, :], work.buf(FI + c)[:, :], xnT[:, 0, c, :].bitcast(F32),
                                          ALU.subtract).then_inc(work.free(FI + c), 1)

                low_rows(0)
                with dve.Fori(0, BLOCKS) as it:
                    st = Steps(z["dve_step"], it, TILES)
                    for i in range(FI):
                        dve.wait_ge(z["hid_high"], it * FI + i + 1)
                        h = hid[i % 4]
                        dve.tensor_tensor(h[:, 1, :], act_out[i % 2][:, :], h[:, 0, :].bitcast(F32),
                                          ALU.subtract).then_inc(z["hid_ready"], 1)
                        if i == LN_AT:
                            layernorm(dve, z, it + 1, xin, stats, mv, std, rstd, xn)
                    low_rows(it + 1)
                    dve.wait_ge(z["res_loaded"], (it + 1) * 16)
                    for t in range(TILES):
                        st.give(dve.tensor_tensor(xres[:, t, :], xres[:, t, :], bias[:, 0, :], ALU.add))
                    dve.wait_ge(st.sem, st.level())
                    dve.wait_ge(z["summed"], (it + 1) * TILES)
                    for t in range(TILES):
                        dve.tensor_tensor(xres[:, t, :], accs[t][:, :], xres[:, t, :], ALU.add).then_inc(z["out_ready"], 1)
                    st.end()


FF0_STEPS = 264


def build(nc, a, out, sems):
    scratch = lambda name, shape: nc.dram_tensor("scratch_" + name, shape, F32).ap()
    s = {"kz": [scratch(f"kz{i}", (BATCH, P, HEADS * CTX)) for i in range(2)],
         "vm": [scratch(f"vm{i}", (BATCH, P, HEADS * (dk + 1))) for i, dk in enumerate((32, 64))],
         "vr": [scratch(f"vr{i}", (BATCH, REM, HEADS * (dk + 1))) for i, dk in enumerate((32, 64))],
         "fold": scratch("fold", (P, DC * D)), "wexp": scratch("wexp", (P, DC * F)),
         "wcon": scratch("wcon", (P, DC * F)), "bexp": scratch("bexp", (1, F))}
    s["sems"] = sems
    s["held"] = sems.enter_context(nc.semaphore("held"))
    blocks = lambda ap: ap.rearrange("(a p t) d -> a p t d", p=P, t=TILES)
    x = [blocks(a["x"])] + [blocks(scratch(f"x{i}", (TOKENS, D))) for i in (1, 2, 3)] + [blocks(out)]
    prepare(nc, a, s)
    attention(nc, a, s, 0, x[0], x[1])
    ffn0(nc, a, s, x[1], x[2])
    attention(nc, a, s, 1, x[2], x[3])
    ffn1(nc, a, s, x[3], x[4])


def kernel(**inputs):
    import numpy as np
    import concourse.bacc as bacc
    from concourse.bass_utils import run_bass_kernel_spmd

    v = {k: np.asarray(w) for k, w in inputs.items()}
    cols = lambda b: b.reshape(-1, P).T
    tiles = lambda w: w.reshape(DC, P, FI, P).transpose(2, 1, 0, 3)
    laid = {
        "x": v["x"].reshape(TOKENS, D), "ctxT": v["ctx_1024"].transpose(0, 2, 1),
        "wq0": v["L0_xattn_w_q"].T, "wkT0": v["L0_xattn_w_k"].T, "wvT0": v["L0_xattn_w_v"].T, "wo0": v["L0_xattn_w_o"].T,
        "bq0": cols(v["L0_xattn_b_q"]), "bk0": cols(v["L0_xattn_b_k"]), "bv0": v["L0_xattn_b_v"], "bo0": v["L0_xattn_b_o"],
        "Wg": tiles(v["L0_ffn_Wg"]), "Wu": tiles(v["L0_ffn_Wu"]), "Wd": v["L0_ffn_Wd"].reshape(FI, P, D),
        "bg": cols(v["L0_ffn_bg"]), "bu": cols(v["L0_ffn_bu"]), "bd": v["L0_ffn_bd"],
        "WqT": v["L0_ffn_Wq"].T, "keysT": v["L0_ffn_keys"].transpose(2, 0, 3, 1).reshape(2 * RH * KEYS, KEYS),
        "downT": tiles(v["L0_ffn_down_embed"].T), "up": v["L0_ffn_up_embed"].reshape(FI, P, D),
        "wkv1": v["L1_xattn_w_kv"], "wq1": v["L1_xattn_w_q"], "wo1": v["L1_xattn_w_out1"], "w2": v["L1_xattn_w_out2"],
        "gamma": v["L1_xattn_gamma"],
        "W_exp": v["L1_ffn_W_exp"], "b_exp": v["L1_ffn_b_exp"].reshape(1, F), "up_bias": v["L1_ffn_up_bias"].reshape(1, F),
        "up_w": v["L1_ffn_up_weights"].transpose(0, 2, 3, 1).reshape(STAGES, 4, F // 2)[:, [0, 3, 2, 1]],
        "down_w": v["L1_ffn_down_weights"].transpose(0, 2, 3, 1).reshape(STAGES, 4, F // 2)[:, [0, 3, 1, 2]],
        "W_conT": v["L1_ffn_W_con"].T, "b_con": v["L1_ffn_b_con"], "down_bias": v["L1_ffn_down_bias"],
    }
    nc = bacc.Bacc("TRN2", target_bir_lowering=False, num_devices=1)
    arrays, a = {}, {}
    for name, w in laid.items():
        arrays["in_" + name] = np.ascontiguousarray(w)
        a[name] = nc.dram_tensor("in_" + name, w.shape, mybir.dt.from_np(w.dtype), kind="ExternalInput").ap()
    out = nc.dram_tensor("out_0", (TOKENS, D), F32, kind="ExternalOutput").ap()
    with ExitStack() as sems:
        build(nc, a, out, sems)
    r = run_bass_kernel_spmd(nc, [arrays], core_ids=[0])
    return r.results[0]["out_0"].reshape(BATCH, TOKENS // BATCH, D)
```
